# Optimizing a Trainium2 kernel written in Bass

```python
import numpy as np
import jax
import jax.numpy as jnp

def _softmax(x, axis=-1):
    return jax.nn.softmax(x, axis=axis)

def _gelu(x):
    return jax.nn.gelu(x, approximate=True)

def _silu(x):
    return jax.nn.silu(x)

def _sigmoid(x):
    return jax.nn.sigmoid(x)

def _layernorm(x, axis=-1, eps=1e-05):
    m = jnp.mean(x, axis=axis, keepdims=True)
    v = jnp.var(x, axis=axis, keepdims=True)
    return (x - m) / jnp.sqrt(v + eps)

def _scatter_add(tgt, idx, src, axis=0):
    return tgt.at[idx].add(src)

def _segment_sum(src, seg, n):
    return jax.ops.segment_sum(src, seg, n)
kernel_name = 'mk_hybrid_d1_jaxref_r8_f8efdf'

def setup_inputs(seed: int=0):
    np.random.seed(seed)
    _w = jnp.asarray

    def _L0_attn_a_setup():
        import jax, jax.numpy as jnp
        import numpy as np
        B_, L_, D_ = (2, 128, 256)
        E_, N_, R_, K_ = (512, 16, 128, 4)
        EPS = 1e-05

        def _forward(resid, norm_w, skip_w, in_w, conv_w, conv_b, wd1, wd2, wd2_b, wB, wC, A_log, W_D, out_w):
            B, L, D = resid.shape
            E, K = conv_w.shape
            N = A_log.shape[1]
            rn = resid * jax.lax.rsqrt(jnp.mean(resid * resid, -1, keepdims=True) + EPS) * norm_w
            skip = rn @ skip_w.T
            x_in = rn @ in_w.T
            xp = jnp.pad(x_in, ((0, 0), (K - 1, 0), (0, 0)))
            conv = conv_b + sum((xp[:, k:k + L, :] * conv_w[:, k] for k in range(K)))
            x = jax.nn.silu(conv)
            delta = jax.nn.softplus(x @ wd1.T @ wd2.T + wd2_b)
            A = -jnp.exp(A_log)
            Bm = x @ wB.T
            Cm = x @ wC.T

            def step(h, inp):
                d_l, b_l, c_l, x_l = inp
                h = jnp.exp(d_l[:, :, None] * A) * h + (d_l * x_l)[:, :, None] * b_l[:, None, :]
                y_l = jnp.einsum('ben,bn->be', h, c_l)
                return (h, y_l)
            h0 = jnp.zeros((B, E, N), resid.dtype)
            xs = (delta.transpose(1, 0, 2), Bm.transpose(1, 0, 2), Cm.transpose(1, 0, 2), x.transpose(1, 0, 2))
            _, ys = jax.lax.scan(step, h0, xs)
            y = ys.transpose(1, 0, 2) + x * W_D
            y = y * jax.nn.silu(skip)
            return resid + y @ out_w.T
        key = jax.random.key(seed)
        ks = jax.random.split(key, 12)
        s = lambda i, shape, scale=0.02: jax.random.normal(ks[i], shape, jnp.float32) * scale
        dt = jnp.exp(jax.random.uniform(ks[10], (E_,)) * (np.log(0.1) - np.log(0.001)) + np.log(0.001))
        inv_dt = dt + jnp.log(-jnp.expm1(-dt))
        return {'resid': jax.random.normal(ks[0], (B_, L_, D_), jnp.float32), 'norm_w': jnp.ones((D_,), jnp.float32), 'skip_w': s(1, (E_, D_)), 'in_w': s(2, (E_, D_)), 'conv_w': s(3, (E_, K_), 0.2), 'conv_b': jnp.zeros((E_,), jnp.float32), 'wd1': s(4, (R_, E_)), 'wd2': s(5, (E_, R_), R_ ** (-0.5)), 'wd2_b': inv_dt, 'wB': s(6, (N_, E_)), 'wC': s(7, (N_, E_)), 'A_log': jnp.log(jnp.broadcast_to(jnp.arange(1, N_ + 1, dtype=jnp.float32), (E_, N_))), 'W_D': jnp.ones((E_,), jnp.float32), 'out_w': s(8, (D_, E_))}
    _L0_attn_a_in = _L0_attn_a_setup()

    def _L0_attn_b_setup():
        import jax, jax.numpy as jnp
        import numpy as np
        import math
        EMB = 256
        HEADS = 16
        HEAD_DIM = EMB // HEADS
        SCALE = math.sqrt(HEAD_DIM)

        def srms_norm(x, eps_min=1e-12):
            d = x.shape[-1]
            xf = x.astype(jnp.float32)
            norm = jnp.linalg.norm(xf * (1.0 / math.sqrt(d)), axis=-1, keepdims=True)
            norm = jnp.maximum(norm, eps_min)
            return (xf / norm).astype(x.dtype)
        key = jax.random.key(seed)
        ks = jax.random.split(key, 6)
        x = jax.random.normal(ks[0], (4, 512, EMB), dtype=jnp.float32)
        std = 1.0 / math.sqrt(EMB)
        Wq = jax.random.normal(ks[1], (EMB, EMB), dtype=jnp.float32) * std
        Wk = jax.random.normal(ks[2], (EMB, EMB), dtype=jnp.float32) * std
        Wv = jax.random.normal(ks[3], (EMB, EMB), dtype=jnp.float32) * std
        Wu = jax.random.normal(ks[4], (EMB, EMB), dtype=jnp.float32) * std
        Wo = jax.random.normal(ks[5], (EMB, EMB), dtype=jnp.float32) * std
        return {'x': x, 'Wq': Wq, 'Wk': Wk, 'Wv': Wv, 'Wu': Wu, 'Wo': Wo}
    _L0_attn_b_in = _L0_attn_b_setup()

    def _L0_ffn_setup():
        import jax, jax.numpy as jnp
        import numpy as np
        HIDDEN = 256
        INTER = 1024
        RETRIEVAL = 128
        NUM_EXPERTS = 512
        NUM_KEYS = 64
        TOP_K = 8
        B, S = (4, 256)
        key = jax.random.key(seed)
        ks = jax.random.split(key, 8)
        sc = 0.02
        return {'hidden_states': jax.random.normal(ks[0], (B, S, HIDDEN), jnp.float32), 'W_q': jax.random.normal(ks[1], (HIDDEN, RETRIEVAL), jnp.float32) * sc, 'keys': jax.random.normal(ks[2], (2, RETRIEVAL // 2, NUM_KEYS), jnp.float32) * sc, 'down_embed': jax.random.normal(ks[3], (NUM_EXPERTS, HIDDEN), jnp.float32) * sc, 'up_embed': jax.random.normal(ks[4], (NUM_EXPERTS, HIDDEN), jnp.float32) * sc, 'gate_w': jax.random.normal(ks[5], (HIDDEN, INTER), jnp.float32) * sc, 'up_w': jax.random.normal(ks[6], (HIDDEN, INTER), jnp.float32) * sc, 'down_w': jax.random.normal(ks[7], (INTER, HIDDEN), jnp.float32) * sc}
    _L0_ffn_in = _L0_ffn_setup()
    _d = {'L0_attn_a_resid': _L0_attn_a_in['resid'], 'L0_attn_a_norm_w': _L0_attn_a_in['norm_w'], 'L0_attn_a_skip_w': _L0_attn_a_in['skip_w'], 'L0_attn_a_in_w': _L0_attn_a_in['in_w'], 'L0_attn_a_conv_w': _L0_attn_a_in['conv_w'], 'L0_attn_a_conv_b': _L0_attn_a_in['conv_b'], 'L0_attn_a_wd1': _L0_attn_a_in['wd1'], 'L0_attn_a_wd2': _L0_attn_a_in['wd2'], 'L0_attn_a_wd2_b': _L0_attn_a_in['wd2_b'], 'L0_attn_a_wB': _L0_attn_a_in['wB'], 'L0_attn_a_wC': _L0_attn_a_in['wC'], 'L0_attn_a_A_log': _L0_attn_a_in['A_log'], 'L0_attn_a_W_D': _L0_attn_a_in['W_D'], 'L0_attn_a_out_w': _L0_attn_a_in['out_w'], 'L0_attn_b_Wq': _L0_attn_b_in['Wq'], 'L0_attn_b_Wk': _L0_attn_b_in['Wk'], 'L0_attn_b_Wv': _L0_attn_b_in['Wv'], 'L0_attn_b_Wu': _L0_attn_b_in['Wu'], 'L0_attn_b_Wo': _L0_attn_b_in['Wo'], 'L0_ffn_W_q': _L0_ffn_in['W_q'], 'L0_ffn_keys': _L0_ffn_in['keys'], 'L0_ffn_down_embed': _L0_ffn_in['down_embed'], 'L0_ffn_up_embed': _L0_ffn_in['up_embed'], 'L0_ffn_gate_w': _L0_ffn_in['gate_w'], 'L0_ffn_up_w': _L0_ffn_in['up_w'], 'L0_ffn_down_w': _L0_ffn_in['down_w']}
    _x0 = _d['L0_attn_a_resid']
    _d['L0_attn_a_resid'] = jax.random.normal(jax.random.fold_in(jax.random.key(seed), 1), (4, 1024, 256), dtype=_x0.dtype)
    del _x0
    return _d

def reference(L0_attn_a_resid, L0_attn_a_norm_w, L0_attn_a_skip_w, L0_attn_a_in_w, L0_attn_a_conv_w, L0_attn_a_conv_b, L0_attn_a_wd1, L0_attn_a_wd2, L0_attn_a_wd2_b, L0_attn_a_wB, L0_attn_a_wC, L0_attn_a_A_log, L0_attn_a_W_D, L0_attn_a_out_w, L0_attn_b_Wq, L0_attn_b_Wk, L0_attn_b_Wv, L0_attn_b_Wu, L0_attn_b_Wo, L0_ffn_W_q, L0_ffn_keys, L0_ffn_down_embed, L0_ffn_up_embed, L0_ffn_gate_w, L0_ffn_up_w, L0_ffn_down_w):

    def _L0_attn_a_ref(resid, norm_w, skip_w, in_w, conv_w, conv_b, wd1, wd2, wd2_b, wB, wC, A_log, W_D, out_w):
        import jax, jax.numpy as jnp
        import numpy as np
        B_, L_, D_ = (2, 128, 256)
        E_, N_, R_, K_ = (512, 16, 128, 4)
        EPS = 1e-05

        def _forward(resid, norm_w, skip_w, in_w, conv_w, conv_b, wd1, wd2, wd2_b, wB, wC, A_log, W_D, out_w):
            B, L, D = resid.shape
            E, K = conv_w.shape
            N = A_log.shape[1]
            rn = resid * jax.lax.rsqrt(jnp.mean(resid * resid, -1, keepdims=True) + EPS) * norm_w
            skip = rn @ skip_w.T
            x_in = rn @ in_w.T
            xp = jnp.pad(x_in, ((0, 0), (K - 1, 0), (0, 0)))
            conv = conv_b + sum((xp[:, k:k + L, :] * conv_w[:, k] for k in range(K)))
            x = jax.nn.silu(conv)
            delta = jax.nn.softplus(x @ wd1.T @ wd2.T + wd2_b)
            A = -jnp.exp(A_log)
            Bm = x @ wB.T
            Cm = x @ wC.T

            def step(h, inp):
                d_l, b_l, c_l, x_l = inp
                h = jnp.exp(d_l[:, :, None] * A) * h + (d_l * x_l)[:, :, None] * b_l[:, None, :]
                y_l = jnp.einsum('ben,bn->be', h, c_l)
                return (h, y_l)
            h0 = jnp.zeros((B, E, N), resid.dtype)
            xs = (delta.transpose(1, 0, 2), Bm.transpose(1, 0, 2), Cm.transpose(1, 0, 2), x.transpose(1, 0, 2))
            _, ys = jax.lax.scan(step, h0, xs)
            y = ys.transpose(1, 0, 2) + x * W_D
            y = y * jax.nn.silu(skip)
            return resid + y @ out_w.T
        return _forward(resid, norm_w, skip_w, in_w, conv_w, conv_b, wd1, wd2, wd2_b, wB, wC, A_log, W_D, out_w)

    def _L0_attn_b_ref(x, Wq, Wk, Wv, Wu, Wo):
        import jax, jax.numpy as jnp
        import numpy as np
        import math
        EMB = 256
        HEADS = 16
        HEAD_DIM = EMB // HEADS
        SCALE = math.sqrt(HEAD_DIM)

        def srms_norm(x, eps_min=1e-12):
            d = x.shape[-1]
            xf = x.astype(jnp.float32)
            norm = jnp.linalg.norm(xf * (1.0 / math.sqrt(d)), axis=-1, keepdims=True)
            norm = jnp.maximum(norm, eps_min)
            return (xf / norm).astype(x.dtype)
        B, L, D = x.shape
        H, dh = (HEADS, HEAD_DIM)
        q = (x @ Wq).reshape(B, L, H, dh).transpose(0, 2, 1, 3)
        k = (x @ Wk).reshape(B, L, H, dh).transpose(0, 2, 1, 3)
        v = (x @ Wv).reshape(B, L, H, dh).transpose(0, 2, 1, 3)
        u = (x @ Wu).reshape(B, L, H, dh).transpose(0, 2, 1, 3)
        q = jax.nn.relu(q) / SCALE
        k = jax.nn.relu(k) / SCALE
        u = jax.nn.silu(u)
        kv = jnp.einsum('bhlk,bhlv->bhkv', k, v)
        out = jnp.einsum('bhlk,bhkv->bhlv', q, kv)
        out = srms_norm(out) * u
        out = out.transpose(0, 2, 1, 3).reshape(B, L, D)
        return out @ Wo

    def _L0_ffn_ref(hidden_states, W_q, keys, down_embed, up_embed, gate_w, up_w, down_w):
        import jax, jax.numpy as jnp
        import numpy as np
        HIDDEN = 256
        INTER = 1024
        RETRIEVAL = 128
        NUM_EXPERTS = 512
        NUM_KEYS = 64
        TOP_K = 8
        B, S = (4, 256)
        b, s, h = hidden_states.shape
        n = b * s
        queries = (hidden_states @ W_q).reshape(2, n, RETRIEVAL // 2)
        routing = jnp.einsum('tnd,tdk->tnk', queries, keys)
        scores2, idx2 = jax.lax.top_k(routing, TOP_K)
        sx, sy = (scores2[0], scores2[1])
        ix, iy = (idx2[0], idx2[1])
        all_scores = (sx[:, :, None] + sy[:, None, :]).reshape(n, TOP_K * TOP_K)
        all_idx = (ix[:, :, None] * NUM_KEYS + iy[:, None, :]).reshape(n, TOP_K * TOP_K)
        scores, pk = jax.lax.top_k(all_scores, TOP_K)
        indices = jnp.take_along_axis(all_idx, pk, axis=-1)
        de = down_embed[indices]
        ue = up_embed[indices]
        x = hidden_states.reshape(n, h)
        ew = jnp.einsum('nh,nkh->nk', x, de)
        ew = jax.nn.silu(ew) * jax.nn.softmax(scores, axis=-1)
        experts_states = jnp.einsum('nk,nkh->nh', ew, ue).reshape(b, s, h)
        mlp = jax.nn.silu(x @ gate_w) * (x @ up_w) @ down_w
        return mlp.reshape(b, s, h) + experts_states
    x = L0_attn_a_resid
    x = x + _L0_attn_a_ref(_layernorm(x, axis=-1), L0_attn_a_norm_w, L0_attn_a_skip_w, L0_attn_a_in_w, L0_attn_a_conv_w, L0_attn_a_conv_b, L0_attn_a_wd1, L0_attn_a_wd2, L0_attn_a_wd2_b, L0_attn_a_wB, L0_attn_a_wC, L0_attn_a_A_log, L0_attn_a_W_D, L0_attn_a_out_w)
    x = x + _L0_ffn_ref(_layernorm(x, axis=-1), L0_ffn_W_q, L0_ffn_keys, L0_ffn_down_embed, L0_ffn_up_embed, L0_ffn_gate_w, L0_ffn_up_w, L0_ffn_down_w)
    x = x + _L0_attn_b_ref(_layernorm(x, axis=-1), L0_attn_b_Wq, L0_attn_b_Wk, L0_attn_b_Wv, L0_attn_b_Wu, L0_attn_b_Wo)
    x = x + _L0_ffn_ref(_layernorm(x, axis=-1), L0_ffn_W_q, L0_ffn_keys, L0_ffn_down_embed, L0_ffn_up_embed, L0_ffn_gate_w, L0_ffn_up_w, L0_ffn_down_w)
    return x

_drawn_inputs = setup_inputs


def setup_inputs(seed=0):
    import zlib

    import numpy as np

    out = dict(_drawn_inputs(seed))
    spreads = {'L0_attn_a_norm_w': (1.0, 0.2),
     'L0_attn_a_conv_b': (0.0, 0.1),
     'L0_attn_a_W_D': (1.0, 0.2)}
    factors = {}
    for name, (base, spread) in spreads.items():
        noise = np.random.default_rng([zlib.crc32(name.encode()), seed]).standard_normal(out[name].shape)
        drawn = base * np.exp(spread * noise) if base else spread * noise
        out[name] = jnp.asarray(drawn.astype(out[name].dtype))
    for name, factor in factors.items():
        out[name] = (out[name] * factor).astype(out[name].dtype)
    return out
```

```python
from contextlib import ExitStack

import numpy as np

import concourse.bass as bass
from concourse import mybir

FP32 = mybir.dt.float32
BF16 = mybir.dt.bfloat16
ALU = mybir.AluOpType
ACT = mybir.ActivationFunctionType
AX = mybir.AxisListType

P = 128
BATCH, SEQ, D = 4, 1024, 256
TOKENS = BATCH * SEQ
CHUNK = 512
CHUNKS = TOKENS // CHUNK
TILES = CHUNK // P
KD = D // P
E, N, R, TAPS = 512, 16, 128, 4
KE = E // P
EPS = 1e-5
EXP_LN_SET = "natural_log_exp_and_others"


def need(eng, sem, value):
    if isinstance(value, int) and value <= 0:
        return
    eng.wait_ge(sem, value)


class Chain:

    def __init__(self, eng, sem):
        self.eng, self.sem, self.base, self.k = eng, sem, 0, 0

    def link(self, ins):
        self.k += 1
        ins.then_inc(self.sem, 1)
        self.eng.wait_ge(self.sem, self.base + self.k)

    def enter(self, i, steps):
        self.outer, self.steps = self.base + self.k, steps
        self.base, self.k = self.outer + i * steps, 0

    def leave(self, times):
        assert self.k == self.steps, f"{self.k} links in the loop's body"
        self.base, self.k = self.outer + times * self.steps, 0


def in_time(ap):
    return ap.rearrange("x (b p h) -> x b h p", b=2, h=2)


def mamba(nc, res, dram):
    RING = 4
    ctx = ExitStack()
    with ctx:
        def sb(name, shape, dt=FP32):
            return ctx.enter_context(nc.sbuf_tensor("m_" + name, shape, dt))

        def sem(name):
            return ctx.enter_context(nc.semaphore("m_" + name))

        inw = sb("inw", [P, KD, E])
        skw = sb("skw", [P, KD, E])
        wd1 = sb("wd1", [P, KE, R])
        wd2 = sb("wd2", [P, E])
        wbc = sb("wbc", [P, KE, P])
        outw = sb("outw", [P, KE, D])
        normw = sb("normw", [P, KD])
        convw = sb("convw", [P, KE, TAPS])
        convb = sb("convb", [P, KE])
        wd2b = sb("wd2b", [P, KE])
        wskip = sb("wskip", [P, KE])
        negA = sb("negA", [P, KE, N])
        ident = sb("ident", [P, P])
        pick = sb("pick", [P, 2 * N], BF16)
        mhalf = sb("mhalf", [P, 2, TILES])
        pause = sb("pause", [P, 2])

        stats = sb("stats", [P, TILES, 6])
        mv = sb("mv", [P, TILES, 2])
        sc = sb("sc", [P, 6, TILES])
        rn = sb("rn", [P, TILES, D])
        rawbc = rn[:, 0:2, :].rearrange("p t d -> p (t d)")
        rnT = sb("rnT", [P, KD, CHUNK])
        xin = sb("xin", [P, KE, 3 + 2 * CHUNK])
        work = sb("work", [P, KE, CHUNK])
        rT = sb("rT", [P, CHUNK])
        xs = sb("xs", [P, 2, KE, CHUNK])
        gate = sb("gate", [P, 2, KE, CHUNK])
        delta = sb("delta", [P, 2, KE, CHUNK])
        dx = sb("dx", [P, 2, KE, CHUNK])
        stack = sb("stack", [P, 2, CHUNK], BF16)
        dA = sb("dA", [P, 2, KE, CHUNK])
        U = sb("U", [P, RING, KE, CHUNK])
        Csb = sb("Csb", [P, 2, CHUNK])
        carry = sb("carry", [P, KE, N])

        y = ctx.enter_context(nc.psum_tensor("m_y", [P, KE, CHUNK], FP32))
        psB = ctx.enter_context(nc.psum_tensor("m_psB", [P, CHUNK], FP32))
        psC = ctx.enter_context(nc.psum_tensor("m_psC", [P, CHUNK], FP32))
        job = ctx.enter_context(nc.psum_tensor("m_job", [P, 2, CHUNK], FP32))

        x_first, x_rest = sem("x_first"), sem("x_rest")
        w_in, w_conv, w_d, w_bc, w_out, w_A = (sem(s) for s in ("w_in", "w_conv", "w_d", "w_bc", "w_out", "w_A"))
        const_ready = sem("const_ready")
        stats_ready, norm_ready, rn_ready = sem("stats_ready"), sem("norm_ready"), sem("rn_ready")
        job_full, job_free = sem("job_full"), sem("job_free")
        conv_done, xs_ready, split_done = sem("conv_done"), sem("xs_ready"), sem("split_done")
        zmin_ready, ln_ready, delta_ready = sem("zmin_ready"), sem("ln_ready"), sem("delta_ready")
        B_full, C_full, C_ready = sem("B_full"), sem("C_full"), sem("C_ready")
        dA_ready, mult_done, h_ready = sem("dA_ready"), sem("mult_done"), sem("h_ready")
        dx_ready = sem("dx_ready")
        hc_ready, nsum_done = sem("hc_ready"), sem("nsum_done")
        y_read, gate_done, out_full, out_free = sem("y_read"), sem("gate_done"), sem("out_full"), sem("out_free")
        dve_own, act_own, pool_own = sem("dve_own"), sem("act_own"), sem("pool_own")

        JOBS = 16
        PE_AT = {4: ("turn",), 5: ("in0", "in1"), 6: ("in2", "in3"), 7: ("in4", "in5"), 8: ("in6", "in7"),
                 10: ("low",), 11: ("bc", "dt0"), 12: ("dt1", "dt2"), 13: ("dt3",)}
        ACT_AT = {4: ("turn",), 6: ("in0", "in1"), 7: ("in2", "in3"), 8: ("in4", "in5"), 9: ("in6", "in7", "silu"),
                  10: ("low",), 11: ("bc",), 12: ("dt0", "dt1"), 13: ("dt2", "dt3"), 14: ("softplus",)}
        DVE_AT = {0: ("stats",), 2: ("norm",), 6: ("conv0",), 7: ("conv1", "conv2"), 8: ("conv3",),
                  12: ("split",), 13: ("least",), 14: ("delta",)}
        POOL_AT = {1: ("factors",), 15: ("dx",)}
        HEAD = range(0, 6)
        TAIL = range(6, N)
        GATED, MULTIPLIED, OUT, ADDED = 1, 2, (2, 3), (3, 4)

        def parts(at, n, c, part, q):
            if not (isinstance(c, int) and c == CHUNKS - 1):
                for name in at.get(n, ()):
                    part(name, c + 1, 1 - q)

        def schedule(head, tail, loop, first, steps=None, chain=None):
            first()
            head(0, 0, False)
            with loop(0, BATCH - 1) as b:
                if chain:
                    chain.enter(b, steps)
                tail(2 * b, 0, True)
                head(2 * b + 1, 1, True)
                tail(2 * b + 1, 1, True)
                head(2 * b + 2, 0, True)
                if chain:
                    chain.leave(BATCH - 1)
            tail(CHUNKS - 2, 0, True)
            head(CHUNKS - 1, 1, True)
            tail(CHUNKS - 1, 1, False)

        block = ctx.enter_context(nc.Block())

        @block.sync
        def _(sp):
            x_v = dram["x"].rearrange("b (s p h) d -> p (b s) (h d)", p=P, h=2)
            res_v = res[:, :, :].rearrange("p (s h) d -> p s (h d)", h=2)
            sp.dma_start(res_v[:, 0:2, :], x_v[:, 0:2, :]).then_inc(x_first, 16)
            sp.dma_start(normw[:, :], dram["norm_w"]).then_inc(w_in, 16)
            sp.dma_start(inw[:, :, :], dram["in_w"]).then_inc(w_in, 16)
            sp.dma_start(skw[:, :, :], dram["skip_w"]).then_inc(w_in, 16)
            sp.dma_start(convw[:, :, :], dram["conv_w"]).then_inc(w_conv, 16)
            sp.dma_start(convb[:, :], dram["conv_b"]).then_inc(w_conv, 16)
            sp.dma_start(wd2b[:, :], dram["wd2_b"]).then_inc(w_conv, 16)
            sp.dma_start(wskip[:, :], dram["W_D"]).then_inc(w_conv, 16)
            sp.dma_start(wd1[:, :, :], dram["wd1"]).then_inc(w_d, 16)
            sp.dma_start(wd2[:, :], dram["wd2"]).then_inc(w_d, 16)
            for k in range(4):
                sp.dma_start(wbc[:, :, 32 * k:32 * k + N], dram["wB"]).then_inc(w_bc, 16)
                sp.dma_start(wbc[:, :, 32 * k + N:32 * k + 2 * N], dram["wC"]).then_inc(w_bc, 16)
            sp.dma_start(negA[:, :, :], dram["A_log"]).then_inc(w_A, 16)
            sp.dma_start(res_v[:, 2:, :], x_v[:, 2:, :]).then_inc(x_rest, 16)
            sp.dma_start(outw[:, :, :], dram["out_w"]).then_inc(w_out, 16)

        @block.gpsimd
        def _(pool):
            own = Chain(pool, pool_own)

            def first():
                pool.memset(mhalf[:, :, :], -0.5)
                pool.memset(pick[:, :], 0.0)
                own.link(pool.memset(ident[:, :], 0.0))
                own.link(pool.affine_select(out=ident[:, :], in_=ident[:, :], compare_op=ALU.not_equal, fill=1.0,
                                            base=0, pattern=[[-1, P]], channel_multiplier=1))
                for row in (0, 64, 96):
                    last = pool.affine_select(out=pick[:, :], in_=pick[:, :], compare_op=ALU.not_equal,
                                              fill=1.0, base=-row, pattern=[[-1, 2 * N]], channel_multiplier=1)
                    own.link(last)
                pool.memset(pause[:, 1:2], 0.0).then_inc(const_ready, 1)
                part("factors", 0, 0)
                part("dx", 0, 0)

            def part(name, c, q):
                if name == "factors":
                    pool.wait_ge(stats_ready, c + 1)
                    pool.tensor_tensor(sc[:, 2:4, :], sc[:, 0:2, :], mhalf[:, :, :], ALU.pow).then_inc(norm_ready, 1)
                elif name == "dx":
                    pool.wait_ge(delta_ready, c + 1)
                    pool.tensor_tensor(dx[:, q, :, :], delta[:, q, :, :], xs[:, q, :, :], ALU.mult).then_inc(dx_ready, 1)

            def slots(c, q, which, finish):
                for n in which:
                    if finish and n == MULTIPLIED:
                        pool.wait_ge(y_read, c)
                        pool.tensor_tensor(gate[:, 1 - q, :, :], gate[:, 1 - q, :, :], xs[:, 1 - q, :, :],
                                           ALU.mult).then_inc(gate_done, 1)
                    parts(POOL_AT, n, c, part, q)
                    m = N * c + n
                    pool.wait_ge(h_ready, m + 1)
                    pool.wait_ge(C_ready, m + 1)
                    u = U[:, n % RING, :, :]
                    pool.tensor_tensor(u, u, Csb[:, n % 2, :].unsqueeze(1).to_broadcast([P, KE, CHUNK]),
                                       ALU.mult).then_inc(hc_ready, 1)

            schedule(lambda c, q, more: slots(c, q, HEAD, more), lambda c, q, _: slots(c, q, TAIL, False),
                     pool.Fori, first)
            pool.wait_ge(y_read, CHUNKS)
            pool.tensor_tensor(gate[:, 1, :, :], gate[:, 1, :, :], xs[:, 1, :, :], ALU.mult).then_inc(gate_done, 1)

        @block.tensor
        def _(pe):
            def take(c, i):
                if i >= 2:
                    pe.wait_ge(job_free, JOBS * c + i - 1)
                else:
                    need(pe, out_free, 2 * c - 1 + i)
                return job[:, i % 2, :]

            def mm(out, pairs):
                for k, (w, x) in enumerate(pairs):
                    last = nc.tensor.matmul(out, w, x, start=k == 0, stop=k == len(pairs) - 1)
                return last

            def part(name, c, q):
                if name == "turn":
                    pe.wait_ge(rn_ready, c + 1)
                    for k in range(KD):
                        out = take(c, k)
                        for j in range(TILES):
                            last = nc.tensor.transpose(out[:, j * P:(j + 1) * P], rn[:, j, k * P:(k + 1) * P],
                                                       ident[:, :])
                        last.then_inc(job_full, 1)
                elif name[:2] == "in":
                    g = int(name[2])
                    if g == 0:
                        pe.wait_ge(job_free, JOBS * c + 2)
                    for i in (g,):
                        w = inw if i < KE else skw
                        out = take(c, 2 + i)
                        e = i % KE * P
                        mm(out, [(w[:, k, e:e + P], rnT[:, k, :]) for k in range(KD)]).then_inc(job_full, 1)
                elif name == "low":
                    pe.wait_ge(xs_ready, c + 1)
                    mm(take(c, 10), [(wd1[:, k, :], xs[:, q, k, :]) for k in range(KE)]).then_inc(job_full, 1)
                elif name == "bc":
                    mm(take(c, 11), [(wbc[:, k, :], xs[:, q, k, :]) for k in range(KE)]).then_inc(job_full, 1)
                elif name[:2] == "dt":
                    e = int(name[2])
                    if e == 0:
                        pe.wait_ge(job_free, JOBS * c + 11)
                    if True:
                        mm(take(c, 12 + e), [(wd2[:, e * P:(e + 1) * P], rT[:, :])]).then_inc(job_full, 1)

            def spread(c, n, q):
                m = N * c + n
                if n == 0:
                    pe.wait_ge(split_done, c + 1)
                need(pe, mult_done, m)
                nc.tensor.matmul(psB[:, :], pick[:, n:n + 1].to_broadcast([P, P]), stack[:, q, :], start=True, stop=True).then_inc(B_full, 1)
                need(pe, C_ready, m)
                nc.tensor.matmul(psC[:, :], pick[:, N + n:N + n + 1].to_broadcast([P, P]), stack[:, q, :], start=True,
                                 stop=True).then_inc(C_full, 1)

            def nsum(c, n, q):
                m = N * c + n
                pe.wait_ge(hc_ready, m + 1)
                if n == 0:
                    need(pe, y_read, c)
                for e in range(KE):
                    last = nc.tensor.matmul(y[:, e, :], ident[:, :], U[:, n % RING, e, :], start=n == 0,
                                            stop=n == N - 1)
                last.then_inc(nsum_done, 1)

            def output(c, q, which):
                pe.wait_ge(gate_done, c + 1)
                for i in which:
                    if isinstance(c, int) and c == CHUNKS - 1:
                        pe.wait_ge(out_free, 2 * c + 1 + i)
                    else:
                        pe.wait_ge(job_free, JOBS * (c + 1) + JOBS - 1 + i)
                    for h in range(2):
                        for k in range(KE):
                            last = nc.tensor.matmul(job[:, i, h * D:(h + 1) * D],
                                                    in_time(gate[:, q, k, :])[:, i, h, :], outw[:, k, :],
                                                    start=k == 0, stop=k == KE - 1)
                    last.then_inc(out_full, 1)

            def slots(c, q, which, finish, last=False):
                for n in which:
                    if n < N - 1:
                        spread(c, n + 1, q)
                    elif not last:
                        spread(c + 1, 0, 1 - q)
                    parts(PE_AT, n, c, part, q)
                    if n > 0:
                        nsum(c, n - 1, q)
                    elif finish:
                        nsum(c - 1, N - 1, 1 - q)
                    if finish and n in OUT:
                        output(c - 1, 1 - q, (OUT.index(n),))

            def head(c, q, more):
                slots(c, q, HEAD, more)

            def tail(c, q, more):
                slots(c, q, TAIL, False, not more)

            def first():
                pe.wait_ge(const_ready, 1)
                pe.wait_ge(w_in, 48)
                part("turn", 0, 0)
                for i in range(8):
                    part(f"in{i}", 0, 0)
                pe.wait_ge(w_d, 32)
                pe.wait_ge(w_bc, 128)
                part("low", 0, 0)
                part("bc", 0, 0)
                for e in range(KE):
                    part(f"dt{e}", 0, 0)
                spread(0, 0, 0)
                pe.wait_ge(w_out, 16)

            schedule(head, tail, pe.Fori, first)
            nsum(CHUNKS - 1, N - 1, 1)
            output(CHUNKS - 1, 1, range(2))

        @block.scalar
        def _(act):
            own = Chain(act, act_own)

            def part(name, c, q):
                def full(i):
                    act.wait_ge(job_full, JOBS * c + i + 1)

                if name == "turn":
                    for k in range(KD):
                        full(k)
                        nc.scalar.activation(in_time(rnT[:, k, :]),
                                             job[:, k, :].rearrange("x (b h p) -> x b h p", b=2, h=2), ACT.Copy,
                                             scale=normw[:, k:k + 1]).then_inc(job_free, 1)
                elif name[:2] == "in":
                    for i in (int(name[2]),):
                        full(2 + i)
                        ps = job[:, i % 2, :]
                        if i < KE:
                            nc.scalar.activation(xin[:, i, 3 + CHUNK * q:3 + CHUNK * (q + 1)], ps, ACT.Copy)
                            nc.scalar.activation(work[:, i, :], ps, ACT.Identity, bias=convb[:, i:i + 1],
                                                 scale=convw[:, i, TAPS - 1:TAPS]).then_inc(job_free, 1)
                        else:
                            own_gate = nc.scalar.activation(gate[:, q, i - KE, :], ps, ACT.Copy)
                            own_gate.then_inc(job_free, 1)
                elif name == "silu":
                    act.wait_ge(conv_done, c + 1)
                    act.wait_ge(job_free, JOBS * c + 10)
                    nc.scalar.activation(xs[:, q, :, :], work[:, :, :], ACT.Silu).then_inc(xs_ready, 1)
                    nc.scalar.activation(gate[:, q, :, :], gate[:, q, :, :], ACT.Silu)
                    nc.scalar.preload_act_table_set(EXP_LN_SET)
                elif name == "low":
                    full(10)
                    nc.scalar.activation(rT[:, :], job[:, 0, :], ACT.Copy).then_inc(job_free, 1)
                elif name == "bc":
                    full(11)
                    nc.scalar.activation(rawbc, job[:, 1, :], ACT.Copy).then_inc(job_free, 1)
                elif name[:2] == "dt":
                    for e in (int(name[2]),):
                        full(12 + e)
                        nc.scalar.activation(delta[:, q, e, :], job[:, e % 2, :], ACT.Identity,
                                             bias=wd2b[:, e:e + 1]).then_inc(job_free, 1)
                elif name == "softplus":
                    act.wait_ge(zmin_ready, c + 1)
                    own.link(nc.scalar.activation(work[:, :, :], work[:, :, :], ACT.Exp))
                    nc.scalar.activation(work[:, :, :], work[:, :, :], ACT.Ln, bias=1.0).then_inc(ln_ready, 1)

            def slots(c, q, which):
                for n in which:
                    m = N * c + n
                    if n == 0:
                        act.wait_ge(delta_ready, c + 1)
                    need(act, h_ready, m - 1)
                    for e in range(KE):
                        last = nc.scalar.activation(dA[:, n % 2, e, :], delta[:, q, e, :], ACT.Exp,
                                                    scale=negA[:, e, n:n + 1])
                    last.then_inc(dA_ready, 1)
                    act.wait_ge(C_full, m + 1)
                    need(act, hc_ready, m - 1)
                    nc.scalar.activation(Csb[:, n % 2, :], psC[:, :], ACT.Copy).then_inc(C_ready, 1)
                    parts(ACT_AT, n, c, part, q)

            def first():
                act.wait_ge(w_A, 16)
                own.link(nc.scalar.activation(negA[:, :, :], negA[:, :, :], ACT.Exp))
                own.link(nc.scalar.activation(negA[:, :, :], negA[:, :, :], ACT.Copy, scale=-1.0))
                act.wait_ge(w_in, 48)
                act.wait_ge(w_conv, 64)
                for name in [n for names in ACT_AT.values() for n in names]:
                    part(name, 0, 0)

            schedule(lambda c, q, _: slots(c, q, HEAD), lambda c, q, _: slots(c, q, TAIL), act.Fori, first, 2, own)

        @block.vector
        def _(dve):
            own = Chain(dve, dve_own)

            def part(name, c, q):
                if name == "stats":
                    for j in range(TILES):
                        last = nc.vector.bn_stats(stats[:, j, :], res[:, TILES * c + j, :])
                    own.link(last)
                    nc.vector.memset(pause[:, 0:1], 0.0)
                    for j in range(TILES):
                        last = nc.vector.bn_aggr(mv[:, j, :], stats[:, j, :])
                    own.link(last)
                    nc.vector.tensor_scalar(sc[:, 0, :], mv[:, :, 1], EPS, None, ALU.add)
                    nc.vector.tensor_scalar(sc[:, 1, :], mv[:, :, 1], 1.0 + EPS, EPS * EPS, ALU.mult,
                                            ALU.add).then_inc(stats_ready, 1)
                elif name == "norm":
                    dve.wait_ge(norm_ready, c + 1)
                    nc.vector.tensor_scalar(sc[:, 4, :], sc[:, 2, :], 1.0, None, ALU.add)
                    own.link(nc.vector.tensor_tensor(sc[:, 5, :], mv[:, :, 0], sc[:, 2, :], ALU.mult))
                    need(dve, job_full, JOBS * (c - 1) + 2)
                    for j in range(TILES):
                        last = nc.vector.tensor_scalar(rn[:, j, :], res[:, TILES * c + j, :], mv[:, j, 0:1],
                                                       sc[:, 3, j:j + 1], ALU.subtract, ALU.mult)
                    last.then_inc(rn_ready, 1)
                    for j in range(TILES):
                        x = res[:, TILES * c + j, :]
                        nc.vector.tensor_scalar(x, x, sc[:, 4, j:j + 1], sc[:, 5, j:j + 1], ALU.mult, ALU.subtract)
                elif name[:4] == "conv":
                    for e in (int(name[4]),):
                        dve.wait_ge(job_free, JOBS * c + 3 + e)
                        for k in range(TAPS - 1):
                            at = CHUNK * q + k
                            last = nc.vector.scalar_tensor_tensor(work[:, e, :], xin[:, e, at:at + CHUNK],
                                                                  convw[:, e, k:k + 1], work[:, e, :],
                                                                  ALU.mult, ALU.add)
                            if k < TAPS - 2:
                                own.link(last)
                    if name == "conv3":
                        last.then_inc(conv_done, 1)
                elif name == "split":
                    dve.wait_ge(job_free, JOBS * c + 12)
                    own.link(nc.vector.tensor_copy(stack[:, q, :], rawbc))
                    for p in (64, 96):
                        own.link(nc.vector.tensor_tensor(rawbc[p:, :], rawbc[p:, :], stack[p:, q, :], ALU.subtract))
                        last = nc.vector.tensor_copy(stack[p:, q, :], rawbc[p:, :])
                        if p == 64:
                            own.link(last)
                    last.then_inc(split_done, 1)
                elif name == "least":
                    dve.wait_ge(job_free, JOBS * c + 16)
                    nc.vector.tensor_scalar(work[:, :, :], delta[:, q, :, :], 40.0, None,
                                            ALU.min).then_inc(zmin_ready, 1)
                elif name == "delta":
                    dve.wait_ge(ln_ready, c + 1)
                    nc.vector.tensor_tensor(delta[:, q, :, :], delta[:, q, :, :], work[:, :, :],
                                            ALU.max).then_inc(delta_ready, 1)

            def unit(c, n, q):
                m = N * c + n
                u = U[:, n % RING, :, :]
                dve.wait_ge(B_full, m + 1)
                if n == 0:
                    dve.wait_ge(dx_ready, c + 1)
                need(dve, nsum_done, m - RING + 1)
                nc.vector.tensor_tensor(u, dx[:, q, :, :], psB[:, :].unsqueeze(1).to_broadcast([P, KE, CHUNK]),
                                        ALU.mult).then_inc(mult_done, 1)
                dve.wait_ge(mult_done, m + 1)
                dve.wait_ge(dA_ready, m + 1)
                for e in range(KE):
                    start = carry[:, e, n:n + 1] if q else 0.0
                    last = nc.vector.tensor_tensor_scan(u[:, e, :], dA[:, n % 2, e, :], u[:, e, :], start,
                                                        ALU.mult, ALU.add)
                if q == 0:
                    own.link(last)
                    last = nc.vector.tensor_copy(carry[:, :, n], u[:, :, CHUNK - 1])
                last.then_inc(h_ready, 1)

            def gated(c, q):
                dve.wait_ge(nsum_done, N * c + N)
                for e in range(KE):
                    x = xs[:, q, e, :]
                    last = nc.vector.scalar_tensor_tensor(x, x, wskip[:, e:e + 1], y[:, e, :], ALU.mult, ALU.add)
                last.then_inc(y_read, 1)

            def add_output(c, which):
                for i in which:
                    dve.wait_ge(out_full, 2 * c + 1 + i)
                    x = res[:, :, :].rearrange("p (s h) d -> p s (h d)", h=2)[:, 2 * c + i, :]
                    nc.vector.tensor_tensor(x, x, job[:, i, :], ALU.add).then_inc(out_free, 1)

            def head(c, q, more):
                for n in HEAD:
                    unit(c, n, q)
                    parts(DVE_AT, n, c, part, q)
                    if more and n == GATED:
                        gated(c - 1, 1 - q)
                    if more and n in ADDED:
                        add_output(c - 1, (ADDED.index(n),))

            def tail(c, q, more):
                for n in TAIL:
                    unit(c, n, q)
                    parts(DVE_AT, n, c, part, q)

            def first():
                nc.vector.memset(stats[:, :, :], 0.0).then_inc(out_free, 2)
                own.link(nc.vector.memset(xin[:, :, 0:3], 0.0))
                dve.wait_ge(x_first, 16)
                dve.wait_ge(w_conv, 64)
                for names in DVE_AT.values():
                    for name in names:
                        part(name, 0, 0)
                dve.wait_ge(x_rest, 16)

            schedule(head, tail, dve.Fori, first, 46, own)
            gated(CHUNKS - 1, 1)
            add_output(CHUNKS - 1, range(2))


HIDDEN, KEYS, EXPERTS, TOP = 1024, 64, 512, 8
KM = (HIDDEN + EXPERTS) // P
KH = HIDDEN // P
ROWS = TOP * KEYS
assert ROWS == EXPERTS


def ffn(nc, res, dram, name):
    ctx = ExitStack()
    with ctx:
        def sb(what, shape, dt=FP32):
            return ctx.enter_context(nc.sbuf_tensor(f"{name}_{what}", shape, dt))

        def sem(what):
            return ctx.enter_context(nc.semaphore(f"{name}_{what}"))

        def ps(what, shape):
            return ctx.enter_context(nc.psum_tensor(f"{name}_{what}", shape, FP32))

        wq = sb("wq", [P, KD, P])
        keyz = sb("keyz", [P, 2, 2, KEYS])
        gw = sb("gw", [P, KD, HIDDEN])
        uw = sb("uw", [P, KD, HIDDEN])
        dw = sb("dw", [P, KD, EXPERTS])
        lw = sb("lw", [P, KM, D])
        ident = sb("ident", [P, P])
        mhalf = sb("mhalf", [P, CHUNKS, TILES])
        eps = sb("eps", [P, CHUNKS, TILES])
        pause = sb("pause", [P, 4])

        stats = sb("stats", [P, TILES, 6])
        mv4 = sb("mv4", [P, TILES, 2])
        mv = sb("mv", [P, CHUNKS, TILES, 2])
        s1 = sb("s1", [P, CHUNKS, TILES])
        zn = sb("zn", [P, 2, TILES, D])
        zT = sb("zT", [P, KD, CHUNKS, CHUNK])
        QT = sb("QT", [P, CHUNKS, CHUNK])
        qs = sb("qs", [P, 2, CHUNK // 2])
        Rt = sb("Rt", [P, 2, 2, 2, KEYS])
        top1 = sb("top1", [P, TILES, 2, TOP])
        sums = sb("sums", [P, TILES, TOP, TOP])
        top2 = sb("top2", [P, TILES, TOP])
        ex = sb("ex", [P, TILES, TOP + KEYS + TOP])
        total = sb("total", [P, TILES])
        S = sb("S", [P, TILES, TOP, KEYS])
        W = sb("W", [P, TILES, TOP, KEYS])
        C = sb("C", [P, TILES, EXPERTS])
        csum = sb("csum", [P, TILES])
        sil = sb("sil", [P, 2, CHUNK])
        H = sb("H", [P, 2, KM, CHUNK])

        psG, psU, psR, psO = ps("psG", [P, 2, CHUNK]), ps("psU", [P, 2, CHUNK]), ps("psR", [P, CHUNK]), ps("psO", [P, 2, CHUNK])

        w_q, w_keys, w_gate, w_up, w_embed, w_low = (sem(s) for s in
                                                     ("w_q", "w_keys", "w_gate", "w_up", "w_embed", "w_low"))
        const_ready, keyz_clear = sem("const_ready"), sem("keyz_clear")
        stats_ready, norm_ready, zn_ready = sem("stats_ready"), sem("norm_ready"), sem("zn_ready")
        turn_full, zT_ready, q_full, QT_ready = sem("turn_full"), sem("zT_ready"), sem("q_full"), sem("QT_ready")
        qs_ready, route_full, Rt_ready = sem("qs_ready"), sem("route_full"), sem("Rt_ready")
        dif_ready, exp_ready, ex_ready, SW_ready, C_ready = (sem(s) for s in ("dif_ready", "exp_ready", "ex_ready",
                                                                              "SW_ready", "C_ready"))
        g_full, g_free, u_full, u_free = sem("g_full"), sem("g_free"), sem("u_full"), sem("u_free")
        out_full, out_free = sem("out_full"), sem("out_free")
        dve_own, pool_own = sem("dve_own"), sem("pool_own")
        SPREAD = [P, TILES, TOP, KEYS]

        def tile(t):
            return Rt[:, :, t, :, :]

        block = ctx.enter_context(nc.Block())

        @block.sync
        def _(sp):
            sp.dma_start(wq[:, :, :], dram["W_q"]).then_inc(w_q, 16)
            sp.wait_ge(keyz_clear, 1)
            sp.dma_start(keyz[0:64, :, 0, :], dram["keys"]).then_inc(w_keys, 16)
            sp.dma_start(keyz[64:128, :, 1, :], dram["keys"]).then_inc(w_keys, 16)
            sp.dma_start(gw[:, :, :], dram["gate_w"]).then_inc(w_gate, 16)
            sp.dma_start(uw[:, :, :], dram["up_w"]).then_inc(w_up, 16)
            sp.dma_start(dw[:, :, :], dram["down_embed"]).then_inc(w_embed, 16)
            sp.dma_start(lw[:, :, :], dram["lower_w"]).then_inc(w_low, 16)

        @block.gpsimd
        def _(pool):
            own = Chain(pool, pool_own)
            pool.memset(keyz[:, :, :, :], 0.0).then_inc(keyz_clear, 1)
            pool.memset(mhalf[:, :, :], -0.5)
            pool.memset(eps[:, :, :], EPS)
            own.link(pool.memset(ident[:, :], 0.0))
            pool.affine_select(out=ident[:, :], in_=ident[:, :], compare_op=ALU.not_equal, fill=1.0, base=0,
                               pattern=[[-1, P]], channel_multiplier=1).then_inc(const_ready, 1)
            pool.wait_ge(stats_ready, CHUNKS)
            own.link(pool.tensor_tensor(s1[:, :, :], mv[:, :, :, 1], eps[:, :, :], ALU.add))
            pool.tensor_tensor(s1[:, :, :], s1[:, :, :], mhalf[:, :, :], ALU.pow).then_inc(norm_ready, 1)
            with pool.Fori(0, CHUNKS) as c:
                pool.wait_ge(Rt_ready, c + 1)
                for b in range(2):
                    pool.tensor_tensor(S[:, 2 * b:2 * b + 2, :, :],
                                       Rt[:, b, 0, :, 0:TOP].unsqueeze(3).to_broadcast([P, 2, TOP, KEYS]),
                                       Rt[:, b, 1, :, :].unsqueeze(2).to_broadcast([P, 2, TOP, KEYS]), ALU.add)
                pool.wait_ge(ex_ready, c + 1)
                pool.tensor_tensor(W[:, :, :, :], ex[:, :, 0:TOP].unsqueeze(3).to_broadcast(SPREAD),
                                   ex[:, :, TOP:TOP + KEYS].unsqueeze(2).to_broadcast(SPREAD),
                                   ALU.mult).then_inc(SW_ready, 1)

        @block.tensor
        def _(pe):
            pe.wait_ge(const_ready, 1)
            pe.wait_ge(w_q, 16)

            def turn(c, q):
                pe.wait_ge(zn_ready, c + 1)
                bank = (psG, psU)[q]
                for k in range(KD):
                    for j in range(TILES):
                        last = nc.tensor.transpose(bank[:, k, j * P:(j + 1) * P], zn[:, q, j, k * P:(k + 1) * P],
                                                   ident[:, :])
                last.then_inc(turn_full, 1)

            def queries(c, q):
                pe.wait_ge(zT_ready, c + 1)
                for k in range(KD):
                    last = nc.tensor.matmul(psO[:, q, :], wq[:, k, :], zT[:, k, c, :], start=k == 0, stop=k == KD - 1)
                last.then_inc(q_full, 1)

            with pe.Fori(0, CHUNKS // 2) as b:
                turn(2 * b, 0)
                turn(2 * b + 1, 1)
                queries(2 * b, 0)
                queries(2 * b + 1, 1)

            def upper(c, i):
                wg, e = (gw, i) if i < KH else (dw, i - KH)
                pe.wait_ge(g_free, KM * c + i + 1)
                for k in range(KD):
                    last = nc.tensor.matmul(psG[:, i % 2, :], wg[:, k, e * P:(e + 1) * P], zT[:, k, c, :],
                                            start=k == 0, stop=k == KD - 1)
                last.then_inc(g_full, 1)
                pe.wait_ge(u_free, KM * c + i + 1)
                if i < KH:
                    for k in range(KD):
                        last = nc.tensor.matmul(psU[:, i % 2, :], uw[:, k, e * P:(e + 1) * P], zT[:, k, c, :],
                                                start=k == 0, stop=k == KD - 1)
                else:
                    if i == KH:
                        pe.wait_ge(C_ready, c + 1)
                    for j in range(TILES):
                        last = nc.tensor.transpose(psU[:, i % 2, j * P:(j + 1) * P], C[:, j, e * P:(e + 1) * P],
                                                   ident[:, :])
                last.then_inc(u_full, 1)

            def chunk(c, q):
                for i in range(KM):
                    upper(c, i)
                    if i == 0:
                        pe.wait_ge(qs_ready, c + 1)
                        for b in range(2):
                            for t in range(2):
                                last = nc.tensor.matmul(psR[:, (2 * b + t) * P:(2 * b + t + 1) * P],
                                                        qs[:, t, b * P:(b + 1) * P],
                                                        keyz[:, t, :, :].rearrange("p h k -> p (h k)"),
                                                        start=True, stop=True)
                        last.then_inc(route_full, 1)
                for i in range(2):
                    pe.wait_ge(out_free, 2 * c + i + 1)
                    for h in range(2):
                        j = 2 * i + h
                        for k in range(KM):
                            if i == 0 and h == 0 and k in (0, KH):
                                pe.wait_ge(u_free, KM * c + 2 + (KH if k == 0 else KM))
                            last = nc.tensor.matmul(psO[:, i, h * D:(h + 1) * D], H[:, q, k, j * P:(j + 1) * P],
                                                    lw[:, k, :], start=k == 0, stop=k == KM - 1)
                    last.then_inc(out_full, 1)

            pe.wait_ge(QT_ready, CHUNKS)
            pe.wait_ge(w_keys, 32)
            pe.wait_ge(w_gate, 16)
            pe.wait_ge(w_up, 16)
            pe.wait_ge(w_embed, 16)
            pe.wait_ge(w_low, 16)
            with pe.Fori(0, CHUNKS // 2) as b:
                chunk(2 * b, 0)
                chunk(2 * b + 1, 1)

        @block.scalar
        def _(act):
            def fetch(c, q):
                act.wait_ge(turn_full, c + 1)
                nc.scalar.activation(zT[:, :, c, :], (psG, psU)[q][:, :, :], ACT.Copy).then_inc(zT_ready, 1)

            def keep_queries(c, q):
                act.wait_ge(q_full, c + 1)
                nc.scalar.activation(in_time(QT[:, c, :]), psO[:, q, :].rearrange("x (b h p) -> x b h p", b=2, h=2),
                                     ACT.Copy).then_inc(QT_ready, 1)

            with act.Fori(0, CHUNKS // 2) as b:
                fetch(2 * b, 0)
                fetch(2 * b + 1, 1)
                keep_queries(2 * b, 0)
                keep_queries(2 * b + 1, 1)
            act.wait_ge(QT_ready, CHUNKS)
            pairs = QT[:, :, :].rearrange("x (t s) (u w) -> x t (s u) w", t=2, u=2)
            with act.Fori(0, CHUNKS) as c:
                nc.scalar.activation(qs[:, :, :], pairs[:, :, c, :], ACT.Copy).then_inc(qs_ready, 1)
                for i in range(KM):
                    act.wait_ge(g_full, KM * c + i + 1)
                    act.wait_ge(u_free, KM * c + i + 1)
                    nc.scalar.activation(sil[:, i % 2, :], psG[:, i % 2, :], ACT.Silu).then_inc(g_free, 1)
                    if i == 0:
                        act.wait_ge(route_full, c + 1)
                        nc.scalar.activation(Rt[:, :, :, :, :].rearrange("p b t h k -> p (b t h k)"), psR[:, :],
                                             ACT.Copy).then_inc(Rt_ready, 1)
                    if i == 3:
                        act.wait_ge(dif_ready, c + 1)
                        nc.scalar.activation(ex[:, :, :], ex[:, :, :], ACT.Exp).then_inc(exp_ready, 1)

        @block.vector
        def _(dve):
            own = Chain(dve, dve_own)
            nc.vector.memset(pause[:, 1:2], 0.0).then_inc(g_free, 2)
            nc.vector.memset(pause[:, 2:3], 0.0).then_inc(u_free, 2)
            nc.vector.memset(pause[:, 3:4], 0.0).then_inc(out_free, 2)
            with dve.Fori(0, CHUNKS) as c:
                own.enter(c, 2)
                for j in range(TILES):
                    last = nc.vector.bn_stats(stats[:, j, :], res[:, TILES * c + j, :])
                own.link(last)
                nc.vector.memset(pause[:, 0:1], 0.0)
                for j in range(TILES):
                    last = nc.vector.bn_aggr(mv4[:, j, :], stats[:, j, :])
                own.link(last)
                nc.vector.tensor_copy(mv[:, c, :, :], mv4[:, :, :]).then_inc(stats_ready, 1)
                own.leave(CHUNKS)

            def normalise(c, q):
                need(dve, turn_full, c - 1)
                for j in range(TILES):
                    last = nc.vector.tensor_scalar(zn[:, q, j, :], res[:, TILES * c + j, :], mv[:, c, j, 0:1],
                                                   s1[:, c, j:j + 1], ALU.subtract, ALU.mult)
                last.then_inc(zn_ready, 1)

            dve.wait_ge(norm_ready, 1)
            normalise(0, 0)
            normalise(1, 1)
            with dve.Fori(1, CHUNKS // 2) as b:
                normalise(2 * b, 0)
                normalise(2 * b + 1, 1)

            def highest(c):
                dve.wait_ge(Rt_ready, c + 1)
                nc.vector.memset(pause[:, 0:1], 0.0)
                for j in range(TILES):
                    for t in range(2):
                        last = nc.vector.max(top1[:, j, t, :], tile(t)[:, j // 2, j % 2, :])
                own.link(last)
                four = [P, TILES, TOP, TOP]
                own.link(nc.vector.tensor_tensor(sums[:, :, :, :], top1[:, :, 0, :].unsqueeze(3).to_broadcast(four),
                                                 top1[:, :, 1, :].unsqueeze(2).to_broadcast(four), ALU.add))
                nc.vector.memset(pause[:, 0:1], 0.0)
                for j in range(TILES):
                    last = nc.vector.max(top2[:, j, :], sums[:, j, :, :].rearrange("p a b -> p (a b)"))
                own.link(last)
                for t, (at, n) in enumerate(((0, TOP), (TOP, KEYS))):
                    part = ex[:, :, at:at + n].rearrange("p (b h) k -> p b h k", b=2)
                    greatest = top1[:, :, t, 0:1].rearrange("p (b h) k -> p b h k", b=2).to_broadcast([P, 2, 2, n])
                    nc.vector.tensor_tensor(part, tile(t)[:, :, :, 0:n], greatest, ALU.subtract)
                nc.vector.tensor_tensor(ex[:, :, TOP + KEYS:], top2[:, :, :],
                                        top2[:, :, 0:1].to_broadcast([P, TILES, TOP]),
                                        ALU.subtract).then_inc(dif_ready, 1)

            def normalise_softmax(c):
                dve.wait_ge(exp_ready, c + 1)
                own.link(nc.vector.reduce_sum(total[:, :], ex[:, :, TOP + KEYS:], AX.X))
                own.link(nc.vector.reciprocal(total[:, :], total[:, :]))
                nc.vector.tensor_tensor(ex[:, :, 0:TOP], ex[:, :, 0:TOP],
                                        total[:, :].unsqueeze(2).to_broadcast([P, TILES, TOP]),
                                        ALU.mult).then_inc(ex_ready, 1)

            def coefficients(c):
                dve.wait_ge(SW_ready, c + 1)
                for j in range(TILES):
                    last = nc.vector.scalar_tensor_tensor(C[:, j, :], S[:, j, :, :].rearrange("p a b -> p (a b)"),
                                                          top2[:, j, TOP - 1:TOP],
                                                          W[:, j, :, :].rearrange("p a b -> p (a b)"),
                                                          ALU.is_ge, ALU.mult, accum_out=csum[:, j:j + 1])
                own.link(last)
                edge = C[:, :, EXPERTS - 1]
                own.link(nc.vector.tensor_tensor(edge, edge, csum[:, :], ALU.subtract))
                nc.vector.tensor_scalar(edge, edge, 1.0, None, ALU.add).then_inc(C_ready, 1)

            def product(c, q, i):
                dve.wait_ge(g_free, KM * c + i + 3)
                dve.wait_ge(u_full, KM * c + i + 1)
                nc.vector.tensor_tensor(H[:, q, i, :], psU[:, i % 2, :], sil[:, i % 2, :],
                                        ALU.mult).then_inc(u_free, 1)

            def chunk(c, q):
                for i in range(KM):
                    product(c, q, i)
                    if i == 0:
                        highest(c)
                    if i == 3:
                        normalise_softmax(c)
                    if i == KH - 1:
                        coefficients(c)
                for i in range(2):
                    dve.wait_ge(out_full, 2 * c + i + 1)
                    x = res[:, :, :].rearrange("p (s h) d -> p s (h d)", h=2)[:, 2 * c + i, :]
                    nc.vector.tensor_tensor(x, x, psO[:, i, :], ALU.add).then_inc(out_free, 1)

            with dve.Fori(0, CHUNKS // 2) as b:
                own.enter(b, 14)
                chunk(2 * b, 0)
                chunk(2 * b + 1, 1)
                own.leave(CHUNKS // 2)


HEADS, HD = 16, 16
SEQ_TILES = SEQ // P
Q_SCALE = 0.25


def attention(nc, res, dram):
    ctx = ExitStack()
    with ctx:
        def sb(what, shape, dt=FP32):
            return ctx.enter_context(nc.sbuf_tensor("a_" + what, shape, dt))

        def sem(what):
            return ctx.enter_context(nc.semaphore("a_" + what))

        def ps(what, shape):
            return ctx.enter_context(nc.psum_tensor("a_" + what, shape, FP32))

        wq = sb("wq", [P, KD, D])
        wkv = sb("wkv", [P, KD, 2 * D])
        wu = sb("wu", [P, KD, D])
        wo = sb("wo", [P, KD, D])
        ident = sb("ident", [P, P])
        same_head = sb("same_head", [P, P])
        mhalf = sb("mhalf", [P, TILES, HEADS])
        eps = sb("eps", [P, SEQ_TILES])
        pause = sb("pause", [P, 4])

        stats = sb("stats", [P, SEQ_TILES, 6])
        mv = sb("mv", [P, SEQ_TILES, 2])
        s1 = sb("s1", [P, SEQ_TILES])
        zn = sb("zn", [P, SEQ_TILES, D])
        zT = sb("zT", [P, KD, SEQ])
        kv = sb("kv", [P, SEQ_TILES, 2 * D])
        qT = sb("qT", [P, KD, SEQ])
        kvh = sb("kvh", [P, KD, P])
        square = sb("square", [P, TILES, D])
        su = sb("su", [P, TILES, D])
        ssq = sb("ssq", [P, TILES, HEADS])
        rinv = sb("rinv", [P, TILES, HEADS])
        og = sb("og", [P, TILES, D])
        ogT = sb("ogT", [P, TILES, D])

        ring = ps("ring", [P, 2, CHUNK])
        acc = ps("acc", [P, 2, CHUNK])
        ou = ps("ou", [P, TILES, 2 * D])

        w_q, w_kv, w_u, w_o, const_ready = sem("w_q"), sem("w_kv"), sem("w_u"), sem("w_o"), sem("const_ready")
        stats_ready, norm_ready, zn_ready = sem("stats_ready"), sem("norm_ready"), sem("zn_ready")
        ring_full, ring_free = sem("ring_full"), sem("ring_free")
        acc_full, kvh_ready, ou_full = sem("acc_full"), sem("kvh_ready"), sem("ou_full")
        square_ready, su_ready, ssq_ready, rinv_ready, og_ready = (sem(s) for s in (
            "square_ready", "su_ready", "ssq_ready", "rinv_ready", "og_ready"))
        out_full, out_free = sem("out_full"), sem("out_free")
        dve_own, pool_own = sem("dve_own"), sem("pool_own")

        TURN, KV, Q, BACK, JOBS = 0, 4, 12, 16, 20
        HALVES = SEQ // CHUNK

        block = ctx.enter_context(nc.Block())

        @block.sync
        def _(sp):
            sp.dma_start(wkv[:, :, :], dram["Wkv"]).then_inc(w_kv, 16)
            sp.dma_start(wq[:, :, :], dram["Wq"]).then_inc(w_q, 16)
            sp.dma_start(wu[:, :, :], dram["Wu"]).then_inc(w_u, 16)
            sp.dma_start(wo[:, :, :], dram["Wo"]).then_inc(w_o, 16)

        @block.gpsimd
        def _(pool):
            own = Chain(pool, pool_own)
            pool.memset(mhalf[:, :, :], -0.5)
            pool.memset(eps[:, :], EPS)
            pool.memset(same_head[:, :], 1.0)
            own.link(pool.memset(ident[:, :], 0.0))
            pool.affine_select(out=ident[:, :], in_=ident[:, :], compare_op=ALU.not_equal, fill=1.0, base=0,
                               pattern=[[-1, P]], channel_multiplier=1)
            blocks = same_head[:, :].rearrange("p (g w) -> p g w", w=HD)
            own.link(pool.affine_select(out=blocks, in_=blocks, compare_op=ALU.is_ge, fill=0.0, base=0,
                                        pattern=[[-HD, P // HD], [0, HD]], channel_multiplier=1))
            pool.affine_select(out=blocks, in_=blocks, compare_op=ALU.is_ge, fill=0.0, base=HD - 1,
                               pattern=[[HD, P // HD], [0, HD]], channel_multiplier=-1).then_inc(const_ready, 1)
            with pool.Fori(0, BATCH) as b:
                own.enter(b, 1)
                pool.wait_ge(stats_ready, b + 1)
                own.link(pool.tensor_tensor(s1[:, :], mv[:, :, 1], eps[:, :], ALU.add))
                pool.tensor_tensor(s1[:, :], s1[:, :], mhalf[:, 0, 0:SEQ_TILES], ALU.pow).then_inc(norm_ready, 1)
                for h in range(HALVES):
                    pool.wait_ge(ssq_ready, HALVES * b + h + 1)
                    pool.tensor_tensor(rinv[:, :, :], ssq[:, :, :], mhalf[:, :, :], ALU.pow).then_inc(rinv_ready, 1)
                own.leave(BATCH)

        @block.tensor
        def _(pe):
            pe.wait_ge(const_ready, 1)
            for s in (w_q, w_kv, w_u, w_o):
                pe.wait_ge(s, 16)
            with pe.Fori(0, BATCH) as b:
                def take(i):
                    pe.wait_ge(ring_free, JOBS * b + i + 1)
                    return ring[:, i % 2, :]

                def finished(i):
                    pe.wait_ge(ring_free, JOBS * b + i + 3)

                for half in range(HALVES):
                    pe.wait_ge(zn_ready, HALVES * b + half + 1)
                    for k in range(KD):
                        out = take(TURN + KD * half + k)
                        for j in range(TILES):
                            last = nc.tensor.transpose(out[:, j * P:(j + 1) * P],
                                                       zn[:, TILES * half + j, k * P:(k + 1) * P], ident[:, :])
                        last.then_inc(ring_full, 1)

                def heads_kv(j):
                    finished(KV + j)
                    if j == 0:
                        pe.wait_ge(out_free, 2 * HALVES * b + 2)
                    for g in range(KD):
                        last = nc.tensor.matmul(acc[:, g, 0:P], kv[:, j, g * P:(g + 1) * P],
                                                kv[:, j, D + g * P:D + (g + 1) * P], start=j == 0,
                                                stop=j == SEQ_TILES - 1)
                    if j == SEQ_TILES - 1:
                        last.then_inc(acc_full, 1)

                for j in range(SEQ_TILES):
                    if j % TILES == 0:
                        finished(TURN + KD * (j // TILES) + KD - 1)
                    out = take(KV + j)
                    for k in range(KD):
                        last = nc.tensor.matmul(out, zT[:, k, j * P:(j + 1) * P], wkv[:, k, :], start=k == 0,
                                                stop=k == KD - 1)
                    last.then_inc(ring_full, 1)
                    if j > 0:
                        heads_kv(j - 1)
                heads_kv(SEQ_TILES - 1)
                for half in range(HALVES):
                    for g in range(KD):
                        out = take(Q + KD * half + g)
                        for k in range(KD):
                            last = nc.tensor.matmul(out, wq[:, k, g * P:(g + 1) * P],
                                                    zT[:, k, half * CHUNK:(half + 1) * CHUNK], start=k == 0,
                                                    stop=k == KD - 1)
                        last.then_inc(ring_full, 1)
                for half in range(HALVES):
                    for j in range(TILES):
                        t = TILES * half + j
                        for k in range(KD):
                            last = nc.tensor.matmul(ou[:, j, D:], zT[:, k, t * P:(t + 1) * P], wu[:, k, :],
                                                    start=k == 0, stop=k == KD - 1)
                        if j == 0:
                            finished(Q + KD * half + KD - 1)
                            pe.wait_ge(kvh_ready, b + 1)
                        for g in range(KD):
                            last = nc.tensor.matmul(ou[:, j, g * P:(g + 1) * P], qT[:, g, t * P:(t + 1) * P],
                                                    kvh[:, g, :], start=True, stop=True)
                        last.then_inc(ou_full, 1)
                    for i in range(2):
                        out = take(BACK + 2 * half + i)
                        for h in range(2):
                            pe.wait_ge(og_ready, SEQ_TILES * b + TILES * half + 2 * i + h + 1)
                            for g in range(KD):
                                last = nc.tensor.transpose(out[:, (2 * h + g) * P:(2 * h + g + 1) * P],
                                                           og[:, 2 * i + h, g * P:(g + 1) * P], ident[:, :])
                        last.then_inc(ring_full, 1)
                    for i in range(2):
                        finished(BACK + 2 * half + i)
                        pe.wait_ge(out_free, 2 * HALVES * b + 2 * half + i + 1)
                        if half == 0 and i == 0:
                            pe.wait_ge(kvh_ready, b + 1)
                        for h in range(2):
                            for g in range(KD):
                                last = nc.tensor.matmul(acc[:, i, h * D:(h + 1) * D],
                                                        ogT[:, 2 * i + h, g * P:(g + 1) * P], wo[:, g, :],
                                                        start=g == 0, stop=g == KD - 1)
                        last.then_inc(out_full, 1)

        @block.scalar
        def _(act):
            with act.Fori(0, BATCH) as b:
                def full(i):
                    act.wait_ge(ring_full, JOBS * b + i + 1)
                    return ring[:, i % 2, :]

                for half in range(HALVES):
                    for k in range(KD):
                        ps_ = full(TURN + KD * half + k)
                        nc.scalar.activation(zT[:, k, half * CHUNK:(half + 1) * CHUNK], ps_,
                                             ACT.Copy).then_inc(ring_free, 1)
                for j in range(SEQ_TILES):
                    ps_ = full(KV + j)
                    nc.scalar.activation(kv[:, j, 0:D], ps_[:, 0:D], ACT.Relu, scale=Q_SCALE)
                    nc.scalar.activation(kv[:, j, D:], ps_[:, D:], ACT.Copy).then_inc(ring_free, 1)
                for half in range(HALVES):
                    for g in range(KD):
                        ps_ = full(Q + KD * half + g)
                        nc.scalar.activation(qT[:, g, half * CHUNK:(half + 1) * CHUNK], ps_, ACT.Relu,
                                             scale=Q_SCALE).then_inc(ring_free, 1)
                for half in range(HALVES):
                    for j in range(TILES):
                        act.wait_ge(ou_full, SEQ_TILES * b + TILES * half + j + 1)
                        nc.scalar.activation(square[:, j, :], ou[:, j, 0:D], ACT.Square).then_inc(square_ready, 1)
                        nc.scalar.activation(su[:, j, :], ou[:, j, D:], ACT.Silu).then_inc(su_ready, 1)
                    for i in range(2):
                        ps_ = full(BACK + 2 * half + i)
                        nc.scalar.activation(ogT[:, 2 * i:2 * i + 2, :].rearrange("p h d -> p (h d)"), ps_,
                                             ACT.Copy).then_inc(ring_free, 1)

        @block.vector
        def _(dve):
            own = Chain(dve, dve_own)
            nc.vector.memset(pause[:, 1:2], 0.0).then_inc(ring_free, 2)
            nc.vector.memset(pause[:, 2:3], 0.0).then_inc(out_free, 2)
            dve.wait_ge(const_ready, 1)
            with dve.Fori(0, BATCH) as b:
                own.enter(b, 5)
                for j in range(SEQ_TILES):
                    last = nc.vector.bn_stats(stats[:, j, :], res[:, SEQ_TILES * b + j, :])
                own.link(last)
                nc.vector.memset(pause[:, 0:1], 0.0)
                for j in range(SEQ_TILES):
                    last = nc.vector.bn_aggr(mv[:, j, :], stats[:, j, :])
                last.then_inc(stats_ready, 1)
                dve.wait_ge(norm_ready, b + 1)
                for half in range(HALVES):
                    for j in range(TILES * half, TILES * (half + 1)):
                        last = nc.vector.tensor_scalar(zn[:, j, :], res[:, SEQ_TILES * b + j, :], mv[:, j, 0:1],
                                                       s1[:, j:j + 1], ALU.subtract, ALU.mult)
                    last.then_inc(zn_ready, 1)
                dve.wait_ge(acc_full, b + 1)
                for g in range(KD):
                    last = nc.vector.tensor_tensor(kvh[:, g, :], acc[:, g, 0:P], same_head[:, :], ALU.mult)
                last.then_inc(kvh_ready, 1)
                for half in range(HALVES):
                    for j in range(TILES):
                        dve.wait_ge(square_ready, SEQ_TILES * b + TILES * half + j + 1)
                        last = nc.vector.reduce_sum(ssq[:, j, :], square[:, j, :].rearrange("p (h w) -> p h w", w=HD),
                                                    AX.X)
                    own.link(last)
                    nc.vector.tensor_scalar(ssq[:, :, :], ssq[:, :, :], 1.0 / HD, 1e-24, ALU.mult,
                                            ALU.max).then_inc(ssq_ready, 1)
                    dve.wait_ge(su_ready, SEQ_TILES * b + TILES * (half + 1))
                    for j in range(TILES):
                        last = nc.vector.tensor_tensor(og[:, j, :], su[:, j, :], ou[:, j, 0:D], ALU.mult)
                        own.link(last) if j == TILES - 1 else None
                    dve.wait_ge(rinv_ready, HALVES * b + half + 1)
                    for j in range(TILES):
                        o = og[:, j, :].rearrange("p (h w) -> p h w", w=HD)
                        nc.vector.tensor_tensor(o, o, rinv[:, j, :].unsqueeze(2).to_broadcast([P, HEADS, HD]),
                                                ALU.mult).then_inc(og_ready, 1)
                    for i in range(2):
                        dve.wait_ge(out_full, 2 * HALVES * b + 2 * half + i + 1)
                        x = res[:, :, :].rearrange("p (s h) d -> p s (h d)", h=2)[:, TILES * b + 2 * half + i, :]
                        nc.vector.tensor_tensor(x, x, acc[:, i, :], ALU.add).then_inc(out_free, 1)
                own.leave(BATCH)


def program(nc, dram, out):
    with nc.sbuf_tensor("res", [P, TOKENS // P, D], FP32) as res:
        mamba(nc, res, dram)
        ffn(nc, res, dram, "f")
        attention(nc, res, dram)
        ffn(nc, res, dram, "g")
        store(nc, res, out)


def store(nc, res, out):
    ctx = ExitStack()
    with ctx:
        done = ctx.enter_context(nc.semaphore("out_done"))
        block = ctx.enter_context(nc.Block())

        @block.sync
        def _(sp):
            out_v = out.rearrange("b (s p h) d -> p (b s) (h d)", p=P, h=2)
            sp.dma_start(out_v, res[:, :, :].rearrange("p (s h) d -> p s (h d)", h=2)).then_inc(done, 16)
            sp.wait_ge(done, 16)


def kernel(**inputs):
    import concourse.bacc as bacc
    from concourse.bass_utils import run_bass_kernel_spmd

    def a(name):
        return np.asarray(inputs["L0_" + name])

    def blocks(w):
        return np.ascontiguousarray(w.reshape(-1, P, w.shape[-1]).transpose(1, 0, 2))

    laid = {
        "x": a("attn_a_resid"),
        "norm_w": blocks(a("attn_a_norm_w")[:, None])[:, :, 0],
        "in_w": blocks(a("attn_a_in_w").T),
        "skip_w": blocks(a("attn_a_skip_w").T),
        "conv_w": blocks(a("attn_a_conv_w")),
        "conv_b": blocks(a("attn_a_conv_b")[:, None])[:, :, 0],
        "wd1": blocks(a("attn_a_wd1").T),
        "wd2": a("attn_a_wd2").T,
        "wd2_b": blocks(a("attn_a_wd2_b")[:, None])[:, :, 0],
        "wB": blocks(a("attn_a_wB").T),
        "wC": blocks(a("attn_a_wC").T),
        "A_log": blocks(a("attn_a_A_log")),
        "W_D": blocks(a("attn_a_W_D")[:, None])[:, :, 0],
        "out_w": blocks(a("attn_a_out_w").T),
        "Wq": blocks(a("attn_b_Wq")),
        "Wkv": blocks(np.concatenate([a("attn_b_Wk"), a("attn_b_Wv")], axis=1)),
        "Wu": blocks(a("attn_b_Wu")),
        "Wo": blocks(a("attn_b_Wo")),
        "W_q": blocks(a("ffn_W_q")),
        "keys": a("ffn_keys").transpose(1, 0, 2),
        "gate_w": blocks(a("ffn_gate_w")),
        "up_w": blocks(a("ffn_up_w")),
        "down_embed": blocks(a("ffn_down_embed").T),
        "lower_w": blocks(np.concatenate([a("ffn_down_w"), a("ffn_up_embed")], axis=0)),
    }
    nc = bacc.Bacc("TRN2", target_bir_lowering=False, num_devices=1)
    arrays, dram = {}, {}
    for name, w in laid.items():
        arrays["in_" + name] = np.ascontiguousarray(w)
        dram[name] = nc.dram_tensor("in_" + name, w.shape, FP32, kind="ExternalInput").ap()
    out = nc.dram_tensor("out", (BATCH, SEQ, D), FP32, kind="ExternalOutput").ap()
    program(nc, dram, out)
    r = run_bass_kernel_spmd(nc, [arrays], core_ids=[0])
    return r.results[0]["out"]
```

```python
from contextlib import ExitStack

import numpy as np

import concourse.bass as bass
from concourse import mybir

FP32 = mybir.dt.float32
BF16 = mybir.dt.bfloat16
ALU = mybir.AluOpType
ACT = mybir.ActivationFunctionType
AX = mybir.AxisListType

P = 128
BATCH, SEQ, D = 4, 1024, 256
TOKENS = BATCH * SEQ
CHUNK = 512
CHUNKS = TOKENS // CHUNK
TILES = CHUNK // P
KD = D // P
E, N, R, TAPS = 512, 16, 128, 4
KE = E // P
EPS = 1e-5
EXP_LN_SET = "natural_log_exp_and_others"


def need(eng, sem, value):
    if isinstance(value, int) and value <= 0:
        return
    eng.wait_ge(sem, value)


class Chain:

    def __init__(self, eng, sem):
        self.eng, self.sem, self.base, self.k = eng, sem, 0, 0

    def link(self, ins):
        self.k += 1
        ins.then_inc(self.sem, 1)
        self.eng.wait_ge(self.sem, self.base + self.k)

    def enter(self, i, steps):
        self.outer, self.steps = self.base + self.k, steps
        self.base, self.k = self.outer + i * steps, 0

    def leave(self, times):
        assert self.k == self.steps, f"{self.k} links in the loop's body"
        self.base, self.k = self.outer + times * self.steps, 0


def in_time(ap):
    return ap.rearrange("x (b p h) -> x b h p", b=2, h=2)


def mamba(nc, res, dram):
    RING = 4
    ctx = ExitStack()
    with ctx:
        def sb(name, shape, dt=FP32):
            return ctx.enter_context(nc.sbuf_tensor("m_" + name, shape, dt))

        def sem(name):
            return ctx.enter_context(nc.semaphore("m_" + name))

        inw = sb("inw", [P, KD, E])
        skw = sb("skw", [P, KD, E])
        wd1 = sb("wd1", [P, KE, R])
        wd2 = sb("wd2", [P, E])
        wbc = sb("wbc", [P, KE, P])
        outw = sb("outw", [P, KE, D])
        normw = sb("normw", [P, KD])
        convw = sb("convw", [P, KE, TAPS])
        convb = sb("convb", [P, KE])
        wd2b = sb("wd2b", [P, KE])
        wskip = sb("wskip", [P, KE])
        negA = sb("negA", [P, KE, N])
        ident = sb("ident", [P, P])
        pick = sb("pick", [P, 2 * N], BF16)
        mhalf = sb("mhalf", [P, 2, TILES])
        pause = sb("pause", [P, 2])

        stats = sb("stats", [P, TILES, 6])
        mv = sb("mv", [P, TILES, 2])
        sc = sb("sc", [P, 6, TILES])
        rn = sb("rn", [P, TILES, D])
        rawbc = rn[:, 0:2, :].rearrange("p t d -> p (t d)")
        rnT = sb("rnT", [P, KD, CHUNK])
        xin = sb("xin", [P, KE, 3 + 2 * CHUNK])
        work = sb("work", [P, KE, CHUNK])
        rT = sb("rT", [P, CHUNK])
        xs = sb("xs", [P, 2, KE, CHUNK])
        gate = sb("gate", [P, 2, KE, CHUNK])
        delta = sb("delta", [P, 2, KE, CHUNK])
        dx = sb("dx", [P, 2, KE, CHUNK])
        stack = sb("stack", [P, 2, CHUNK], BF16)
        dA = sb("dA", [P, 2, KE, CHUNK])
        U = sb("U", [P, RING, KE, CHUNK])
        Csb = sb("Csb", [P, 2, CHUNK])
        carry = sb("carry", [P, KE, N])

        y = ctx.enter_context(nc.psum_tensor("m_y", [P, KE, CHUNK], FP32))
        psB = ctx.enter_context(nc.psum_tensor("m_psB", [P, CHUNK], FP32))
        psC = ctx.enter_context(nc.psum_tensor("m_psC", [P, CHUNK], FP32))
        job = ctx.enter_context(nc.psum_tensor("m_job", [P, 2, CHUNK], FP32))

        x_first, x_rest = sem("x_first"), sem("x_rest")
        w_in, w_conv, w_d, w_bc, w_out, w_A = (sem(s) for s in ("w_in", "w_conv", "w_d", "w_bc", "w_out", "w_A"))
        const_ready = sem("const_ready")
        stats_ready, norm_ready, rn_ready = sem("stats_ready"), sem("norm_ready"), sem("rn_ready")
        job_full, job_free = sem("job_full"), sem("job_free")
        conv_done, xs_ready, split_done = sem("conv_done"), sem("xs_ready"), sem("split_done")
        zmin_ready, ln_ready, delta_ready = sem("zmin_ready"), sem("ln_ready"), sem("delta_ready")
        B_full, C_full, C_ready = sem("B_full"), sem("C_full"), sem("C_ready")
        dA_ready, mult_done, h_ready = sem("dA_ready"), sem("mult_done"), sem("h_ready")
        dx_ready = sem("dx_ready")
        hc_ready, nsum_done = sem("hc_ready"), sem("nsum_done")
        y_read, gate_done, out_full, out_free = sem("y_read"), sem("gate_done"), sem("out_full"), sem("out_free")
        dve_own, act_own, pool_own = sem("dve_own"), sem("act_own"), sem("pool_own")

        JOBS = 16
        PE_AT = {4: ("turn",), 5: ("in0", "in1"), 6: ("in2", "in3"), 7: ("in4", "in5"), 8: ("in6", "in7"),
                 10: ("low",), 11: ("bc", "dt0"), 12: ("dt1", "dt2"), 13: ("dt3",)}
        ACT_AT = {4: ("turn",), 6: ("in0", "in1"), 7: ("in2", "in3"), 8: ("in4", "in5"), 9: ("in6", "in7", "silu"),
                  10: ("low",), 11: ("bc",), 12: ("dt0", "dt1"), 13: ("dt2", "dt3"), 14: ("softplus",)}
        DVE_AT = {0: ("stats",), 2: ("norm",), 6: ("conv0",), 7: ("conv1", "conv2"), 8: ("conv3",),
                  12: ("split",), 13: ("least",), 14: ("delta",)}
        POOL_AT = {1: ("factors",), 15: ("dx",)}
        HEAD = range(0, 6)
        TAIL = range(6, N)
        GATED, MULTIPLIED, OUT, ADDED = 1, 2, (2, 3), (3, 4)

        def parts(at, n, c, part, q):
            if not (isinstance(c, int) and c == CHUNKS - 1):
                for name in at.get(n, ()):
                    part(name, c + 1, 1 - q)

        def schedule(head, tail, loop, first, steps=None, chain=None):
            first()
            head(0, 0, False)
            with loop(0, BATCH - 1) as b:
                if chain:
                    chain.enter(b, steps)
                tail(2 * b, 0, True)
                head(2 * b + 1, 1, True)
                tail(2 * b + 1, 1, True)
                head(2 * b + 2, 0, True)
                if chain:
                    chain.leave(BATCH - 1)
            tail(CHUNKS - 2, 0, True)
            head(CHUNKS - 1, 1, True)
            tail(CHUNKS - 1, 1, False)

        block = ctx.enter_context(nc.Block())

        @block.sync
        def _(sp):
            x_v = dram["x"].rearrange("b (s p h) d -> p (b s) (h d)", p=P, h=2)
            res_v = res[:, :, :].rearrange("p (s h) d -> p s (h d)", h=2)
            sp.dma_start(res_v[:, 0:2, :], x_v[:, 0:2, :]).then_inc(x_first, 16)
            sp.dma_start(normw[:, :], dram["norm_w"]).then_inc(w_in, 16)
            sp.dma_start(inw[:, :, :], dram["in_w"]).then_inc(w_in, 16)
            sp.dma_start(skw[:, :, :], dram["skip_w"]).then_inc(w_in, 16)
            sp.dma_start(convw[:, :, :], dram["conv_w"]).then_inc(w_conv, 16)
            sp.dma_start(convb[:, :], dram["conv_b"]).then_inc(w_conv, 16)
            sp.dma_start(wd2b[:, :], dram["wd2_b"]).then_inc(w_conv, 16)
            sp.dma_start(wskip[:, :], dram["W_D"]).then_inc(w_conv, 16)
            sp.dma_start(wd1[:, :, :], dram["wd1"]).then_inc(w_d, 16)
            sp.dma_start(wd2[:, :], dram["wd2"]).then_inc(w_d, 16)
            for k in range(4):
                sp.dma_start(wbc[:, :, 32 * k:32 * k + N], dram["wB"]).then_inc(w_bc, 16)
                sp.dma_start(wbc[:, :, 32 * k + N:32 * k + 2 * N], dram["wC"]).then_inc(w_bc, 16)
            sp.dma_start(negA[:, :, :], dram["A_log"]).then_inc(w_A, 16)
            sp.dma_start(res_v[:, 2:, :], x_v[:, 2:, :]).then_inc(x_rest, 16)
            sp.dma_start(outw[:, :, :], dram["out_w"]).then_inc(w_out, 16)

        @block.gpsimd
        def _(pool):
            own = Chain(pool, pool_own)

            def first():
                pool.memset(mhalf[:, :, :], -0.5)
                pool.memset(pick[:, :], 0.0)
                own.link(pool.memset(ident[:, :], 0.0))
                own.link(pool.affine_select(out=ident[:, :], in_=ident[:, :], compare_op=ALU.not_equal, fill=1.0,
                                            base=0, pattern=[[-1, P]], channel_multiplier=1))
                for row in (0, 64, 96):
                    last = pool.affine_select(out=pick[:, :], in_=pick[:, :], compare_op=ALU.not_equal,
                                              fill=1.0, base=-row, pattern=[[-1, 2 * N]], channel_multiplier=1)
                    own.link(last)
                pool.memset(pause[:, 1:2], 0.0).then_inc(const_ready, 1)
                part("factors", 0, 0)
                part("dx", 0, 0)

            def part(name, c, q):
                if name == "factors":
                    pool.wait_ge(stats_ready, c + 1)
                    pool.tensor_tensor(sc[:, 2:4, :], sc[:, 0:2, :], mhalf[:, :, :], ALU.pow).then_inc(norm_ready, 1)
                elif name == "dx":
                    pool.wait_ge(delta_ready, c + 1)
                    pool.tensor_tensor(dx[:, q, :, :], delta[:, q, :, :], xs[:, q, :, :], ALU.mult).then_inc(dx_ready, 1)

            def slots(c, q, which, finish):
                for n in which:
                    if finish and n == MULTIPLIED:
                        pool.wait_ge(y_read, c)
                        pool.tensor_tensor(gate[:, 1 - q, :, :], gate[:, 1 - q, :, :], xs[:, 1 - q, :, :],
                                           ALU.mult).then_inc(gate_done, 1)
                    parts(POOL_AT, n, c, part, q)
                    m = N * c + n
                    pool.wait_ge(h_ready, m + 1)
                    pool.wait_ge(C_ready, m + 1)
                    u = U[:, n % RING, :, :]
                    pool.tensor_tensor(u, u, Csb[:, n % 2, :].unsqueeze(1).to_broadcast([P, KE, CHUNK]),
                                       ALU.mult).then_inc(hc_ready, 1)

            schedule(lambda c, q, more: slots(c, q, HEAD, more), lambda c, q, _: slots(c, q, TAIL, False),
                     pool.Fori, first)
            pool.wait_ge(y_read, CHUNKS)
            pool.tensor_tensor(gate[:, 1, :, :], gate[:, 1, :, :], xs[:, 1, :, :], ALU.mult).then_inc(gate_done, 1)

        @block.tensor
        def _(pe):
            def take(c, i):
                if i >= 2:
                    pe.wait_ge(job_free, JOBS * c + i - 1)
                else:
                    need(pe, out_free, 2 * c - 1 + i)
                return job[:, i % 2, :]

            def mm(out, pairs):
                for k, (w, x) in enumerate(pairs):
                    last = nc.tensor.matmul(out, w, x, start=k == 0, stop=k == len(pairs) - 1)
                return last

            def part(name, c, q):
                if name == "turn":
                    pe.wait_ge(rn_ready, c + 1)
                    for k in range(KD):
                        out = take(c, k)
                        for j in range(TILES):
                            last = nc.tensor.transpose(out[:, j * P:(j + 1) * P], rn[:, j, k * P:(k + 1) * P],
                                                       ident[:, :])
                        last.then_inc(job_full, 1)
                elif name[:2] == "in":
                    g = int(name[2])
                    if g == 0:
                        pe.wait_ge(job_free, JOBS * c + 2)
                    for i in (g,):
                        w = inw if i < KE else skw
                        out = take(c, 2 + i)
                        e = i % KE * P
                        mm(out, [(w[:, k, e:e + P], rnT[:, k, :]) for k in range(KD)]).then_inc(job_full, 1)
                elif name == "low":
                    pe.wait_ge(xs_ready, c + 1)
                    mm(take(c, 10), [(wd1[:, k, :], xs[:, q, k, :]) for k in range(KE)]).then_inc(job_full, 1)
                elif name == "bc":
                    mm(take(c, 11), [(wbc[:, k, :], xs[:, q, k, :]) for k in range(KE)]).then_inc(job_full, 1)
                elif name[:2] == "dt":
                    e = int(name[2])
                    if e == 0:
                        pe.wait_ge(job_free, JOBS * c + 11)
                    if True:
                        mm(take(c, 12 + e), [(wd2[:, e * P:(e + 1) * P], rT[:, :])]).then_inc(job_full, 1)

            def spread(c, n, q):
                m = N * c + n
                if n == 0:
                    pe.wait_ge(split_done, c + 1)
                need(pe, mult_done, m)
                nc.tensor.matmul(psB[:, :], pick[:, n:n + 1].to_broadcast([P, P]), stack[:, q, :], start=True, stop=True).then_inc(B_full, 1)
                need(pe, C_ready, m)
                nc.tensor.matmul(psC[:, :], pick[:, N + n:N + n + 1].to_broadcast([P, P]), stack[:, q, :], start=True,
                                 stop=True).then_inc(C_full, 1)

            def nsum(c, n, q):
                m = N * c + n
                pe.wait_ge(hc_ready, m + 1)
                if n == 0:
                    need(pe, y_read, c)
                for e in range(KE):
                    last = nc.tensor.matmul(y[:, e, :], ident[:, :], U[:, n % RING, e, :], start=n == 0,
                                            stop=n == N - 1)
                last.then_inc(nsum_done, 1)

            def output(c, q, which):
                pe.wait_ge(gate_done, c + 1)
                for i in which:
                    if isinstance(c, int) and c == CHUNKS - 1:
                        pe.wait_ge(out_free, 2 * c + 1 + i)
                    else:
                        pe.wait_ge(job_free, JOBS * (c + 1) + JOBS - 1 + i)
                    for h in range(2):
                        for k in range(KE):
                            last = nc.tensor.matmul(job[:, i, h * D:(h + 1) * D],
                                                    in_time(gate[:, q, k, :])[:, i, h, :], outw[:, k, :],
                                                    start=k == 0, stop=k == KE - 1)
                    last.then_inc(out_full, 1)

            def slots(c, q, which, finish, last=False):
                for n in which:
                    if n < N - 1:
                        spread(c, n + 1, q)
                    elif not last:
                        spread(c + 1, 0, 1 - q)
                    parts(PE_AT, n, c, part, q)
                    if n > 0:
                        nsum(c, n - 1, q)
                    elif finish:
                        nsum(c - 1, N - 1, 1 - q)
                    if finish and n in OUT:
                        output(c - 1, 1 - q, (OUT.index(n),))

            def head(c, q, more):
                slots(c, q, HEAD, more)

            def tail(c, q, more):
                slots(c, q, TAIL, False, not more)

            def first():
                pe.wait_ge(const_ready, 1)
                pe.wait_ge(w_in, 48)
                part("turn", 0, 0)
                for i in range(8):
                    part(f"in{i}", 0, 0)
                pe.wait_ge(w_d, 32)
                pe.wait_ge(w_bc, 128)
                part("low", 0, 0)
                part("bc", 0, 0)
                for e in range(KE):
                    part(f"dt{e}", 0, 0)
                spread(0, 0, 0)
                pe.wait_ge(w_out, 16)

            schedule(head, tail, pe.Fori, first)
            nsum(CHUNKS - 1, N - 1, 1)
            output(CHUNKS - 1, 1, range(2))

        @block.scalar
        def _(act):
            own = Chain(act, act_own)

            def part(name, c, q):
                def full(i):
                    act.wait_ge(job_full, JOBS * c + i + 1)

                if name == "turn":
                    for k in range(KD):
                        full(k)
                        nc.scalar.activation(in_time(rnT[:, k, :]),
                                             job[:, k, :].rearrange("x (b h p) -> x b h p", b=2, h=2), ACT.Copy,
                                             scale=normw[:, k:k + 1]).then_inc(job_free, 1)
                elif name[:2] == "in":
                    for i in (int(name[2]),):
                        full(2 + i)
                        ps = job[:, i % 2, :]
                        if i < KE:
                            nc.scalar.activation(xin[:, i, 3 + CHUNK * q:3 + CHUNK * (q + 1)], ps, ACT.Copy)
                            nc.scalar.activation(work[:, i, :], ps, ACT.Identity, bias=convb[:, i:i + 1],
                                                 scale=convw[:, i, TAPS - 1:TAPS]).then_inc(job_free, 1)
                        else:
                            own_gate = nc.scalar.activation(gate[:, q, i - KE, :], ps, ACT.Copy)
                            own_gate.then_inc(job_free, 1)
                elif name == "silu":
                    act.wait_ge(conv_done, c + 1)
                    act.wait_ge(job_free, JOBS * c + 10)
                    nc.scalar.activation(xs[:, q, :, :], work[:, :, :], ACT.Silu).then_inc(xs_ready, 1)
                    nc.scalar.activation(gate[:, q, :, :], gate[:, q, :, :], ACT.Silu)
                    nc.scalar.preload_act_table_set(EXP_LN_SET)
                elif name == "low":
                    full(10)
                    nc.scalar.activation(rT[:, :], job[:, 0, :], ACT.Copy).then_inc(job_free, 1)
                elif name == "bc":
                    full(11)
                    nc.scalar.activation(rawbc, job[:, 1, :], ACT.Copy).then_inc(job_free, 1)
                elif name[:2] == "dt":
                    for e in (int(name[2]),):
                        full(12 + e)
                        nc.scalar.activation(delta[:, q, e, :], job[:, e % 2, :], ACT.Identity,
                                             bias=wd2b[:, e:e + 1]).then_inc(job_free, 1)
                elif name == "softplus":
                    act.wait_ge(zmin_ready, c + 1)
                    own.link(nc.scalar.activation(work[:, :, :], work[:, :, :], ACT.Exp))
                    nc.scalar.activation(work[:, :, :], work[:, :, :], ACT.Ln, bias=1.0).then_inc(ln_ready, 1)

            def slots(c, q, which):
                for n in which:
                    m = N * c + n
                    if n == 0:
                        act.wait_ge(delta_ready, c + 1)
                    need(act, h_ready, m - 1)
                    for e in range(KE):
                        last = nc.scalar.activation(dA[:, n % 2, e, :], delta[:, q, e, :], ACT.Exp,
                                                    scale=negA[:, e, n:n + 1])
                    last.then_inc(dA_ready, 1)
                    act.wait_ge(C_full, m + 1)
                    need(act, hc_ready, m - 1)
                    nc.scalar.activation(Csb[:, n % 2, :], psC[:, :], ACT.Copy).then_inc(C_ready, 1)
                    parts(ACT_AT, n, c, part, q)

            def first():
                act.wait_ge(w_A, 16)
                own.link(nc.scalar.activation(negA[:, :, :], negA[:, :, :], ACT.Exp))
                own.link(nc.scalar.activation(negA[:, :, :], negA[:, :, :], ACT.Copy, scale=-1.0))
                act.wait_ge(w_in, 48)
                act.wait_ge(w_conv, 64)
                for name in [n for names in ACT_AT.values() for n in names]:
                    part(name, 0, 0)

            schedule(lambda c, q, _: slots(c, q, HEAD), lambda c, q, _: slots(c, q, TAIL), act.Fori, first, 2, own)

        @block.vector
        def _(dve):
            own = Chain(dve, dve_own)

            def part(name, c, q):
                if name == "stats":
                    for j in range(TILES):
                        last = nc.vector.bn_stats(stats[:, j, :], res[:, TILES * c + j, :])
                    own.link(last)
                    nc.vector.memset(pause[:, 0:1], 0.0)
                    for j in range(TILES):
                        last = nc.vector.bn_aggr(mv[:, j, :], stats[:, j, :])
                    own.link(last)
                    nc.vector.tensor_scalar(sc[:, 0, :], mv[:, :, 1], EPS, None, ALU.add)
                    nc.vector.tensor_scalar(sc[:, 1, :], mv[:, :, 1], 1.0 + EPS, EPS * EPS, ALU.mult,
                                            ALU.add).then_inc(stats_ready, 1)
                elif name == "norm":
                    dve.wait_ge(norm_ready, c + 1)
                    nc.vector.tensor_scalar(sc[:, 4, :], sc[:, 2, :], 1.0, None, ALU.add)
                    own.link(nc.vector.tensor_tensor(sc[:, 5, :], mv[:, :, 0], sc[:, 2, :], ALU.mult))
                    need(dve, job_full, JOBS * (c - 1) + 2)
                    for j in range(TILES):
                        last = nc.vector.tensor_scalar(rn[:, j, :], res[:, TILES * c + j, :], mv[:, j, 0:1],
                                                       sc[:, 3, j:j + 1], ALU.subtract, ALU.mult)
                    last.then_inc(rn_ready, 1)
                    for j in range(TILES):
                        x = res[:, TILES * c + j, :]
                        nc.vector.tensor_scalar(x, x, sc[:, 4, j:j + 1], sc[:, 5, j:j + 1], ALU.mult, ALU.subtract)
                elif name[:4] == "conv":
                    for e in (int(name[4]),):
                        dve.wait_ge(job_free, JOBS * c + 3 + e)
                        for k in range(TAPS - 1):
                            at = CHUNK * q + k
                            last = nc.vector.scalar_tensor_tensor(work[:, e, :], xin[:, e, at:at + CHUNK],
                                                                  convw[:, e, k:k + 1], work[:, e, :],
                                                                  ALU.mult, ALU.add)
                            if k < TAPS - 2:
                                own.link(last)
                    if name == "conv3":
                        last.then_inc(conv_done, 1)
                elif name == "split":
                    dve.wait_ge(job_free, JOBS * c + 12)
                    own.link(nc.vector.tensor_copy(stack[:, q, :], rawbc))
                    for p in (64, 96):
                        own.link(nc.vector.tensor_tensor(rawbc[p:, :], rawbc[p:, :], stack[p:, q, :], ALU.subtract))
                        last = nc.vector.tensor_copy(stack[p:, q, :], rawbc[p:, :])
                        if p == 64:
                            own.link(last)
                    last.then_inc(split_done, 1)
                elif name == "least":
                    dve.wait_ge(job_free, JOBS * c + 16)
                    nc.vector.tensor_scalar(work[:, :, :], delta[:, q, :, :], 40.0, None,
                                            ALU.min).then_inc(zmin_ready, 1)
                elif name == "delta":
                    dve.wait_ge(ln_ready, c + 1)
                    nc.vector.tensor_tensor(delta[:, q, :, :], delta[:, q, :, :], work[:, :, :],
                                            ALU.max).then_inc(delta_ready, 1)

            def unit(c, n, q):
                m = N * c + n
                u = U[:, n % RING, :, :]
                dve.wait_ge(B_full, m + 1)
                if n == 0:
                    dve.wait_ge(dx_ready, c + 1)
                need(dve, nsum_done, m - RING + 1)
                nc.vector.tensor_tensor(u, dx[:, q, :, :], psB[:, :].unsqueeze(1).to_broadcast([P, KE, CHUNK]),
                                        ALU.mult).then_inc(mult_done, 1)
                dve.wait_ge(mult_done, m + 1)
                dve.wait_ge(dA_ready, m + 1)
                for e in range(KE):
                    start = carry[:, e, n:n + 1] if q else 0.0
                    last = nc.vector.tensor_tensor_scan(u[:, e, :], dA[:, n % 2, e, :], u[:, e, :], start,
                                                        ALU.mult, ALU.add)
                if q == 0:
                    own.link(last)
                    last = nc.vector.tensor_copy(carry[:, :, n], u[:, :, CHUNK - 1])
                last.then_inc(h_ready, 1)

            def gated(c, q):
                dve.wait_ge(nsum_done, N * c + N)
                for e in range(KE):
                    x = xs[:, q, e, :]
                    last = nc.vector.scalar_tensor_tensor(x, x, wskip[:, e:e + 1], y[:, e, :], ALU.mult, ALU.add)
                last.then_inc(y_read, 1)

            def add_output(c, which):
                for i in which:
                    dve.wait_ge(out_full, 2 * c + 1 + i)
                    x = res[:, :, :].rearrange("p (s h) d -> p s (h d)", h=2)[:, 2 * c + i, :]
                    nc.vector.tensor_tensor(x, x, job[:, i, :], ALU.add).then_inc(out_free, 1)

            def head(c, q, more):
                for n in HEAD:
                    unit(c, n, q)
                    parts(DVE_AT, n, c, part, q)
                    if more and n == GATED:
                        gated(c - 1, 1 - q)
                    if more and n in ADDED:
                        add_output(c - 1, (ADDED.index(n),))

            def tail(c, q, more):
                for n in TAIL:
                    unit(c, n, q)
                    parts(DVE_AT, n, c, part, q)

            def first():
                nc.vector.memset(stats[:, :, :], 0.0).then_inc(out_free, 2)
                own.link(nc.vector.memset(xin[:, :, 0:3], 0.0))
                dve.wait_ge(x_first, 16)
                dve.wait_ge(w_conv, 64)
                for names in DVE_AT.values():
                    for name in names:
                        part(name, 0, 0)
                dve.wait_ge(x_rest, 16)

            schedule(head, tail, dve.Fori, first, 46, own)
            gated(CHUNKS - 1, 1)
            add_output(CHUNKS - 1, range(2))


HIDDEN, KEYS, EXPERTS, TOP = 1024, 64, 512, 8
KM = (HIDDEN + EXPERTS) // P
KH = HIDDEN // P
ROWS = TOP * KEYS
assert ROWS == EXPERTS
UPPER = 2 * HIDDEN + EXPERTS
WEIGHTS = KD * UPPER + KM * D
PIECES = 4
FP32R = mybir.dt.float32r


def ffn(nc, res, dram, name):
    ctx = ExitStack()
    with ctx:
        def sb(what, shape, dt=FP32):
            return ctx.enter_context(nc.sbuf_tensor(f"{name}_{what}", shape, dt))

        keyz = sb("keyz", [P, 2, 2, KEYS])
        weights = [sb(f"weights_{part}", [P, PIECES, WEIGHTS // PIECES], FP32R) for part in ("hi", "lo")]
        z = [sb("z_hi", [P, KD, CHUNK], FP32R), sb("z_lo", [P, KD, CHUNK], FP32R)]
        ident = sb("ident", [P, P])
        mv = sb("mv", [P, CHUNKS, TILES, 2])
        s1 = sb("s1", [P, CHUNKS, TILES])
        QT = sb("QT", [P, CHUNKS, CHUNK])
        ffn_queries(nc, res, dram, name + "q", keyz, weights, z, ident, mv, s1, QT)
        ffn_layers(nc, res, name + "l", keyz, weights, z, ident, mv, s1, QT)


def ffn_queries(nc, res, dram, name, keyz, weights, z, ident, mv, s1, QT):
    ctx = ExitStack()
    with ctx:
        def sb(what, shape, dt=FP32):
            return ctx.enter_context(nc.sbuf_tensor(f"{name}_{what}", shape, dt))

        def sem(what):
            return ctx.enter_context(nc.semaphore(f"{name}_{what}"))

        def ps(what, shape):
            return ctx.enter_context(nc.psum_tensor(f"{name}_{what}", shape, FP32))

        wq = sb("wq", [P, KD, P])
        whole = sb("whole", [P, PIECES, WEIGHTS // PIECES])
        mhalf = sb("mhalf", [P, TILES])
        pause = sb("pause", [P, 1])
        stats = sb("stats", [P, TILES, 6])
        mv4 = sb("mv4", [P, TILES, 2])
        var = sb("var", [P, 2, TILES])
        inv = sb("inv", [P, 2, TILES])
        zn = sb("zn", [P, 2, TILES, D])
        zT = sb("zT", [P, 2, KD, CHUNK])
        psT, psQ = ps("psT", [P, 2, KD, CHUNK]), ps("psQ", [P, 2, CHUNK])

        w_q, w_keys, w_piece = sem("w_q"), sem("w_keys"), [sem(f"w_piece{i}") for i in range(PIECES)]
        const_ready, keyz_clear = sem("const_ready"), sem("keyz_clear")
        var_ready, inv_ready, zn_ready = sem("var_ready"), sem("inv_ready"), sem("zn_ready")
        turn_full, zT_ready, q_full, QT_ready = sem("turn_full"), sem("zT_ready"), sem("q_full"), sem("QT_ready")
        hi_ready, z_high, z_low = sem("hi_ready"), sem("z_high"), sem("z_low")
        dve_own, pool_own = sem("dve_own"), sem("pool_own")

        block = ctx.enter_context(nc.Block())

        @block.sync
        def _(sp):
            sp.dma_start(wq[:, :, :], dram["W_q"]).then_inc(w_q, 16)
            for i in range(PIECES):
                sp.dma_start(whole[:, i, :], dram["ffn_w"][:, i, :]).then_inc(w_piece[i], 16)
            sp.wait_ge(keyz_clear, 1)
            sp.dma_start(keyz[0:64, :, 0, :], dram["keys"]).then_inc(w_keys, 16)
            sp.dma_start(keyz[64:128, :, 1, :], dram["keys"]).then_inc(w_keys, 16)
            sp.wait_ge(w_keys, 32)

        @block.gpsimd
        def _(pool):
            own = Chain(pool, pool_own)
            pool.memset(mhalf[:, :], -0.5)
            own.link(pool.memset(ident[:, :], 0.0))
            pool.affine_select(out=ident[:, :], in_=ident[:, :], compare_op=ALU.not_equal, fill=1.0, base=0,
                               pattern=[[-1, P]], channel_multiplier=1).then_inc(const_ready, 1)
            pool.memset(keyz[:, :, :, :], 0.0).then_inc(keyz_clear, 1)

            def root(c, q):
                pool.wait_ge(var_ready, c + 1)
                pool.tensor_tensor(inv[:, q, :], var[:, q, :], mhalf[:, :], ALU.pow).then_inc(inv_ready, 1)

            with pool.Fori(0, CHUNKS // 2) as b:
                root(2 * b, 0)
                root(2 * b + 1, 1)

        @block.tensor
        def _(pe):
            pe.wait_ge(const_ready, 1)

            def turn(c, q):
                pe.wait_ge(zn_ready, c + 1)
                for k in range(KD):
                    for j in range(TILES):
                        last = nc.tensor.transpose(psT[:, q, k, j * P:(j + 1) * P], zn[:, q, j, k * P:(k + 1) * P],
                                                   ident[:, :])
                last.then_inc(turn_full, 1)

            def queries(c, q):
                pe.wait_ge(zT_ready, c + 1)
                for k in range(KD):
                    last = nc.tensor.matmul(psQ[:, q, :], wq[:, k, :], zT[:, q, k, :], start=k == 0, stop=k == KD - 1)
                last.then_inc(q_full, 1)

            turn(0, 0)
            pe.wait_ge(w_q, 16)
            with pe.Fori(0, CHUNKS // 2 - 1) as b:
                turn(2 * b + 1, 1)
                queries(2 * b, 0)
                pe.wait_ge(z_low, 1)
                turn(2 * b + 2, 0)
                queries(2 * b + 1, 1)
            turn(CHUNKS - 1, 1)
            queries(CHUNKS - 2, 0)
            queries(CHUNKS - 1, 1)

        @block.scalar
        def _(act):
            def fetch(c, q):
                act.wait_ge(turn_full, c + 1)
                nc.scalar.activation(zT[:, q, :, :], psT[:, q, :, :], ACT.Copy).then_inc(zT_ready, 1)

            def keep_queries(c, q):
                act.wait_ge(q_full, c + 1)
                nc.scalar.activation(in_time(QT[:, c, :]), psQ[:, q, :].rearrange("x (b h p) -> x b h p", b=2, h=2),
                                     ACT.Copy).then_inc(QT_ready, 1)

            def high(i):
                nc.scalar.activation(weights[0][:, i, :], whole[:, i, :], ACT.Copy).then_inc(hi_ready, 1)

            fetch(0, 0)
            nc.scalar.activation(z[0][:, :, :], psT[:, 0, :, :], ACT.Copy).then_inc(z_high, 1)
            with act.Fori(0, CHUNKS // 2 - 1) as b:
                fetch(2 * b + 1, 1)
                keep_queries(2 * b, 0)
                fetch(2 * b + 2, 0)
                keep_queries(2 * b + 1, 1)
            fetch(CHUNKS - 1, 1)
            for i in range(PIECES):
                act.wait_ge(w_piece[i], 16)
                high(i)
                if i == 0:
                    keep_queries(CHUNKS - 2, 0)
                if i == 1:
                    keep_queries(CHUNKS - 1, 1)

        @block.vector
        def _(dve):
            own = Chain(dve, dve_own)

            def statistics(c, q):
                for j in range(TILES):
                    last = nc.vector.bn_stats(stats[:, j, :], res[:, TILES * c + j, :])
                own.link(last)
                nc.vector.memset(pause[:, 0:1], 0.0)
                for j in range(TILES):
                    last = nc.vector.bn_aggr(mv4[:, j, :], stats[:, j, :])
                own.link(last)
                nc.vector.tensor_copy(mv[:, c, :, :], mv4[:, :, :])
                own.link(nc.vector.tensor_scalar(var[:, q, :], mv4[:, :, 1], EPS, None, ALU.add))
                nc.vector.memset(pause[:, 0:1], 0.0).then_inc(var_ready, 1)

            def normalise(c, q):
                dve.wait_ge(inv_ready, c + 1)
                own.link(nc.vector.tensor_copy(s1[:, c, :], inv[:, q, :]))
                if not (isinstance(c, int) and c < 2):
                    dve.wait_ge(turn_full, c - 1)
                for j in range(TILES):
                    last = nc.vector.tensor_scalar(zn[:, q, j, :], res[:, TILES * c + j, :], mv[:, c, j, 0:1],
                                                   s1[:, c, j:j + 1], ALU.subtract, ALU.mult)
                last.then_inc(zn_ready, 1)

            statistics(0, 0)
            statistics(1, 1)
            normalise(0, 0)
            normalise(1, 1)
            dve.wait_ge(z_high, 1)
            nc.vector.tensor_tensor(z[1][:, :, :], psT[:, 0, :, :], z[0][:, :, :].bitcast(FP32),
                                    ALU.subtract).then_inc(z_low, 1)
            with dve.Fori(1, CHUNKS // 2) as b:
                own.enter(b - 1, 8)
                statistics(2 * b, 0)
                statistics(2 * b + 1, 1)
                normalise(2 * b, 0)
                normalise(2 * b + 1, 1)
                own.leave(CHUNKS // 2 - 1)
            for i in range(PIECES):
                dve.wait_ge(hi_ready, i + 1)
                nc.vector.tensor_tensor(weights[1][:, i, :], whole[:, i, :], weights[0][:, i, :].bitcast(FP32),
                                        ALU.subtract)


def ffn_layers(nc, res, name, keyz, weights, z, ident, mv, s1, QT):
    ctx = ExitStack()
    with ctx:
        def sb(what, shape, dt=FP32):
            return ctx.enter_context(nc.sbuf_tensor(f"{name}_{what}", shape, dt))

        def sem(what):
            return ctx.enter_context(nc.semaphore(f"{name}_{what}"))

        def ps(what, shape):
            return ctx.enter_context(nc.psum_tensor(f"{name}_{what}", shape, FP32))

        pause = sb("pause", [P, 5])
        zn = sb("zn", [P, TILES, D])
        qs = sb("qs", [P, 2, CHUNK // 2])
        Rt = sb("Rt", [P, 2, 2, 2, KEYS])
        top1 = sb("top1", [P, TILES, 2, TOP])
        sums = sb("sums", [P, TILES, TOP, TOP])
        top2 = sb("top2", [P, TILES, TOP])
        ex = sb("ex", [P, TILES, TOP + KEYS + TOP])
        total = sb("total", [P, TILES])
        S = sb("S", [P, TILES, TOP, KEYS])
        W = sb("W", [P, TILES, TOP, KEYS])
        csum = sb("csum", [P, TILES])
        sil = sb("sil", [P, 2, CHUNK])
        prod = sb("prod", [P, 2, CHUNK])
        H = [sb("H_hi", [P, KM, CHUNK], FP32R), sb("H_lo", [P, KM, CHUNK], FP32R)]

        psG, psU, psX, psO = (ps(s, [P, 2, CHUNK]) for s in ("psG", "psU", "psX", "psO"))

        zn_ready, turn_full, zhi_ready, z_ready = sem("zn_ready"), sem("turn_full"), sem("zhi_ready"), sem("z_ready")
        qs_ready, route_full, Rt_ready = sem("qs_ready"), sem("route_full"), sem("Rt_ready")
        dif_ready, exp_ready, ex_ready, SW_ready, C_ready = (sem(s) for s in ("dif_ready", "exp_ready", "ex_ready",
                                                                              "SW_ready", "C_ready"))
        g_full, g_free, u_full, u_free = sem("g_full"), sem("g_free"), sem("u_full"), sem("u_free")
        hi_ready, lo_ready = sem("hi_ready"), sem("lo_ready")
        out_full, out_free = sem("out_full"), sem("out_free")
        dve_own = sem("dve_own")
        SPREAD = [P, TILES, TOP, KEYS]

        def tile(t):
            return Rt[:, :, t, :, :]

        block = ctx.enter_context(nc.Block())

        @block.gpsimd
        def _(pool):
            with pool.Fori(0, CHUNKS) as c:
                pool.wait_ge(Rt_ready, c + 1)
                for b in range(2):
                    pool.tensor_tensor(S[:, 2 * b:2 * b + 2, :, :],
                                       Rt[:, b, 0, :, 0:TOP].unsqueeze(3).to_broadcast([P, 2, TOP, KEYS]),
                                       Rt[:, b, 1, :, :].unsqueeze(2).to_broadcast([P, 2, TOP, KEYS]), ALU.add)
                pool.wait_ge(ex_ready, c + 1)
                pool.tensor_tensor(W[:, :, :, :], ex[:, :, 0:TOP].unsqueeze(3).to_broadcast(SPREAD),
                                   ex[:, :, TOP:TOP + KEYS].unsqueeze(2).to_broadcast(SPREAD),
                                   ALU.mult).then_inc(SW_ready, 1)

        @block.tensor
        def _(pe):
            C = W[:, :, :, :].rearrange("p j a b -> p j (a b)")
            flat = [w[:, :, :].rearrange("p i w -> p (i w)") for w in weights]
            upper = [w[:, 0:KD * UPPER].rearrange("p (k w) -> p k w", k=KD) for w in flat]
            lower = [w[:, KD * UPPER:].rearrange("p (k w) -> p k w", k=KM) for w in flat]

            def split_mm(out, w, x, blocks):
                terms = [(w[i][at], x[j][to]) for at, to in blocks for i, j in ((0, 0), (0, 1), (1, 0))]
                for n, (a, b) in enumerate(terms):
                    last = nc.tensor.matmul(out, a, b, start=n == 0, stop=n == len(terms) - 1)
                return last

            def turn(c):
                pe.wait_ge(zn_ready, c)
                for k in range(KD):
                    for j in range(TILES):
                        last = nc.tensor.transpose(psX[:, k, j * P:(j + 1) * P], zn[:, j, k * P:(k + 1) * P],
                                                   ident[:, :])
                last.then_inc(turn_full, 1)

            def hidden(c, i):
                def column(at):
                    return [((slice(None), k, slice(at * P, (at + 1) * P)), (slice(None), k, slice(None)))
                            for k in range(KD)]

                pe.wait_ge(g_free, KM * c + i + 1)
                split_mm(psG[:, i % 2, :], upper, z, column(i if i < KH else KH + i)).then_inc(g_full, 1)
                pe.wait_ge(u_free, KM * c + i + 1)
                if i < KH:
                    last = split_mm(psU[:, i % 2, :], upper, z, column(KH + i))
                else:
                    if i == KH:
                        pe.wait_ge(C_ready, c + 1)
                    for j in range(TILES):
                        e = i - KH
                        last = nc.tensor.transpose(psU[:, i % 2, j * P:(j + 1) * P], C[:, j, e * P:(e + 1) * P],
                                                   ident[:, :])
                last.then_inc(u_full, 1)

            def chunk(c, more):
                pe.wait_ge(z_ready, c + 1)
                for i in range(KM):
                    hidden(c, i)
                    if i == 0:
                        pe.wait_ge(qs_ready, c + 1)
                        for b in range(2):
                            for t in range(2):
                                last = nc.tensor.matmul(psX[:, 0, (2 * b + t) * P:(2 * b + t + 1) * P],
                                                        qs[:, t, b * P:(b + 1) * P],
                                                        keyz[:, t, :, :].rearrange("p h k -> p (h k)"),
                                                        start=True, stop=True)
                        last.then_inc(route_full, 1)
                for i in range(2):
                    pe.wait_ge(out_free, 2 * c + i + 1)
                    for h in range(2):
                        j = 2 * i + h
                        terms = [(k, a, b) for k in range(KM) for a, b in ((0, 0), (0, 1), (1, 0))]
                        for n, (k, a, b) in enumerate(terms):
                            if j == 0 and n % 3 == 0 and (k == 0 or k >= KH):
                                pe.wait_ge(lo_ready, KM * c + max(k + 1, KH) + 2)
                            last = nc.tensor.matmul(psO[:, i, h * D:(h + 1) * D], H[a][:, k, j * P:(j + 1) * P],
                                                    lower[b][:, k, :], start=n == 0, stop=n == len(terms) - 1)
                    last.then_inc(out_full, 1)
                    if i == 0 and more:
                        turn(c + 1)

            with pe.Fori(0, CHUNKS - 1) as c:
                chunk(c, True)
            chunk(CHUNKS - 1, False)

        @block.scalar
        def _(act):
            pairs = QT[:, :, :].rearrange("x (t s) (u w) -> x t (s u) w", t=2, u=2)

            def prepare(c):
                nc.scalar.activation(qs[:, :, :], pairs[:, :, c, :], ACT.Copy).then_inc(qs_ready, 1)
                if isinstance(c, int) and c == 0:
                    return
                act.wait_ge(turn_full, c)
                nc.scalar.activation(z[0][:, :, :], psX[:, :, :], ACT.Copy).then_inc(zhi_ready, 1)

            def high(c, i):
                act.wait_ge(u_free, KM * c + i + 3)
                nc.scalar.activation(H[0][:, i, :], prod[:, i % 2, :], ACT.Copy).then_inc(hi_ready, 1)

            def chunk(c, more):
                for i in range(KM):
                    act.wait_ge(g_full, KM * c + i + 1)
                    act.wait_ge(u_free, KM * c + i + 1)
                    nc.scalar.activation(sil[:, i % 2, :], psG[:, i % 2, :], ACT.Silu).then_inc(g_free, 1)
                    if i > 0:
                        high(c, i - 1)
                    if i == 0:
                        act.wait_ge(route_full, c + 1)
                        nc.scalar.activation(Rt[:, :, :, :, :].rearrange("p b t h k -> p (b t h k)"), psX[:, 0, :],
                                             ACT.Copy).then_inc(Rt_ready, 1)
                    if i == 3:
                        act.wait_ge(dif_ready, c + 1)
                        nc.scalar.activation(ex[:, :, :], ex[:, :, :], ACT.Exp).then_inc(exp_ready, 1)
                high(c, KM - 1)
                if more:
                    prepare(c + 1)

            prepare(0)
            with act.Fori(0, CHUNKS - 1) as c:
                chunk(c, True)
            chunk(CHUNKS - 1, False)

        @block.vector
        def _(dve):
            own = Chain(dve, dve_own)
            nc.vector.memset(pause[:, 1:2], 0.0).then_inc(g_free, 2)
            nc.vector.memset(pause[:, 2:3], 0.0).then_inc(u_free, 2)
            nc.vector.memset(pause[:, 3:4], 0.0).then_inc(out_free, 2)
            nc.vector.memset(pause[:, 4:5], 0.0).then_inc(lo_ready, 2)
            nc.vector.memset(pause[:, 0:1], 0.0).then_inc(z_ready, 1)

            def normalise(c):
                for j in range(TILES):
                    last = nc.vector.tensor_scalar(zn[:, j, :], res[:, TILES * c + j, :], mv[:, c, j, 0:1],
                                                   s1[:, c, j:j + 1], ALU.subtract, ALU.mult)
                last.then_inc(zn_ready, 1)

            def low_z(c):
                dve.wait_ge(zhi_ready, c)
                nc.vector.tensor_tensor(z[1][:, :, :], psX[:, :, :], z[0][:, :, :].bitcast(FP32),
                                        ALU.subtract).then_inc(z_ready, 1)

            def highest(c):
                dve.wait_ge(Rt_ready, c + 1)
                nc.vector.memset(pause[:, 0:1], 0.0)
                for j in range(TILES):
                    for t in range(2):
                        last = nc.vector.max(top1[:, j, t, :], tile(t)[:, j // 2, j % 2, :])
                own.link(last)
                four = [P, TILES, TOP, TOP]
                own.link(nc.vector.tensor_tensor(sums[:, :, :, :], top1[:, :, 0, :].unsqueeze(3).to_broadcast(four),
                                                 top1[:, :, 1, :].unsqueeze(2).to_broadcast(four), ALU.add))
                nc.vector.memset(pause[:, 0:1], 0.0)
                for j in range(TILES):
                    last = nc.vector.max(top2[:, j, :], sums[:, j, :, :].rearrange("p a b -> p (a b)"))
                own.link(last)
                for t, (at, n) in enumerate(((0, TOP), (TOP, KEYS))):
                    part = ex[:, :, at:at + n].rearrange("p (b h) k -> p b h k", b=2)
                    greatest = top1[:, :, t, 0:1].rearrange("p (b h) k -> p b h k", b=2).to_broadcast([P, 2, 2, n])
                    nc.vector.tensor_tensor(part, tile(t)[:, :, :, 0:n], greatest, ALU.subtract)
                nc.vector.tensor_tensor(ex[:, :, TOP + KEYS:], top2[:, :, :],
                                        top2[:, :, 0:1].to_broadcast([P, TILES, TOP]),
                                        ALU.subtract).then_inc(dif_ready, 1)

            def normalise_softmax(c):
                dve.wait_ge(exp_ready, c + 1)
                own.link(nc.vector.reduce_sum(total[:, :], ex[:, :, TOP + KEYS:], AX.X))
                own.link(nc.vector.reciprocal(total[:, :], total[:, :]))
                nc.vector.tensor_tensor(ex[:, :, 0:TOP], ex[:, :, 0:TOP],
                                        total[:, :].unsqueeze(2).to_broadcast([P, TILES, TOP]),
                                        ALU.mult).then_inc(ex_ready, 1)

            def coefficients(c):
                dve.wait_ge(SW_ready, c + 1)
                for j in range(TILES):
                    last = nc.vector.scalar_tensor_tensor(W[:, j, :, :].rearrange("p a b -> p (a b)"), S[:, j, :, :].rearrange("p a b -> p (a b)"),
                                                          top2[:, j, TOP - 1:TOP],
                                                          W[:, j, :, :].rearrange("p a b -> p (a b)"),
                                                          ALU.is_ge, ALU.mult, accum_out=csum[:, j:j + 1])
                own.link(last)
                edge = W[:, :, TOP - 1, KEYS - 1]
                own.link(nc.vector.tensor_tensor(edge, edge, csum[:, :], ALU.subtract))
                nc.vector.tensor_scalar(edge, edge, 1.0, None, ALU.add).then_inc(C_ready, 1)

            def product(c, i):
                dve.wait_ge(g_free, KM * c + i + 3)
                dve.wait_ge(u_full, KM * c + i + 1)
                dve.wait_ge(lo_ready, KM * c + i + 1)
                nc.vector.tensor_tensor(prod[:, i % 2, :], psU[:, i % 2, :], sil[:, i % 2, :],
                                        ALU.mult).then_inc(u_free, 1)

            def low(c, i):
                dve.wait_ge(hi_ready, KM * c + i + 1)
                nc.vector.tensor_tensor(H[1][:, i, :], prod[:, i % 2, :], H[0][:, i, :].bitcast(FP32),
                                        ALU.subtract).then_inc(lo_ready, 1)

            def chunk(c, more):
                for i in range(KM):
                    product(c, i)
                    if i > 0:
                        low(c, i - 1)
                    if i == 0:
                        highest(c)
                    if i == 3:
                        normalise_softmax(c)
                    if i == KH - 2:
                        coefficients(c)
                    if i == KH + 1 and more:
                        normalise(c + 1)
                low(c, KM - 1)
                for i in range(2):
                    dve.wait_ge(out_full, 2 * c + i + 1)
                    x = res[:, :, :].rearrange("p (s h) d -> p s (h d)", h=2)[:, 2 * c + i, :]
                    nc.vector.tensor_tensor(x, x, psO[:, i, :], ALU.add).then_inc(out_free, 1)
                    if i == 0 and more:
                        low_z(c + 1)

            with dve.Fori(0, CHUNKS - 1) as c:
                own.enter(c, 7)
                chunk(c, True)
                own.leave(CHUNKS - 1)
            chunk(CHUNKS - 1, False)


HEADS, HD = 16, 16
SEQ_TILES = SEQ // P
Q_SCALE = 0.25


def attention(nc, res, dram):
    ctx = ExitStack()
    with ctx:
        def sb(what, shape, dt=FP32):
            return ctx.enter_context(nc.sbuf_tensor("a_" + what, shape, dt))

        def sem(what):
            return ctx.enter_context(nc.semaphore("a_" + what))

        def ps(what, shape):
            return ctx.enter_context(nc.psum_tensor("a_" + what, shape, FP32))

        wq = sb("wq", [P, KD, D])
        wkv = sb("wkv", [P, KD, 2 * D])
        wu = sb("wu", [P, KD, D])
        wo = sb("wo", [P, KD, D])
        ident = sb("ident", [P, P])
        same_head = sb("same_head", [P, P])
        mhalf = sb("mhalf", [P, TILES, HEADS])
        eps = sb("eps", [P, SEQ_TILES])
        pause = sb("pause", [P, 4])

        stats = sb("stats", [P, SEQ_TILES, 6])
        mv = sb("mv", [P, SEQ_TILES, 2])
        s1 = sb("s1", [P, SEQ_TILES])
        zn = sb("zn", [P, SEQ_TILES, D])
        zT = sb("zT", [P, KD, SEQ])
        kv = sb("kv", [P, SEQ_TILES, 2 * D])
        qT = sb("qT", [P, KD, SEQ])
        kvh = sb("kvh", [P, KD, P])
        square = sb("square", [P, TILES, D])
        su = sb("su", [P, TILES, D])
        ssq = sb("ssq", [P, TILES, HEADS])
        rinv = sb("rinv", [P, TILES, HEADS])
        og = sb("og", [P, TILES, D])
        ogT = sb("ogT", [P, TILES, D])

        ring = ps("ring", [P, 2, CHUNK])
        acc = ps("acc", [P, 2, CHUNK])
        ou = ps("ou", [P, TILES, 2 * D])

        w_q, w_kv, w_u, w_o, const_ready = sem("w_q"), sem("w_kv"), sem("w_u"), sem("w_o"), sem("const_ready")
        stats_ready, norm_ready, zn_ready = sem("stats_ready"), sem("norm_ready"), sem("zn_ready")
        ring_full, ring_free = sem("ring_full"), sem("ring_free")
        acc_full, kvh_ready, ou_full = sem("acc_full"), sem("kvh_ready"), sem("ou_full")
        square_ready, su_ready, ssq_ready, rinv_ready, og_ready = (sem(s) for s in (
            "square_ready", "su_ready", "ssq_ready", "rinv_ready", "og_ready"))
        out_full, out_free = sem("out_full"), sem("out_free")
        dve_own, pool_own = sem("dve_own"), sem("pool_own")

        TURN, KV, Q, BACK, JOBS = 0, 4, 12, 16, 20
        HALVES = SEQ // CHUNK

        block = ctx.enter_context(nc.Block())

        @block.sync
        def _(sp):
            sp.dma_start(wkv[:, :, :], dram["Wkv"]).then_inc(w_kv, 16)
            sp.dma_start(wq[:, :, :], dram["Wq"]).then_inc(w_q, 16)
            sp.dma_start(wu[:, :, :], dram["Wu"]).then_inc(w_u, 16)
            sp.dma_start(wo[:, :, :], dram["Wo"]).then_inc(w_o, 16)

        @block.gpsimd
        def _(pool):
            own = Chain(pool, pool_own)
            pool.memset(mhalf[:, :, :], -0.5)
            pool.memset(eps[:, :], EPS)
            pool.memset(same_head[:, :], 1.0)
            own.link(pool.memset(ident[:, :], 0.0))
            pool.affine_select(out=ident[:, :], in_=ident[:, :], compare_op=ALU.not_equal, fill=1.0, base=0,
                               pattern=[[-1, P]], channel_multiplier=1)
            blocks = same_head[:, :].rearrange("p (g w) -> p g w", w=HD)
            own.link(pool.affine_select(out=blocks, in_=blocks, compare_op=ALU.is_ge, fill=0.0, base=0,
                                        pattern=[[-HD, P // HD], [0, HD]], channel_multiplier=1))
            pool.affine_select(out=blocks, in_=blocks, compare_op=ALU.is_ge, fill=0.0, base=HD - 1,
                               pattern=[[HD, P // HD], [0, HD]], channel_multiplier=-1).then_inc(const_ready, 1)
            with pool.Fori(0, BATCH) as b:
                own.enter(b, 1)
                pool.wait_ge(stats_ready, b + 1)
                own.link(pool.tensor_tensor(s1[:, :], mv[:, :, 1], eps[:, :], ALU.add))
                pool.tensor_tensor(s1[:, :], s1[:, :], mhalf[:, 0, 0:SEQ_TILES], ALU.pow).then_inc(norm_ready, 1)
                for h in range(HALVES):
                    pool.wait_ge(ssq_ready, HALVES * b + h + 1)
                    pool.tensor_tensor(rinv[:, :, :], ssq[:, :, :], mhalf[:, :, :], ALU.pow).then_inc(rinv_ready, 1)
                own.leave(BATCH)

        @block.tensor
        def _(pe):
            pe.wait_ge(const_ready, 1)
            for s in (w_q, w_kv, w_u, w_o):
                pe.wait_ge(s, 16)
            with pe.Fori(0, BATCH) as b:
                def take(i):
                    pe.wait_ge(ring_free, JOBS * b + i + 1)
                    return ring[:, i % 2, :]

                def finished(i):
                    pe.wait_ge(ring_free, JOBS * b + i + 3)

                for half in range(HALVES):
                    pe.wait_ge(zn_ready, HALVES * b + half + 1)
                    for k in range(KD):
                        out = take(TURN + KD * half + k)
                        for j in range(TILES):
                            last = nc.tensor.transpose(out[:, j * P:(j + 1) * P],
                                                       zn[:, TILES * half + j, k * P:(k + 1) * P], ident[:, :])
                        last.then_inc(ring_full, 1)

                def heads_kv(j):
                    finished(KV + j)
                    if j == 0:
                        pe.wait_ge(out_free, 2 * HALVES * b + 2)
                    for g in range(KD):
                        last = nc.tensor.matmul(acc[:, g, 0:P], kv[:, j, g * P:(g + 1) * P],
                                                kv[:, j, D + g * P:D + (g + 1) * P], start=j == 0,
                                                stop=j == SEQ_TILES - 1)
                    if j == SEQ_TILES - 1:
                        last.then_inc(acc_full, 1)

                for j in range(SEQ_TILES):
                    if j % TILES == 0:
                        finished(TURN + KD * (j // TILES) + KD - 1)
                    out = take(KV + j)
                    for k in range(KD):
                        last = nc.tensor.matmul(out, zT[:, k, j * P:(j + 1) * P], wkv[:, k, :], start=k == 0,
                                                stop=k == KD - 1)
                    last.then_inc(ring_full, 1)
                    if j > 0:
                        heads_kv(j - 1)
                heads_kv(SEQ_TILES - 1)
                for half in range(HALVES):
                    for g in range(KD):
                        out = take(Q + KD * half + g)
                        for k in range(KD):
                            last = nc.tensor.matmul(out, wq[:, k, g * P:(g + 1) * P],
                                                    zT[:, k, half * CHUNK:(half + 1) * CHUNK], start=k == 0,
                                                    stop=k == KD - 1)
                        last.then_inc(ring_full, 1)
                for half in range(HALVES):
                    for j in range(TILES):
                        t = TILES * half + j
                        for k in range(KD):
                            last = nc.tensor.matmul(ou[:, j, D:], zT[:, k, t * P:(t + 1) * P], wu[:, k, :],
                                                    start=k == 0, stop=k == KD - 1)
                        if j == 0:
                            finished(Q + KD * half + KD - 1)
                            pe.wait_ge(kvh_ready, b + 1)
                        for g in range(KD):
                            last = nc.tensor.matmul(ou[:, j, g * P:(g + 1) * P], qT[:, g, t * P:(t + 1) * P],
                                                    kvh[:, g, :], start=True, stop=True)
                        last.then_inc(ou_full, 1)
                    for i in range(2):
                        out = take(BACK + 2 * half + i)
                        for h in range(2):
                            pe.wait_ge(og_ready, SEQ_TILES * b + TILES * half + 2 * i + h + 1)
                            for g in range(KD):
                                last = nc.tensor.transpose(out[:, (2 * h + g) * P:(2 * h + g + 1) * P],
                                                           og[:, 2 * i + h, g * P:(g + 1) * P], ident[:, :])
                        last.then_inc(ring_full, 1)
                    for i in range(2):
                        finished(BACK + 2 * half + i)
                        pe.wait_ge(out_free, 2 * HALVES * b + 2 * half + i + 1)
                        if half == 0 and i == 0:
                            pe.wait_ge(kvh_ready, b + 1)
                        for h in range(2):
                            for g in range(KD):
                                last = nc.tensor.matmul(acc[:, i, h * D:(h + 1) * D],
                                                        ogT[:, 2 * i + h, g * P:(g + 1) * P], wo[:, g, :],
                                                        start=g == 0, stop=g == KD - 1)
                        last.then_inc(out_full, 1)

        @block.scalar
        def _(act):
            with act.Fori(0, BATCH) as b:
                def full(i):
                    act.wait_ge(ring_full, JOBS * b + i + 1)
                    return ring[:, i % 2, :]

                for half in range(HALVES):
                    for k in range(KD):
                        ps_ = full(TURN + KD * half + k)
                        nc.scalar.activation(zT[:, k, half * CHUNK:(half + 1) * CHUNK], ps_,
                                             ACT.Copy).then_inc(ring_free, 1)
                for j in range(SEQ_TILES):
                    ps_ = full(KV + j)
                    nc.scalar.activation(kv[:, j, 0:D], ps_[:, 0:D], ACT.Relu, scale=Q_SCALE)
                    nc.scalar.activation(kv[:, j, D:], ps_[:, D:], ACT.Copy).then_inc(ring_free, 1)
                for half in range(HALVES):
                    for g in range(KD):
                        ps_ = full(Q + KD * half + g)
                        nc.scalar.activation(qT[:, g, half * CHUNK:(half + 1) * CHUNK], ps_, ACT.Relu,
                                             scale=Q_SCALE).then_inc(ring_free, 1)
                for half in range(HALVES):
                    for j in range(TILES):
                        act.wait_ge(ou_full, SEQ_TILES * b + TILES * half + j + 1)
                        nc.scalar.activation(square[:, j, :], ou[:, j, 0:D], ACT.Square).then_inc(square_ready, 1)
                        nc.scalar.activation(su[:, j, :], ou[:, j, D:], ACT.Silu).then_inc(su_ready, 1)
                    for i in range(2):
                        ps_ = full(BACK + 2 * half + i)
                        nc.scalar.activation(ogT[:, 2 * i:2 * i + 2, :].rearrange("p h d -> p (h d)"), ps_,
                                             ACT.Copy).then_inc(ring_free, 1)

        @block.vector
        def _(dve):
            own = Chain(dve, dve_own)
            nc.vector.memset(pause[:, 1:2], 0.0).then_inc(ring_free, 2)
            nc.vector.memset(pause[:, 2:3], 0.0).then_inc(out_free, 2)
            dve.wait_ge(const_ready, 1)
            with dve.Fori(0, BATCH) as b:
                own.enter(b, 5)
                for j in range(SEQ_TILES):
                    last = nc.vector.bn_stats(stats[:, j, :], res[:, SEQ_TILES * b + j, :])
                own.link(last)
                nc.vector.memset(pause[:, 0:1], 0.0)
                for j in range(SEQ_TILES):
                    last = nc.vector.bn_aggr(mv[:, j, :], stats[:, j, :])
                last.then_inc(stats_ready, 1)
                dve.wait_ge(norm_ready, b + 1)
                for half in range(HALVES):
                    for j in range(TILES * half, TILES * (half + 1)):
                        last = nc.vector.tensor_scalar(zn[:, j, :], res[:, SEQ_TILES * b + j, :], mv[:, j, 0:1],
                                                       s1[:, j:j + 1], ALU.subtract, ALU.mult)
                    last.then_inc(zn_ready, 1)
                dve.wait_ge(acc_full, b + 1)
                for g in range(KD):
                    last = nc.vector.tensor_tensor(kvh[:, g, :], acc[:, g, 0:P], same_head[:, :], ALU.mult)
                last.then_inc(kvh_ready, 1)
                for half in range(HALVES):
                    for j in range(TILES):
                        dve.wait_ge(square_ready, SEQ_TILES * b + TILES * half + j + 1)
                        last = nc.vector.reduce_sum(ssq[:, j, :], square[:, j, :].rearrange("p (h w) -> p h w", w=HD),
                                                    AX.X)
                    own.link(last)
                    nc.vector.tensor_scalar(ssq[:, :, :], ssq[:, :, :], 1.0 / HD, 1e-24, ALU.mult,
                                            ALU.max).then_inc(ssq_ready, 1)
                    dve.wait_ge(su_ready, SEQ_TILES * b + TILES * (half + 1))
                    for j in range(TILES):
                        last = nc.vector.tensor_tensor(og[:, j, :], su[:, j, :], ou[:, j, 0:D], ALU.mult)
                        own.link(last) if j == TILES - 1 else None
                    dve.wait_ge(rinv_ready, HALVES * b + half + 1)
                    for j in range(TILES):
                        o = og[:, j, :].rearrange("p (h w) -> p h w", w=HD)
                        nc.vector.tensor_tensor(o, o, rinv[:, j, :].unsqueeze(2).to_broadcast([P, HEADS, HD]),
                                                ALU.mult).then_inc(og_ready, 1)
                    for i in range(2):
                        dve.wait_ge(out_full, 2 * HALVES * b + 2 * half + i + 1)
                        x = res[:, :, :].rearrange("p (s h) d -> p s (h d)", h=2)[:, TILES * b + 2 * half + i, :]
                        nc.vector.tensor_tensor(x, x, acc[:, i, :], ALU.add).then_inc(out_free, 1)
                own.leave(BATCH)


def program(nc, dram, out):
    with nc.sbuf_tensor("res", [P, TOKENS // P, D], FP32) as res:
        mamba(nc, res, dram)
        ffn(nc, res, dram, "f")
        attention(nc, res, dram)
        ffn(nc, res, dram, "g")
        store(nc, res, out)


def store(nc, res, out):
    ctx = ExitStack()
    with ctx:
        done = ctx.enter_context(nc.semaphore("out_done"))
        block = ctx.enter_context(nc.Block())

        @block.sync
        def _(sp):
            out_v = out.rearrange("b (s p h) d -> p (b s) (h d)", p=P, h=2)
            sp.dma_start(out_v, res[:, :, :].rearrange("p (s h) d -> p s (h d)", h=2)).then_inc(done, 16)
            sp.wait_ge(done, 16)


def kernel(**inputs):
    import concourse.bacc as bacc
    from concourse.bass_utils import run_bass_kernel_spmd

    def a(name):
        return np.asarray(inputs["L0_" + name])

    def blocks(w):
        return np.ascontiguousarray(w.reshape(-1, P, w.shape[-1]).transpose(1, 0, 2))

    laid = {
        "x": a("attn_a_resid"),
        "norm_w": blocks(a("attn_a_norm_w")[:, None])[:, :, 0],
        "in_w": blocks(a("attn_a_in_w").T),
        "skip_w": blocks(a("attn_a_skip_w").T),
        "conv_w": blocks(a("attn_a_conv_w")),
        "conv_b": blocks(a("attn_a_conv_b")[:, None])[:, :, 0],
        "wd1": blocks(a("attn_a_wd1").T),
        "wd2": a("attn_a_wd2").T,
        "wd2_b": blocks(a("attn_a_wd2_b")[:, None])[:, :, 0],
        "wB": blocks(a("attn_a_wB").T),
        "wC": blocks(a("attn_a_wC").T),
        "A_log": blocks(a("attn_a_A_log")),
        "W_D": blocks(a("attn_a_W_D")[:, None])[:, :, 0],
        "out_w": blocks(a("attn_a_out_w").T),
        "Wq": blocks(a("attn_b_Wq")),
        "Wkv": blocks(np.concatenate([a("attn_b_Wk"), a("attn_b_Wv")], axis=1)),
        "Wu": blocks(a("attn_b_Wu")),
        "Wo": blocks(a("attn_b_Wo")),
        "W_q": blocks(a("ffn_W_q")),
        "keys": a("ffn_keys").transpose(1, 0, 2),
        "ffn_w": np.concatenate([
            blocks(np.concatenate([a("ffn_gate_w"), a("ffn_up_w"), a("ffn_down_embed").T], axis=1)).reshape(P, -1),
            blocks(np.concatenate([a("ffn_down_w"), a("ffn_up_embed")], axis=0)).reshape(P, -1),
        ], axis=1).reshape(P, PIECES, -1),
    }
    nc = bacc.Bacc("TRN2", target_bir_lowering=False, num_devices=1)
    arrays, dram = {}, {}
    for name, w in laid.items():
        arrays["in_" + name] = np.ascontiguousarray(w)
        dram[name] = nc.dram_tensor("in_" + name, w.shape, FP32, kind="ExternalInput").ap()
    out = nc.dram_tensor("out", (BATCH, SEQ, D), FP32, kind="ExternalOutput").ap()
    program(nc, dram, out)
    r = run_bass_kernel_spmd(nc, [arrays], core_ids=[0])
    return r.results[0]["out"]
```

```python
from contextlib import ExitStack

import numpy as np

import concourse.bass as bass
from concourse import mybir

FP32 = mybir.dt.float32
BF16 = mybir.dt.bfloat16
ALU = mybir.AluOpType
ACT = mybir.ActivationFunctionType
AX = mybir.AxisListType

P = 128
BATCH, SEQ, D = 4, 1024, 256
TOKENS = BATCH * SEQ
CHUNK = 512
CHUNKS = TOKENS // CHUNK
TILES = CHUNK // P
KD = D // P
E, N, R, TAPS = 512, 16, 128, 4
KE = E // P
EPS = 1e-5
EXP_LN_SET = "natural_log_exp_and_others"


def need(eng, sem, value):
    if isinstance(value, int) and value <= 0:
        return
    eng.wait_ge(sem, value)


class Chain:

    def __init__(self, eng, sem):
        self.eng, self.sem, self.base, self.k = eng, sem, 0, 0

    def link(self, ins):
        self.k += 1
        ins.then_inc(self.sem, 1)
        self.eng.wait_ge(self.sem, self.base + self.k)

    def enter(self, i, steps):
        self.outer, self.steps = self.base + self.k, steps
        self.base, self.k = self.outer + i * steps, 0

    def leave(self, times):
        assert self.k == self.steps, f"{self.k} links in the loop's body"
        self.base, self.k = self.outer + times * self.steps, 0


def in_time(ap):
    return ap.rearrange("x (b p h) -> x b h p", b=2, h=2)


def mamba(nc, res, dram):
    RING = 4
    ctx = ExitStack()
    with ctx:
        def sb(name, shape, dt=FP32):
            return ctx.enter_context(nc.sbuf_tensor("m_" + name, shape, dt))

        def sem(name):
            return ctx.enter_context(nc.semaphore("m_" + name))

        inw = sb("inw", [P, KD, E])
        skw = sb("skw", [P, KD, E])
        wd1 = sb("wd1", [P, KE, R])
        wd2 = sb("wd2", [P, E])
        wbc = sb("wbc", [P, KE, P])
        outw = sb("outw", [P, KE, D])
        normw = sb("normw", [P, KD])
        convw = sb("convw", [P, KE, TAPS])
        convb = sb("convb", [P, KE])
        wd2b = sb("wd2b", [P, KE])
        wskip = sb("wskip", [P, KE])
        negA = sb("negA", [P, KE, N])
        ident = sb("ident", [P, P])
        pick = sb("pick", [P, 2 * N], BF16)
        mhalf = sb("mhalf", [P, 2, TILES])
        pause = sb("pause", [P, 3])

        stats = sb("stats", [P, TILES, 6])
        mv = sb("mv", [P, TILES, 2])
        sc = sb("sc", [P, 7, TILES])
        rn = sb("rn", [P, TILES, D])
        rawbc = rn[:, 0:2, :].rearrange("p t d -> p (t d)")
        rnT = sb("rnT", [P, KD, CHUNK])
        xin = sb("xin", [P, KE, TAPS - 1 + CHUNK])
        work = sb("work", [P, KE, CHUNK])
        rT = sb("rT", [P, CHUNK])
        xs = sb("xs", [P, 2, KE, CHUNK])
        gate = sb("gate", [P, 2, KE, CHUNK])
        delta = sb("delta", [P, 2, KE, CHUNK])
        dx = sb("dx", [P, 2, KE, CHUNK])
        stack = sb("stack", [P, 2, CHUNK], BF16)
        dA = sb("dA", [P, 2, KE, CHUNK])
        U = sb("U", [P, RING, KE, CHUNK])
        BC = sb("BC", [P, RING, 2, CHUNK])
        carry = sb("carry", [P, KE, N])

        y = ctx.enter_context(nc.psum_tensor("m_y", [P, KE, CHUNK], FP32))
        psBC = ctx.enter_context(nc.psum_tensor("m_psBC", [P, 2, CHUNK], FP32))
        job = ctx.enter_context(nc.psum_tensor("m_job", [P, 2, CHUNK], FP32))

        x_first, x_rest = sem("x_first"), sem("x_rest")
        w_in, w_conv, w_d, w_bc, w_out, w_A = (sem(s) for s in ("w_in", "w_conv", "w_d", "w_bc", "w_out", "w_A"))
        const_ready = sem("const_ready")
        stats_ready, norm_ready, rn_ready = sem("stats_ready"), sem("norm_ready"), sem("rn_ready")
        job_full, job_free = sem("job_full"), sem("job_free")
        conv_done, xs_ready, split_done = sem("conv_done"), sem("xs_ready"), sem("split_done")
        ln_ready, delta_ready = sem("ln_ready"), sem("delta_ready")
        BC_full, BC_ready, xin_ready = sem("BC_full"), sem("BC_ready"), sem("xin_ready")
        dA_ready, mult_done, h_ready = sem("dA_ready"), sem("mult_done"), sem("h_ready")
        dx_ready = sem("dx_ready")
        hc_ready, nsum_done = sem("hc_ready"), sem("nsum_done")
        factors_ready, x_ready, gate_ready = sem("factors_ready"), sem("x_ready"), sem("gate_ready")
        y_read, gate_done, out_full, out_free = sem("y_read"), sem("gate_done"), sem("out_full"), sem("out_free")
        dve_own, act_own, pool_own = sem("dve_own"), sem("act_own"), sem("pool_own")

        PE_AT = {0: ("turn",), 1: ("in0", "in1"), 4: ("in2",), 5: ("in3",), 6: ("in4",), 7: ("in5",), 8: ("in6",),
                 9: ("in7",), 10: ("low",), 11: ("bc",), 12: ("dt0", "dt1"), 13: ("dt2", "dt3")}
        ACT_AT = {0: ("turn",), 1: ("in0",), 2: ("in1",), 4: ("in2",), 5: ("in3",), 6: ("in4",), 7: ("in5",),
                  8: ("in6",), 9: ("in7", "silu", "silu_gate", "exp_table"), 10: ("low",), 11: ("bc",),
                  12: ("dt0", "dt1"), 13: ("dt2", "dt3", "softplus"), 15: ("norm", "double")}
        DVE_AT = {0: ("edge",), 3: ("conv0",), 4: ("conv1",), 6: ("conv2",), 7: ("conv3",), 12: ("stats",),
                  13: ("split",), 14: ("delta",), 15: ("norm",)}
        POOL_AT = {13: ("factors",), 15: ("dx",)}
        ORDER = ("turn",) + tuple(name for names in PE_AT.values() for name in names)
        JOB = {name: i for i, name in enumerate(ORDER)}
        JOBS = len(ORDER)
        EARLY = ("stats", "factors", "norm", "double")
        HEAD = range(0, 6)
        TAIL = range(6, N)
        GATED, MULTIPLIED, OUT, ADDED = 1, 2, (2, 3), (3, 4)

        BEFORE = sum((2 if name == "turn" else 1) for n in range(OUT[0] + 1) for name in PE_AT.get(n, ()))
        assert BEFORE % 2 == 0 and OUT[1] not in PE_AT

        def pieces(c):
            return [slice(e, e + 1) for e in range(KE)] if isinstance(c, int) and c == 0 else [slice(0, KE)]

        def parts(at, n, c, part, q):
            for name in at.get(n, ()):
                further = 2 if name in EARLY else 1
                if not isinstance(c, int) or c + further < CHUNKS:
                    assert name not in EARLY or n in TAIL
                    part(name, c + further, q if name in EARLY else 1 - q)

        LEAD = 2

        def ahead(c, n, q, last):
            if n + LEAD < N:
                return c, n + LEAD, q
            return None if last else (c + 1, n + LEAD - N, 1 - q)

        def schedule(head, tail, loop, first, steps=None, chain=None):
            first()
            head(0, 0, False)
            with loop(0, BATCH - 1) as b:
                if chain:
                    chain.enter(b, steps)
                tail(2 * b, 0, True)
                head(2 * b + 1, 1, True)
                tail(2 * b + 1, 1, True)
                head(2 * b + 2, 0, True)
                if chain:
                    chain.leave(BATCH - 1)
            tail(CHUNKS - 2, 0, True)
            head(CHUNKS - 1, 1, True)
            tail(CHUNKS - 1, 1, False)

        block = ctx.enter_context(nc.Block())

        @block.sync
        def _(sp):
            x_v = dram["x"].rearrange("b (s p h) d -> p (b s) (h d)", p=P, h=2)
            res_v = res[:, :, :].rearrange("p (s h) d -> p s (h d)", h=2)
            sp.dma_start(res_v[:, 0:2, :], x_v[:, 0:2, :]).then_inc(x_first, 16)
            sp.dma_start(normw[:, :], dram["norm_w"]).then_inc(w_in, 16)
            sp.dma_start(inw[:, :, :], dram["in_w"]).then_inc(w_in, 16)
            sp.dma_start(skw[:, :, :], dram["skip_w"]).then_inc(w_in, 16)
            sp.dma_start(convw[:, :, :], dram["conv_w"]).then_inc(w_conv, 16)
            sp.dma_start(convb[:, :], dram["conv_b"]).then_inc(w_conv, 16)
            sp.dma_start(wd2b[:, :], dram["wd2_b"]).then_inc(w_conv, 16)
            sp.dma_start(wskip[:, :], dram["W_D"]).then_inc(w_conv, 16)
            sp.dma_start(wd1[:, :, :], dram["wd1"]).then_inc(w_d, 16)
            sp.dma_start(wd2[:, :], dram["wd2"]).then_inc(w_d, 16)
            for k in range(4):
                sp.dma_start(wbc[:, :, 32 * k:32 * k + N], dram["wB"]).then_inc(w_bc, 16)
                sp.dma_start(wbc[:, :, 32 * k + N:32 * k + 2 * N], dram["wC"]).then_inc(w_bc, 16)
            sp.dma_start(negA[:, :, :], dram["A_log"]).then_inc(w_A, 16)
            sp.dma_start(res_v[:, 2:, :], x_v[:, 2:, :]).then_inc(x_rest, 16)
            sp.dma_start(outw[:, :, :], dram["out_w"]).then_inc(w_out, 16)

        @block.gpsimd
        def _(pool):
            own = Chain(pool, pool_own)

            def first():
                pool.memset(mhalf[:, :, :], -0.5)
                pool.memset(pick[:, :], 0.0)
                own.link(pool.memset(ident[:, :], 0.0))
                own.link(pool.affine_select(out=ident[:, :], in_=ident[:, :], compare_op=ALU.not_equal, fill=1.0,
                                            base=0, pattern=[[-1, P]], channel_multiplier=1))
                for row in (0, 64, 96):
                    last = pool.affine_select(out=pick[:, :], in_=pick[:, :], compare_op=ALU.not_equal,
                                              fill=1.0, base=-row, pattern=[[-1, 2 * N]], channel_multiplier=1)
                    own.link(last)
                pool.memset(pause[:, 1:2], 0.0).then_inc(const_ready, 1)
                part("factors", 0, 0)
                part("factors", 1, 1)

            def part(name, c, q):
                if name == "factors":
                    pool.wait_ge(stats_ready, c + 1)
                    pool.tensor_tensor(sc[:, 2:4, :], sc[:, 0:2, :], mhalf[:, :, :], ALU.pow).then_inc(norm_ready, 1)
                elif name == "dx":
                    pool.wait_ge(delta_ready, KE * (c + 1))
                    pool.tensor_tensor(dx[:, q, :, :], delta[:, q, :, :], xs[:, q, :, :], ALU.mult).then_inc(dx_ready, 1)

            def slots(c, q, which, finish):
                for n in which:
                    if finish and n == MULTIPLIED:
                        pool.wait_ge(gate_ready, c)
                        pool.wait_ge(y_read, c)
                        pool.tensor_tensor(gate[:, 1 - q, :, :], gate[:, 1 - q, :, :], xs[:, 1 - q, :, :],
                                           ALU.mult).then_inc(gate_done, 1)
                    parts(POOL_AT, n, c, part, q)
                    m = N * c + n
                    pool.wait_ge(h_ready, m + 1)
                    u = U[:, n % RING, :, :]
                    pool.tensor_tensor(u, u, BC[:, n % RING, 1, :].unsqueeze(1).to_broadcast([P, KE, CHUNK]),
                                       ALU.mult).then_inc(hc_ready, 1)

            schedule(lambda c, q, more: slots(c, q, HEAD, more), lambda c, q, _: slots(c, q, TAIL, False),
                     pool.Fori, first)

        @block.tensor
        def _(pe):
            def take(c, i):
                if i in (BEFORE, BEFORE + 1):
                    need(pe, out_free, 2 * c - 1 + i - BEFORE)
                    pe.wait_ge(job_free, JOBS * c + i - 1)
                else:
                    need(pe, job_free, JOBS * c + i - 1)
                return job[:, i % 2, :]

            def mm(out, pairs):
                for k, (w, x) in enumerate(pairs):
                    last = nc.tensor.matmul(out, w, x, start=k == 0, stop=k == len(pairs) - 1)
                return last

            def part(name, c, q):
                if name == "turn":
                    pe.wait_ge(rn_ready, c + 1)
                    for k in range(KD):
                        out = take(c, k)
                        for j in range(TILES):
                            last = nc.tensor.transpose(out[:, j * P:(j + 1) * P], rn[:, j, k * P:(k + 1) * P],
                                                       ident[:, :])
                        last.then_inc(job_full, 1)
                elif name[:2] == "in":
                    i = int(name[2])
                    if i == 0:
                        pe.wait_ge(job_free, JOBS * c + 2)
                    w = inw if i < KE else skw
                    e = i % KE * P
                    mm(take(c, JOB[name]), [(w[:, k, e:e + P], rnT[:, k, :]) for k in range(KD)]).then_inc(job_full, 1)
                elif name == "low":
                    out = take(c, JOB[name])
                    for es in pieces(c):
                        pe.wait_ge(xs_ready, KE * c + es.stop)
                        for k in range(es.start, es.stop):
                            last = nc.tensor.matmul(out, wd1[:, k, :], xs[:, q, k, :], start=k == 0, stop=k == KE - 1)
                    last.then_inc(job_full, 1)
                elif name == "bc":
                    mm(take(c, JOB[name]), [(wbc[:, k, :], xs[:, q, k, :]) for k in range(KE)]).then_inc(job_full, 1)
                elif name[:2] == "dt":
                    e = int(name[2])
                    if e == 0:
                        pe.wait_ge(job_free, JOBS * c + JOB["low"] + 1)
                    mm(take(c, JOB[name]), [(wd2[:, e * P:(e + 1) * P], rT[:, :])]).then_inc(job_full, 1)

            def spread(c, n, q):
                if n == 0:
                    pe.wait_ge(split_done, c + 1)
                need(pe, BC_ready, N * c + n)
                for i in range(2):
                    r = i * N + n
                    last = nc.tensor.matmul(psBC[:, i, :], pick[:, r:r + 1].to_broadcast([P, P]), stack[:, q, :],
                                            start=True, stop=True)
                last.then_inc(BC_full, 1)

            def nsum(c, n, q):
                m = N * c + n
                pe.wait_ge(hc_ready, m + 1)
                if n == 0:
                    need(pe, y_read, c)
                for e in range(KE):
                    last = nc.tensor.matmul(y[:, e, :], ident[:, :], U[:, n % RING, e, :], start=n == 0,
                                            stop=n == N - 1)
                last.then_inc(nsum_done, 1)

            def output(c, q, which):
                pe.wait_ge(gate_done, c + 1)
                for i in which:
                    if not isinstance(c, int) or c < CHUNKS - 2:
                        pe.wait_ge(job_free, JOBS * (c + 2) + BEFORE - 1 + i)
                    elif c == CHUNKS - 2:
                        pe.wait_ge(job_free, JOBS * CHUNKS + i - 1)
                    else:
                        pe.wait_ge(out_free, 2 * c + 1 + i)
                    for h in range(2):
                        for k in range(KE):
                            last = nc.tensor.matmul(job[:, i, h * D:(h + 1) * D],
                                                    in_time(gate[:, q, k, :])[:, i, h, :], outw[:, k, :],
                                                    start=k == 0, stop=k == KE - 1)
                    last.then_inc(out_full, 1)

            def slots(c, q, which, finish, last=False):
                for n in which:
                    if ahead(c, n, q, last):
                        spread(*ahead(c, n, q, last))
                    parts(PE_AT, n, c, part, q)
                    if n > 0:
                        nsum(c, n - 1, q)
                    elif finish:
                        nsum(c - 1, N - 1, 1 - q)
                    if finish and n in OUT:
                        output(c - 1, 1 - q, (OUT.index(n),))

            def head(c, q, more):
                slots(c, q, HEAD, more)

            def tail(c, q, more):
                slots(c, q, TAIL, False, not more)

            def first():
                pe.wait_ge(const_ready, 1)
                pe.wait_ge(w_in, 48)
                for name in ORDER[1:]:
                    if name == "low":
                        pe.wait_ge(w_d, 32)
                        pe.wait_ge(w_bc, 128)
                    part(name, 0, 0)
                for n in range(LEAD):
                    spread(0, n, 0)
                pe.wait_ge(w_out, 16)

            schedule(head, tail, pe.Fori, first)
            nsum(CHUNKS - 1, N - 1, 1)
            output(CHUNKS - 1, 1, range(2))

        @block.scalar
        def _(act):
            own = Chain(act, act_own)

            def part(name, c, q):
                def full(i):
                    act.wait_ge(job_full, JOBS * c + i + 1)

                if name == "norm":
                    act.wait_ge(factors_ready, c + 1)
                    need(act, split_done, c)
                    for j in range(TILES):
                        last = nc.scalar.activation(rn[:, j, :], res[:, TILES * c + j, :], ACT.Identity,
                                                    bias=sc[:, 6, j:j + 1], scale=sc[:, 3, j:j + 1])
                    last.then_inc(rn_ready, 1)
                elif name == "double":
                    for j in range(TILES):
                        x = res[:, TILES * c + j, :]
                        last = nc.scalar.activation(x, x, ACT.Identity, bias=sc[:, 5, j:j + 1],
                                                    scale=sc[:, 4, j:j + 1])
                    last.then_inc(x_ready, 1)
                elif name == "turn":
                    for k in range(KD):
                        full(k)
                        nc.scalar.activation(in_time(rnT[:, k, :]),
                                             job[:, k, :].rearrange("x (b h p) -> x b h p", b=2, h=2), ACT.Copy,
                                             scale=normw[:, k:k + 1]).then_inc(job_free, 1)
                elif name[:2] == "in":
                    i = int(name[2])
                    full(JOB[name])
                    ps = job[:, JOB[name] % 2, :]
                    if i < KE:
                        if i == 0:
                            act.wait_ge(xin_ready, c + 1)
                        nc.scalar.activation(xin[:, i, TAPS - 1:], ps, ACT.Copy)
                        nc.scalar.activation(work[:, i, :], ps, ACT.Identity, bias=convb[:, i:i + 1],
                                             scale=convw[:, i, TAPS - 1:TAPS]).then_inc(job_free, 1)
                    else:
                        nc.scalar.activation(gate[:, q, i - KE, :], ps, ACT.Copy).then_inc(job_free, 1)
                elif name == "silu":
                    for es in pieces(c):
                        act.wait_ge(conv_done, KE * c + es.stop)
                        nc.scalar.activation(xs[:, q, es, :], work[:, es, :],
                                             ACT.Silu).then_inc(xs_ready, es.stop - es.start)
                elif name == "silu_gate":
                    act.wait_ge(job_free, JOBS * c + JOB["in7"] + 1)
                    nc.scalar.activation(gate[:, q, :, :], gate[:, q, :, :], ACT.Silu).then_inc(gate_ready, 1)
                elif name == "exp_table":
                    nc.scalar.preload_act_table_set(EXP_LN_SET)
                elif name == "low":
                    full(JOB[name])
                    nc.scalar.activation(rT[:, :], job[:, JOB[name] % 2, :], ACT.Copy).then_inc(job_free, 1)
                elif name == "bc":
                    full(JOB[name])
                    nc.scalar.activation(rawbc, job[:, JOB[name] % 2, :], ACT.Copy).then_inc(job_free, 1)
                elif name[:2] == "dt":
                    e = int(name[2])
                    full(JOB[name])
                    z = job[:, JOB[name] % 2, :]
                    nc.scalar.activation(delta[:, q, e, :], z, ACT.Identity, bias=wd2b[:, e:e + 1])
                    nc.scalar.activation(work[:, e, :], z, ACT.Abs, bias=wd2b[:, e:e + 1]).then_inc(job_free, 1)
                elif name == "softplus":
                    act.wait_ge(job_free, JOBS * c + JOB["dt3"] + 1)
                    for es in pieces(c):
                        w = work[:, es, :]
                        own.link(nc.scalar.activation(w, w, ACT.Exp, scale=-1.0))
                        nc.scalar.activation(w, w, ACT.Ln, bias=1.0).then_inc(ln_ready, es.stop - es.start)

            def decay(c, n, q):
                if n == 0:
                    act.wait_ge(delta_ready, KE * (c + 1))
                need(act, h_ready, N * c + n - 1)
                for e in range(KE):
                    last = nc.scalar.activation(dA[:, n % 2, e, :], delta[:, q, e, :], ACT.Exp,
                                                scale=negA[:, e, n:n + 1])
                last.then_inc(dA_ready, 1)

            def keep_BC(c, n, q):
                m = N * c + n
                act.wait_ge(BC_full, m + 1)
                need(act, hc_ready, m - RING + 1)
                nc.scalar.activation(BC[:, n % RING, :, :], psBC[:, :, :], ACT.Copy).then_inc(BC_ready, 1)

            def slots(c, q, which, last=False):
                for n in which:
                    if n < N - 1:
                        decay(c, n + 1, q)
                    elif not last:
                        decay(c + 1, 0, 1 - q)
                    if ahead(c, n, q, last):
                        keep_BC(*ahead(c, n, q, last))
                    parts(ACT_AT, n, c, part, q)

            def first():
                part("norm", 0, 0)
                act.wait_ge(w_in, 48)
                act.wait_ge(w_conv, 64)
                for name in [n for names in ACT_AT.values() for n in names if n not in EARLY]:
                    part(name, 0, 0)
                    if name == "turn":
                        part("double", 0, 0)
                    if name == "exp_table":
                        act.wait_ge(w_A, 16)
                        own.link(nc.scalar.activation(negA[:, :, :], negA[:, :, :], ACT.Exp))
                        own.link(nc.scalar.activation(negA[:, :, :], negA[:, :, :], ACT.Copy, scale=-1.0))
                for n in range(LEAD):
                    keep_BC(0, n, 0)
                decay(0, 0, 0)
                part("norm", 1, 1)
                part("double", 1, 1)

            schedule(lambda c, q, _: slots(c, q, HEAD), lambda c, q, more: slots(c, q, TAIL, not more), act.Fori,
                     first, 2, own)

        @block.vector
        def _(dve):
            own = Chain(dve, dve_own)

            def part(name, c, q):
                if name == "edge":
                    if q:
                        last = nc.vector.tensor_copy(xin[:, :, 0:TAPS - 1], xin[:, :, CHUNK:])
                    else:
                        last = nc.vector.memset(xin[:, :, 0:TAPS - 1], 0.0)
                    last.then_inc(xin_ready, 1)
                elif name == "stats":
                    for j in range(TILES):
                        last = nc.vector.bn_stats(stats[:, j, :], res[:, TILES * c + j, :])
                    own.link(last)
                    nc.vector.memset(pause[:, 0:1], 0.0)
                    for j in range(TILES):
                        last = nc.vector.bn_aggr(mv[:, j, :], stats[:, j, :])
                    own.link(last)
                    nc.vector.tensor_scalar(sc[:, 0, :], mv[:, :, 1], EPS, None, ALU.add)
                    nc.vector.tensor_scalar(sc[:, 1, :], mv[:, :, 1], 1.0 + EPS, EPS * EPS, ALU.mult,
                                            ALU.add).then_inc(stats_ready, 1)
                elif name == "norm":
                    dve.wait_ge(norm_ready, c + 1)
                    nc.vector.tensor_scalar(sc[:, 4, :], sc[:, 2, :], 1.0, None, ALU.add)
                    nc.vector.scalar_tensor_tensor(sc[:, 5, :], mv[:, :, 0], -1.0, sc[:, 2, :], ALU.mult, ALU.mult)
                    nc.vector.scalar_tensor_tensor(sc[:, 6, :], mv[:, :, 0], -1.0, sc[:, 3, :], ALU.mult,
                                                   ALU.mult).then_inc(factors_ready, 1)
                elif name[:4] == "conv":
                    for e in (int(name[4]),):
                        dve.wait_ge(job_free, JOBS * c + JOB[f"in{e}"] + 1)
                        for k in range(TAPS - 1):
                            last = nc.vector.scalar_tensor_tensor(work[:, e, :], xin[:, e, k:k + CHUNK],
                                                                  convw[:, e, k:k + 1], work[:, e, :],
                                                                  ALU.mult, ALU.add)
                            if k < TAPS - 2:
                                own.link(last)
                    last.then_inc(conv_done, 1)
                elif name == "split":
                    dve.wait_ge(job_free, JOBS * c + JOB["bc"] + 1)
                    own.link(nc.vector.tensor_copy(stack[:, q, :], rawbc))
                    for p in (64, 96):
                        own.link(nc.vector.tensor_tensor(rawbc[p:, :], rawbc[p:, :], stack[p:, q, :], ALU.subtract))
                        last = nc.vector.tensor_copy(stack[p:, q, :], rawbc[p:, :])
                        if p == 64:
                            own.link(last)
                    last.then_inc(split_done, 1)
                elif name == "delta":
                    for es in pieces(c):
                        dve.wait_ge(ln_ready, KE * c + es.stop)
                        nc.vector.scalar_tensor_tensor(delta[:, q, es, :], delta[:, q, es, :], 0.0, work[:, es, :],
                                                       ALU.max, ALU.add).then_inc(delta_ready, es.stop - es.start)

            def unit(c, n, q):
                m = N * c + n
                u = U[:, n % RING, :, :]
                dve.wait_ge(BC_ready, m + 1)
                if n == 0:
                    dve.wait_ge(dx_ready, c + 1)
                need(dve, nsum_done, m - RING + 1)
                nc.vector.tensor_tensor(u, dx[:, q, :, :], BC[:, n % RING, 0, :].unsqueeze(1).to_broadcast([P, KE, CHUNK]),
                                        ALU.mult).then_inc(mult_done, 1)
                dve.wait_ge(mult_done, m + 1)
                dve.wait_ge(dA_ready, m + 1)
                for e in range(KE):
                    start = carry[:, e, n:n + 1] if q else 0.0
                    last = nc.vector.tensor_tensor_scan(u[:, e, :], dA[:, n % 2, e, :], u[:, e, :], start,
                                                        ALU.mult, ALU.add)
                if q == 0:
                    own.link(last)
                    last = nc.vector.tensor_copy(carry[:, :, n], u[:, :, CHUNK - 1])
                last.then_inc(h_ready, 1)

            def gated(c, q):
                dve.wait_ge(nsum_done, N * c + N)
                for e in range(KE):
                    x = xs[:, q, e, :]
                    last = nc.vector.scalar_tensor_tensor(x, x, wskip[:, e:e + 1], y[:, e, :], ALU.mult, ALU.add)
                last.then_inc(y_read, 1)

            def add_output(c, which):
                for i in which:
                    dve.wait_ge(out_full, 2 * c + 1 + i)
                    dve.wait_ge(x_ready, c + 1)
                    x = res[:, :, :].rearrange("p (s h) d -> p s (h d)", h=2)[:, 2 * c + i, :]
                    nc.vector.tensor_tensor(x, x, job[:, i, :], ALU.add).then_inc(out_free, 1)

            def head(c, q, more):
                for n in HEAD:
                    unit(c, n, q)
                    parts(DVE_AT, n, c, part, q)
                    if more and n == GATED:
                        gated(c - 1, 1 - q)
                    if more and n in ADDED:
                        add_output(c - 1, (ADDED.index(n),))

            def tail(c, q, more):
                for n in TAIL:
                    unit(c, n, q)
                    parts(DVE_AT, n, c, part, q)

            def first():
                nc.vector.memset(pause[:, 2:3], 0.0).then_inc(out_free, 2)
                dve.wait_ge(x_first, 16)
                dve.wait_ge(w_conv, 64)
                part("stats", 0, 0)
                part("norm", 0, 0)
                for name in [n for names in DVE_AT.values() for n in names if n not in EARLY]:
                    part(name, 0, 0)
                    if name == "split":
                        dve.wait_ge(x_rest, 16)
                        part("stats", 1, 1)
                        part("norm", 1, 1)
                dve.wait_ge(delta_ready, KE)
                nc.vector.tensor_tensor(dx[:, 0, :, :], delta[:, 0, :, :], xs[:, 0, :, :], ALU.mult).then_inc(dx_ready, 1)

            schedule(head, tail, dve.Fori, first, 44, own)
            gated(CHUNKS - 1, 1)
            dve.wait_ge(y_read, CHUNKS)
            dve.wait_ge(gate_ready, CHUNKS)
            nc.vector.tensor_tensor(gate[:, 1, :, :], gate[:, 1, :, :], xs[:, 1, :, :], ALU.mult).then_inc(gate_done, 1)
            add_output(CHUNKS - 1, range(2))


HIDDEN, KEYS, EXPERTS, TOP = 1024, 64, 512, 8
KM = (HIDDEN + EXPERTS) // P
KH = HIDDEN // P
ROWS = TOP * KEYS
assert ROWS == EXPERTS
UPPER = 2 * HIDDEN + EXPERTS
WEIGHTS = KD * UPPER + KM * D
PIECES = 4
FP32R = mybir.dt.float32r


class Shared:

    def __init__(self, sb):
        self.keyz = sb("keyz", [P, 2, 2, KEYS])
        self.weights = [sb(f"weights_{part}", [P, PIECES, WEIGHTS // PIECES], FP32R) for part in ("hi", "lo")]
        self.wq = sb("wq", [P, KD, P])
        self.ident = sb("ident", [P, P])


class Norms:

    def __init__(self, sb):
        self.mv = sb("mv", [P, CHUNKS * TILES, 2])
        self.var = sb("var", [P, CHUNKS * TILES])
        self.inv = sb("inv", [P, CHUNKS * TILES, 1])


def token_statistics(nc, own, norms, res, stats, mv4, pause, c):
    for j in range(TILES):
        last = nc.vector.bn_stats(stats[:, j, :], res[:, TILES * c + j, :])
    own.link(last)
    nc.vector.memset(pause[:, 0:1], 0.0)
    for j in range(TILES):
        last = nc.vector.bn_aggr(mv4[:, j, :], stats[:, j, :])
    own.link(last)
    return nc.vector.tensor_copy(norms.mv[:, :, :].rearrange("p (c j) v -> p c j v", j=TILES)[:, c, :, :], mv4[:, :, :])


def ffn(nc, res, dram, name, shared, norms, first, out=None):
    ctx = ExitStack()
    with ctx:
        def sb(what, shape, dt=FP32):
            return ctx.enter_context(nc.sbuf_tensor(f"{name}_{what}", shape, dt))

        z = [sb("z_hi", [P, KD, CHUNK], FP32R), sb("z_lo", [P, KD, CHUNK], FP32R)]
        QT = sb("QT", [P, CHUNKS, CHUNK])
        ffn_queries(nc, res, dram, name + "q", shared, norms, first, z, QT)
        ffn_layers(nc, res, name + "l", shared, norms, first, z, QT, out)


def ffn_queries(nc, res, dram, name, shared, norms, first, z, QT):
    ctx = ExitStack()
    with ctx:
        def sb(what, shape, dt=FP32):
            return ctx.enter_context(nc.sbuf_tensor(f"{name}_{what}", shape, dt))

        def sem(what):
            return ctx.enter_context(nc.semaphore(f"{name}_{what}"))

        def ps(what, shape):
            return ctx.enter_context(nc.psum_tensor(f"{name}_{what}", shape, FP32))

        keyz, weights, wq, ident = shared.keyz, shared.weights, shared.wq, shared.ident
        whole = sb("whole", [P, PIECES, WEIGHTS // PIECES]) if first else None
        mhalf = sb("mhalf", [P, TILES])
        pause = sb("pause", [P, 2])
        stats = sb("stats", [P, TILES, 6])
        mv4 = sb("mv4", [P, TILES, 2])
        zn = sb("zn", [P, 2, TILES, D])
        zT = sb("zT", [P, 2, KD, CHUNK])
        psT, psQ = ps("psT", [P, 2, KD, CHUNK]), ps("psQ", [P, 2, CHUNK])

        w_q, w_keys, w_piece = sem("w_q"), sem("w_keys"), [sem(f"w_piece{i}") for i in range(PIECES)]
        const_ready, keyz_clear = sem("const_ready"), sem("keyz_clear")
        var_ready, inv_ready, zn_ready = sem("var_ready"), sem("inv_ready"), sem("zn_ready")
        turn_full, zT_ready, q_full, QT_ready = sem("turn_full"), sem("zT_ready"), sem("q_full"), sem("QT_ready")
        hi_ready, z_high, z_low = sem("hi_ready"), sem("z_high"), sem("z_low")
        dve_own, pool_own = sem("dve_own"), sem("pool_own")

        def low(eng, i):
            eng.wait_ge(hi_ready, i + 1)
            eng.tensor_tensor(weights[1][:, i, :], whole[:, i, :], weights[0][:, i, :].bitcast(FP32), ALU.subtract)

        block = ctx.enter_context(nc.Block())

        @block.sync
        def _(sp):
            if first:
                sp.dma_start(wq[:, :, :], dram["W_q"]).then_inc(w_q, 16)
                for i in range(PIECES):
                    sp.dma_start(whole[:, i, :], dram["ffn_w"][:, i, :]).then_inc(w_piece[i], 16)
                sp.wait_ge(keyz_clear, 1)
                sp.dma_start(keyz[0:64, :, 0, :], dram["keys"]).then_inc(w_keys, 16)
                sp.dma_start(keyz[64:128, :, 1, :], dram["keys"]).then_inc(w_keys, 16)
                sp.wait_ge(w_keys, 32)

        @block.gpsimd
        def _(pool):
            own = Chain(pool, pool_own)
            pool.memset(mhalf[:, :], -0.5)
            if first:
                own.link(pool.memset(ident[:, :], 0.0))
                own.link(pool.affine_select(out=ident[:, :], in_=ident[:, :], compare_op=ALU.not_equal, fill=1.0,
                                            base=0, pattern=[[-1, P]], channel_multiplier=1))
                pool.memset(keyz[:, :, :, :], 0.0).then_inc(keyz_clear, 1)
            pool.memset(pause[:, 1:2], 0.0).then_inc(const_ready, 1)
            pool.wait_ge(const_ready, 1)

            for c in range(CHUNKS):
                at = slice(TILES * c, TILES * (c + 1))
                pool.wait_ge(var_ready, c + 1 if first else 1)
                pool.tensor_tensor(norms.inv[:, at, 0], norms.var[:, at], mhalf[:, :], ALU.pow).then_inc(inv_ready, 1)
            for i in range(PIECES // 2) if first else ():
                low(pool, i)

        @block.tensor
        def _(pe):
            pe.wait_ge(const_ready, 1)

            def turn(c, q):
                pe.wait_ge(zn_ready, c + 1)
                for k in range(KD):
                    for j in range(TILES):
                        last = nc.tensor.transpose(psT[:, q, k, j * P:(j + 1) * P], zn[:, q, j, k * P:(k + 1) * P],
                                                   ident[:, :])
                last.then_inc(turn_full, 1)

            def queries(c, q):
                pe.wait_ge(zT_ready, c + 1)
                for k in range(KD):
                    last = nc.tensor.matmul(psQ[:, q, :], wq[:, k, :], zT[:, q, k, :], start=k == 0, stop=k == KD - 1)
                last.then_inc(q_full, 1)

            turn(0, 0)
            if first:
                pe.wait_ge(w_q, 16)
            with pe.Fori(0, CHUNKS // 2 - 1) as b:
                turn(2 * b + 1, 1)
                queries(2 * b, 0)
                pe.wait_ge(z_low, 1)
                turn(2 * b + 2, 0)
                queries(2 * b + 1, 1)
            turn(CHUNKS - 1, 1)
            queries(CHUNKS - 2, 0)
            queries(CHUNKS - 1, 1)

        @block.scalar
        def _(act):
            def fetch(c, q):
                act.wait_ge(turn_full, c + 1)
                nc.scalar.activation(zT[:, q, :, :], psT[:, q, :, :], ACT.Copy).then_inc(zT_ready, 1)

            def keep_queries(c, q):
                act.wait_ge(q_full, c + 1)
                nc.scalar.activation(in_time(QT[:, c, :]), psQ[:, q, :].rearrange("x (b h p) -> x b h p", b=2, h=2),
                                     ACT.Copy).then_inc(QT_ready, 1)

            def high(i):
                nc.scalar.activation(weights[0][:, i, :], whole[:, i, :], ACT.Copy).then_inc(hi_ready, 1)

            fetch(0, 0)
            nc.scalar.activation(z[0][:, :, :], psT[:, 0, :, :], ACT.Copy).then_inc(z_high, 1)
            with act.Fori(0, CHUNKS // 2 - 2) as b:
                fetch(2 * b + 1, 1)
                keep_queries(2 * b, 0)
                fetch(2 * b + 2, 0)
                keep_queries(2 * b + 1, 1)
            for i in range(PIECES):
                c = CHUNKS - PIECES + i
                if c + 1 < CHUNKS:
                    fetch(c + 1, (c + 1) % 2)
                if first:
                    act.wait_ge(w_piece[i], 16)
                    high(i)
                keep_queries(c, c % 2)

        @block.vector
        def _(dve):
            own = Chain(dve, dve_own)

            def statistics(c):
                own.link(token_statistics(nc, own, norms, res, stats, mv4, pause, c))
                per_chunk = norms.var[:, :].rearrange("p (c j) -> p c j", j=TILES)
                nc.vector.tensor_scalar(per_chunk[:, c, :], mv4[:, :, 1], EPS, None, ALU.add).then_inc(var_ready, 1)

            def normalise(c, q):
                dve.wait_ge(inv_ready, c + 1)
                if not (isinstance(c, int) and c < 2):
                    dve.wait_ge(turn_full, c - 1)
                for j in range(TILES):
                    i = TILES * c + j
                    last = nc.vector.tensor_scalar(zn[:, q, j, :], res[:, i, :], norms.mv[:, i, 0:1],
                                                   norms.inv[:, i, 0:1], ALU.subtract, ALU.mult)
                last.then_inc(zn_ready, 1)

            if first:
                statistics(0)
                statistics(1)
            else:
                nc.vector.tensor_scalar(norms.var[:, :], norms.mv[:, :, 1], EPS, None, ALU.add).then_inc(var_ready, 1)
            normalise(0, 0)
            if first:
                statistics(2)
            normalise(1, 1)
            if first:
                statistics(3)
            dve.wait_ge(z_high, 1)
            nc.vector.tensor_tensor(z[1][:, :, :], psT[:, 0, :, :], z[0][:, :, :].bitcast(FP32),
                                    ALU.subtract).then_inc(z_low, 1)
            with dve.Fori(1, CHUNKS // 2 - 1) as b:
                own.enter(b - 1, 6 if first else 0)
                normalise(2 * b, 0)
                if first:
                    statistics(2 * b + 2)
                normalise(2 * b + 1, 1)
                if first:
                    statistics(2 * b + 3)
                own.leave(CHUNKS // 2 - 2)
            normalise(CHUNKS - 2, 0)
            normalise(CHUNKS - 1, 1)
            for i in range(PIECES // 2, PIECES) if first else ():
                low(dve, i)


def ffn_layers(nc, res, name, shared, norms, first, z, QT, out):
    ctx = ExitStack()
    with ctx:
        def sb(what, shape, dt=FP32):
            return ctx.enter_context(nc.sbuf_tensor(f"{name}_{what}", shape, dt))

        def sem(what):
            return ctx.enter_context(nc.semaphore(f"{name}_{what}"))

        def ps(what, shape):
            return ctx.enter_context(nc.psum_tensor(f"{name}_{what}", shape, FP32))

        keyz, weights, ident = shared.keyz, shared.weights, shared.ident
        pause = sb("pause", [P, 5])
        stats = sb("stats", [P, TILES, 6])
        mv4 = sb("mv4", [P, TILES, 2])
        zn = sb("zn", [P, TILES, D])
        qs = sb("qs", [P, 2, CHUNK // 2])
        Rt = sb("Rt", [P, 2, 2, 2, KEYS])
        top1 = sb("top1", [P, TILES, 2, TOP])
        sums = sb("sums", [P, TILES, TOP, TOP])
        top2 = sb("top2", [P, TILES, TOP])
        ex = sb("ex", [P, TILES, TOP + KEYS + TOP])
        total = sb("total", [P, TILES])
        S = sb("S", [P, TILES, TOP, KEYS])
        W = sb("W", [P, TILES, TOP, KEYS])
        csum = sb("csum", [P, TILES])
        sil = sb("sil", [P, 2, CHUNK])
        prod = sb("prod", [P, 2, CHUNK])
        H = [sb("H_hi", [P, KM, CHUNK], FP32R), sb("H_lo", [P, KM, CHUNK], FP32R)]

        psG, psU, psX, psO = (ps(s, [P, 2, CHUNK]) for s in ("psG", "psU", "psX", "psO"))

        zn_ready, turn_full, zhi_ready, z_ready = sem("zn_ready"), sem("turn_full"), sem("zhi_ready"), sem("z_ready")
        qs_ready, route_full, Rt_ready = sem("qs_ready"), sem("route_full"), sem("Rt_ready")
        dif_ready, exp_ready, ex_ready, SW_ready, C_ready = (sem(s) for s in ("dif_ready", "exp_ready", "ex_ready",
                                                                              "SW_ready", "C_ready"))
        g_full, g_free, u_full, u_free = sem("g_full"), sem("g_free"), sem("u_full"), sem("u_free")
        hi_ready, lo_ready = sem("hi_ready"), sem("lo_ready")
        out_full, out_free = sem("out_full"), sem("out_free")
        dve_own = sem("dve_own")
        SPREAD = [P, TILES, TOP, KEYS]

        def tile(t):
            return Rt[:, :, t, :, :]

        stored = sem("stored")

        block = ctx.enter_context(nc.Block())

        if out is not None:
            @block.sync
            def _(sp):
                out_v = out.rearrange("b (s p h) d -> p (b s) (h d)", p=P, h=2)
                res_v = res[:, :, :].rearrange("p (s h) d -> p s (h d)", h=2)
                for c in range(CHUNKS):
                    sp.wait_ge(out_free, 2 * c + 4)
                    sp.dma_start(out_v[:, 2 * c:2 * c + 2, :], res_v[:, 2 * c:2 * c + 2, :]).then_inc(stored, 16)
                sp.wait_ge(stored, 16 * CHUNKS)

        @block.gpsimd
        def _(pool):
            with pool.Fori(0, CHUNKS) as c:
                pool.wait_ge(Rt_ready, c + 1)
                for b in range(2):
                    pool.tensor_tensor(S[:, 2 * b:2 * b + 2, :, :],
                                       Rt[:, b, 0, :, 0:TOP].unsqueeze(3).to_broadcast([P, 2, TOP, KEYS]),
                                       Rt[:, b, 1, :, :].unsqueeze(2).to_broadcast([P, 2, TOP, KEYS]), ALU.add)
                pool.wait_ge(ex_ready, c + 1)
                pool.tensor_tensor(W[:, :, :, :], ex[:, :, 0:TOP].unsqueeze(3).to_broadcast(SPREAD),
                                   ex[:, :, TOP:TOP + KEYS].unsqueeze(2).to_broadcast(SPREAD),
                                   ALU.mult).then_inc(SW_ready, 1)

        @block.tensor
        def _(pe):
            C = W[:, :, :, :].rearrange("p j a b -> p j (a b)")
            flat = [w[:, :, :].rearrange("p i w -> p (i w)") for w in weights]
            upper = [w[:, 0:KD * UPPER].rearrange("p (k w) -> p k w", k=KD) for w in flat]
            lower = [w[:, KD * UPPER:].rearrange("p (k w) -> p k w", k=KM) for w in flat]

            def split_mm(out, w, x, blocks):
                terms = [(w[i][at], x[j][to]) for at, to in blocks for i, j in ((0, 0), (0, 1), (1, 0))]
                for n, (a, b) in enumerate(terms):
                    last = nc.tensor.matmul(out, a, b, start=n == 0, stop=n == len(terms) - 1)
                return last

            def turn(c):
                pe.wait_ge(zn_ready, c)
                for k in range(KD):
                    for j in range(TILES):
                        last = nc.tensor.transpose(psX[:, k, j * P:(j + 1) * P], zn[:, j, k * P:(k + 1) * P],
                                                   ident[:, :])
                last.then_inc(turn_full, 1)

            def hidden(c, i):
                def column(at):
                    return [((slice(None), k, slice(at * P, (at + 1) * P)), (slice(None), k, slice(None)))
                            for k in range(KD)]

                pe.wait_ge(g_free, KM * c + i + 1)
                split_mm(psG[:, i % 2, :], upper, z, column(i if i < KH else KH + i)).then_inc(g_full, 1)
                pe.wait_ge(u_free, KM * c + i + 1)
                if i < KH:
                    last = split_mm(psU[:, i % 2, :], upper, z, column(KH + i))
                else:
                    if i == KH:
                        pe.wait_ge(C_ready, c + 1)
                    for j in range(TILES):
                        e = i - KH
                        last = nc.tensor.transpose(psU[:, i % 2, j * P:(j + 1) * P], C[:, j, e * P:(e + 1) * P],
                                                   ident[:, :])
                last.then_inc(u_full, 1)

            def chunk(c, more):
                pe.wait_ge(z_ready, c + 1)
                for i in range(KM):
                    hidden(c, i)
                    if i == 0:
                        pe.wait_ge(qs_ready, c + 1)
                        for b in range(2):
                            for t in range(2):
                                last = nc.tensor.matmul(psX[:, 0, (2 * b + t) * P:(2 * b + t + 1) * P],
                                                        qs[:, t, b * P:(b + 1) * P],
                                                        keyz[:, t, :, :].rearrange("p h k -> p (h k)"),
                                                        start=True, stop=True)
                        last.then_inc(route_full, 1)
                for i in range(2):
                    pe.wait_ge(out_free, 2 * c + i + 1)
                    for h in range(2):
                        j = 2 * i + h
                        terms = [(k, a, b) for k in range(KM) for a, b in ((0, 0), (0, 1), (1, 0))]
                        for n, (k, a, b) in enumerate(terms):
                            if j == 0 and n % 3 == 0 and (k == 0 or k >= KH):
                                pe.wait_ge(lo_ready, KM * c + max(k + 1, KH) + 2)
                            last = nc.tensor.matmul(psO[:, i, h * D:(h + 1) * D], H[a][:, k, j * P:(j + 1) * P],
                                                    lower[b][:, k, :], start=n == 0, stop=n == len(terms) - 1)
                    last.then_inc(out_full, 1)
                    if i == 0 and more:
                        turn(c + 1)

            with pe.Fori(0, CHUNKS - 1) as c:
                chunk(c, True)
            chunk(CHUNKS - 1, False)

        @block.scalar
        def _(act):
            pairs = QT[:, :, :].rearrange("x (t s) (u w) -> x t (s u) w", t=2, u=2)

            def prepare(c):
                nc.scalar.activation(qs[:, :, :], pairs[:, :, c, :], ACT.Copy).then_inc(qs_ready, 1)
                if isinstance(c, int) and c == 0:
                    return
                act.wait_ge(turn_full, c)
                nc.scalar.activation(z[0][:, :, :], psX[:, :, :], ACT.Copy).then_inc(zhi_ready, 1)

            def high(c, i):
                act.wait_ge(u_free, KM * c + i + 3)
                nc.scalar.activation(H[0][:, i, :], prod[:, i % 2, :], ACT.Copy).then_inc(hi_ready, 1)

            def chunk(c, more):
                for i in range(KM):
                    act.wait_ge(g_full, KM * c + i + 1)
                    act.wait_ge(u_free, KM * c + i + 1)
                    nc.scalar.activation(sil[:, i % 2, :], psG[:, i % 2, :], ACT.Silu).then_inc(g_free, 1)
                    if i > 0:
                        high(c, i - 1)
                    if i == 0:
                        act.wait_ge(route_full, c + 1)
                        nc.scalar.activation(Rt[:, :, :, :, :].rearrange("p b t h k -> p (b t h k)"), psX[:, 0, :],
                                             ACT.Copy).then_inc(Rt_ready, 1)
                    if i == 3:
                        act.wait_ge(dif_ready, c + 1)
                        nc.scalar.activation(ex[:, :, :], ex[:, :, :], ACT.Exp).then_inc(exp_ready, 1)
                high(c, KM - 1)
                if more:
                    prepare(c + 1)

            prepare(0)
            with act.Fori(0, CHUNKS - 1) as c:
                chunk(c, True)
            chunk(CHUNKS - 1, False)

        @block.vector
        def _(dve):
            own = Chain(dve, dve_own)
            nc.vector.memset(pause[:, 1:2], 0.0).then_inc(g_free, 2)
            nc.vector.memset(pause[:, 2:3], 0.0).then_inc(u_free, 2)
            nc.vector.memset(pause[:, 3:4], 0.0).then_inc(out_free, 2)
            nc.vector.memset(pause[:, 4:5], 0.0).then_inc(lo_ready, 2)
            nc.vector.memset(pause[:, 0:1], 0.0).then_inc(z_ready, 1)

            def normalise(c):
                for j in range(TILES):
                    i = TILES * c + j
                    last = nc.vector.tensor_scalar(zn[:, j, :], res[:, i, :], norms.mv[:, i, 0:1],
                                                   norms.inv[:, i, 0:1], ALU.subtract, ALU.mult)
                last.then_inc(zn_ready, 1)

            def low_z(c):
                dve.wait_ge(zhi_ready, c)
                nc.vector.tensor_tensor(z[1][:, :, :], psX[:, :, :], z[0][:, :, :].bitcast(FP32),
                                        ALU.subtract).then_inc(z_ready, 1)

            def highest(c):
                dve.wait_ge(Rt_ready, c + 1)
                nc.vector.memset(pause[:, 0:1], 0.0)
                for j in range(TILES):
                    for t in range(2):
                        last = nc.vector.max(top1[:, j, t, :], tile(t)[:, j // 2, j % 2, :])
                own.link(last)
                four = [P, TILES, TOP, TOP]
                own.link(nc.vector.tensor_tensor(sums[:, :, :, :], top1[:, :, 0, :].unsqueeze(3).to_broadcast(four),
                                                 top1[:, :, 1, :].unsqueeze(2).to_broadcast(four), ALU.add))
                nc.vector.memset(pause[:, 0:1], 0.0)
                for j in range(TILES):
                    last = nc.vector.max(top2[:, j, :], sums[:, j, :, :].rearrange("p a b -> p (a b)"))
                own.link(last)
                for t, (at, n) in enumerate(((0, TOP), (TOP, KEYS))):
                    part = ex[:, :, at:at + n].rearrange("p (b h) k -> p b h k", b=2)
                    greatest = top1[:, :, t, 0:1].rearrange("p (b h) k -> p b h k", b=2).to_broadcast([P, 2, 2, n])
                    nc.vector.tensor_tensor(part, tile(t)[:, :, :, 0:n], greatest, ALU.subtract)
                nc.vector.tensor_tensor(ex[:, :, TOP + KEYS:], top2[:, :, :],
                                        top2[:, :, 0:1].to_broadcast([P, TILES, TOP]),
                                        ALU.subtract).then_inc(dif_ready, 1)

            def normalise_softmax(c):
                dve.wait_ge(exp_ready, c + 1)
                own.link(nc.vector.reduce_sum(total[:, :], ex[:, :, TOP + KEYS:], AX.X))
                own.link(nc.vector.reciprocal(total[:, :], total[:, :]))
                nc.vector.tensor_tensor(ex[:, :, 0:TOP], ex[:, :, 0:TOP],
                                        total[:, :].unsqueeze(2).to_broadcast([P, TILES, TOP]),
                                        ALU.mult).then_inc(ex_ready, 1)

            def coefficients(c):
                dve.wait_ge(SW_ready, c + 1)
                for j in range(TILES):
                    last = nc.vector.scalar_tensor_tensor(W[:, j, :, :].rearrange("p a b -> p (a b)"), S[:, j, :, :].rearrange("p a b -> p (a b)"),
                                                          top2[:, j, TOP - 1:TOP],
                                                          W[:, j, :, :].rearrange("p a b -> p (a b)"),
                                                          ALU.is_ge, ALU.mult, accum_out=csum[:, j:j + 1])
                own.link(last)
                edge = W[:, :, TOP - 1, KEYS - 1]
                own.link(nc.vector.tensor_tensor(edge, edge, csum[:, :], ALU.subtract))
                nc.vector.tensor_scalar(edge, edge, 1.0, None, ALU.add).then_inc(C_ready, 1)

            def product(c, i):
                dve.wait_ge(g_free, KM * c + i + 3)
                dve.wait_ge(u_full, KM * c + i + 1)
                dve.wait_ge(lo_ready, KM * c + i + 1)
                nc.vector.tensor_tensor(prod[:, i % 2, :], psU[:, i % 2, :], sil[:, i % 2, :],
                                        ALU.mult).then_inc(u_free, 1)

            def low(c, i):
                dve.wait_ge(hi_ready, KM * c + i + 1)
                nc.vector.tensor_tensor(H[1][:, i, :], prod[:, i % 2, :], H[0][:, i, :].bitcast(FP32),
                                        ALU.subtract).then_inc(lo_ready, 1)

            def chunk(c, more):
                for i in range(KM):
                    product(c, i)
                    if i > 0:
                        low(c, i - 1)
                    if i == 0:
                        highest(c)
                    if i == 3:
                        normalise_softmax(c)
                    if i == KH - 2:
                        coefficients(c)
                    if i == KH + 1 and more:
                        normalise(c + 1)
                low(c, KM - 1)
                for i in range(2):
                    dve.wait_ge(out_full, 2 * c + i + 1)
                    x = res[:, :, :].rearrange("p (s h) d -> p s (h d)", h=2)[:, 2 * c + i, :]
                    nc.vector.tensor_tensor(x, x, psO[:, i, :], ALU.add).then_inc(out_free, 1)
                    if i == 0 and more:
                        low_z(c + 1)
                if first:
                    dve.wait_ge(out_free, 2 * c + 4)
                    nc.vector.memset(pause[:, 0:1], 0.0)
                    token_statistics(nc, own, norms, res, stats, mv4, pause, c)

            with dve.Fori(0, CHUNKS - 1) as c:
                own.enter(c, 9 if first else 7)
                chunk(c, True)
                own.leave(CHUNKS - 1)
            chunk(CHUNKS - 1, False)


HEADS, HD = 16, 16
SEQ_TILES = SEQ // P
Q_SCALE = 0.25


def attention(nc, res, dram, norms):
    ctx = ExitStack()
    with ctx:
        def sb(what, shape, dt=FP32):
            return ctx.enter_context(nc.sbuf_tensor("a_" + what, shape, dt))

        def sem(what):
            return ctx.enter_context(nc.semaphore("a_" + what))

        def ps(what, shape):
            return ctx.enter_context(nc.psum_tensor("a_" + what, shape, FP32))

        whole = sb("whole", [P, KD, 4 * D])
        w = [sb("w_hi", [P, KD, 4 * D], FP32R), sb("w_lo", [P, KD, 4 * D], FP32R)]
        KV_COLUMNS, Q_COLUMNS, U_COLUMNS = 0, 2 * D, 3 * D
        wo = sb("wo", [P, KD, D])
        ident = sb("ident", [P, P])
        same_head = sb("same_head", [P, P])
        mhalf = sb("mhalf", [P, TILES, HEADS])
        pause = sb("pause", [P, 4])

        stats = sb("stats", [P, TILES, 6])
        mv4 = sb("mv4", [P, TILES, 2])
        zn = sb("zn", [P, SEQ_TILES, D])
        z = [sb("z_hi", [P, KD, SEQ], FP32R), sb("z_lo", [P, KD, SEQ], FP32R)]
        kv = sb("kv", [P, SEQ_TILES, 2 * D])
        qT = sb("qT", [P, KD, SEQ])
        kvh = sb("kvh", [P, KD, P])
        square = sb("square", [P, SEQ_TILES, D])
        su = sb("su", [P, SEQ_TILES, D])
        ssq = sb("ssq", [P, SEQ_TILES, HEADS])
        rinv = sb("rinv", [P, SEQ_TILES, HEADS])
        og = sb("og", [P, SEQ_TILES, D])
        ogT = sb("ogT", [P, TILES, D])

        ring = ps("ring", [P, 2, CHUNK])
        acc = ps("acc", [P, 2, CHUNK])
        ou = ps("ou", [P, TILES, 2 * D])

        w_whole, w_high, w_low, w_o, const_ready = (sem(s) for s in ("w_whole", "w_high", "w_low", "w_o", "const_ready"))
        turn_full, z_high, z_low = sem("turn_full"), sem("z_high"), sem("z_low")
        var_ready, inv_ready, zn_ready = sem("var_ready"), sem("inv_ready"), sem("zn_ready")
        ring_full, ring_free = sem("ring_full"), sem("ring_free")
        acc_full, kvh_ready, ou_full, ou_free = sem("acc_full"), sem("kvh_ready"), sem("ou_full"), sem("ou_free")
        square_ready, su_ready, ssq_ready, rinv_ready, og_ready = (sem(s) for s in (
            "square_ready", "su_ready", "ssq_ready", "rinv_ready", "og_ready"))
        out_full, out_free = sem("out_full"), sem("out_free")
        dve_own, pool_own = sem("dve_own"), sem("pool_own")

        FIRST_Q, FIRST = 8, 12
        KV, BACK, Q, JOBS = 0, (8, 14), 10, 16
        HALVES = SEQ // CHUNK
        assert FIRST_Q == KV + SEQ_TILES

        def start(b):
            return FIRST + JOBS * b

        block = ctx.enter_context(nc.Block())

        @block.sync
        def _(sp):
            sp.dma_start(whole[:, :, :], dram["Wkvqu"]).then_inc(w_whole, 16)
            sp.dma_start(wo[:, :, :], dram["Wo"]).then_inc(w_o, 16)

        @block.gpsimd
        def _(pool):
            own = Chain(pool, pool_own)
            pool.memset(mhalf[:, :, :], -0.5)
            pool.memset(same_head[:, :], 1.0)
            own.link(pool.memset(ident[:, :], 0.0))
            pool.affine_select(out=ident[:, :], in_=ident[:, :], compare_op=ALU.not_equal, fill=1.0, base=0,
                               pattern=[[-1, P]], channel_multiplier=1)
            blocks = same_head[:, :].rearrange("p (g w) -> p g w", w=HD)
            own.link(pool.affine_select(out=blocks, in_=blocks, compare_op=ALU.is_ge, fill=0.0, base=0,
                                        pattern=[[-HD, P // HD], [0, HD]], channel_multiplier=1))
            pool.affine_select(out=blocks, in_=blocks, compare_op=ALU.is_ge, fill=0.0, base=HD - 1,
                               pattern=[[HD, P // HD], [0, HD]], channel_multiplier=-1).then_inc(const_ready, 1)
            def inverse_norms(b):
                for h in range(HALVES):
                    pool.wait_ge(ssq_ready, HALVES * b + h + 1)
                    at = slice(TILES * h, TILES * (h + 1))
                    pool.tensor_tensor(rinv[:, at, :], ssq[:, at, :], mhalf[:, :, :], ALU.pow).then_inc(rinv_ready, 1)

            pool.wait_ge(var_ready, 1)
            for n in range(BATCH):
                at = slice(SEQ_TILES * n, SEQ_TILES * (n + 1))
                pool.tensor_tensor(norms.inv[:, at, 0], norms.var[:, at], mhalf[:, 0, 0:SEQ_TILES],
                                   ALU.pow).then_inc(inv_ready, 1)
            with pool.Fori(0, BATCH) as b:
                inverse_norms(b)

        @block.tensor
        def _(pe):
            pe.wait_ge(const_ready, 1)
            def split_mm(out, terms):
                terms = [(a[i], b[j]) for a, b in terms for i, j in ((0, 0), (0, 1), (1, 0))]
                for n, (a, b) in enumerate(terms):
                    last = nc.tensor.matmul(out, a, b, start=n == 0, stop=n == len(terms) - 1)
                return last

            def turn(n, half, first):
                pe.wait_ge(zn_ready, HALVES * n + half + 1)
                for k in range(KD):
                    if half == 1:
                        pe.wait_ge(z_low, KD * HALVES * n + k + 1)
                    elif not (isinstance(n, int) and n == 0):
                        pe.wait_ge(ring_free, first - 1 + k)
                    for j in range(TILES):
                        last = nc.tensor.transpose(ring[:, k, j * P:(j + 1) * P],
                                                   zn[:, TILES * half + j, k * P:(k + 1) * P], ident[:, :])
                    last.then_inc(turn_full, 1)

            def heads_kv(n, first, j):
                pe.wait_ge(ring_free, first + j + 1)
                if j == 0 and not (isinstance(n, int) and n == 0):
                    pe.wait_ge(out_free, 2 * HALVES * (n - 1) + 2)
                for g in range(KD):
                    last = nc.tensor.matmul(acc[:, g, 0:P], kv[:, j, g * P:(g + 1) * P],
                                            kv[:, j, D + g * P:D + (g + 1) * P], start=j == 0,
                                            stop=j == SEQ_TILES - 1)
                if j == SEQ_TILES - 1:
                    last.then_inc(acc_full, 1)

            def keys_values(n, first):
                for j in range(SEQ_TILES):
                    if j < 2:
                        pe.wait_ge(z_low, KD * HALVES * n + KD + j + 1)
                    else:
                        pe.wait_ge(ring_free, first + j - 1)
                    split_mm(ring[:, j % 2, :], [([x[:, k, j * P:(j + 1) * P] for x in z],
                                                  [m[:, k, KV_COLUMNS:KV_COLUMNS + 2 * D] for m in w])
                                                 for k in range(KD)]).then_inc(ring_full, 1)
                    if j > 0:
                        heads_kv(n, first, j - 1)
                heads_kv(n, first, SEQ_TILES - 1)

            def queries(first):
                for half in range(HALVES):
                    for g in range(KD):
                        i = KD * half + g
                        pe.wait_ge(ring_free, first + i - 1)
                        at = Q_COLUMNS + g * P
                        split_mm(ring[:, i % 2, :], [([m[:, k, at:at + P] for m in w],
                                                      [x[:, k, half * CHUNK:(half + 1) * CHUNK] for x in z])
                                                     for k in range(KD)]).then_inc(ring_full, 1)

            def heads_out(b, half):
                for t in range(TILES * half, TILES * (half + 1)):
                    j = t % TILES
                    pe.wait_ge(ou_free, SEQ_TILES * b + t + 1)
                    split_mm(ou[:, j, D:], [([x[:, k, t * P:(t + 1) * P] for x in z],
                                             [m[:, k, U_COLUMNS:U_COLUMNS + D] for m in w]) for k in range(KD)])
                    if t == 0:
                        pe.wait_ge(ring_free, start(b))
                        pe.wait_ge(kvh_ready, b + 1)
                    for g in range(KD):
                        last = nc.tensor.matmul(ou[:, j, g * P:(g + 1) * P], qT[:, g, t * P:(t + 1) * P],
                                                kvh[:, g, :], start=True, stop=True)
                    last.then_inc(ou_full, 1)

            def output(b, half, first):
                for i in range(2):
                    pe.wait_ge(ring_free, first + i - 1)
                    for h in range(2):
                        t = TILES * half + 2 * i + h
                        pe.wait_ge(og_ready, SEQ_TILES * b + t + 1)
                        for g in range(KD):
                            last = nc.tensor.transpose(ring[:, i, (2 * h + g) * P:(2 * h + g + 1) * P],
                                                       og[:, t, g * P:(g + 1) * P], ident[:, :])
                    last.then_inc(ring_full, 1)
                for i in range(2):
                    pe.wait_ge(ring_free, first + i + 1)
                    pe.wait_ge(out_free, 2 * HALVES * b + 2 * half + i + 1)
                    for h in range(2):
                        for g in range(KD):
                            last = nc.tensor.matmul(acc[:, i, h * D:(h + 1) * D],
                                                    ogT[:, 2 * i + h, g * P:(g + 1) * P], wo[:, g, :],
                                                    start=g == 0, stop=g == KD - 1)
                    last.then_inc(out_full, 1)

            for half in range(HALVES):
                turn(0, half, 0)
            pe.wait_ge(w_low, 1)
            pe.wait_ge(w_o, 16)
            keys_values(0, KV)
            queries(FIRST_Q)
            with pe.Fori(0, BATCH - 1) as b:
                for half in range(HALVES):
                    heads_out(b, half)
                    turn(b + 1, half, start(b))
                keys_values(b + 1, start(b) + KV)
                pe.wait_ge(kvh_ready, b + 2)
                output(b, 0, start(b) + BACK[0])
                queries(start(b) + Q)
                output(b, 1, start(b) + BACK[1])
            for half in range(HALVES):
                heads_out(BATCH - 1, half)
            for half in range(HALVES):
                output(BATCH - 1, half, start(BATCH - 1) + 2 * half)

        @block.scalar
        def _(act):
            def turned(n, half):
                for k in range(KD):
                    act.wait_ge(turn_full, KD * (HALVES * n + half) + k + 1)
                    nc.scalar.activation(z[0][:, k, half * CHUNK:(half + 1) * CHUNK], ring[:, k, :],
                                         ACT.Copy).then_inc(z_high, 1)

            def keys_values(first):
                for j in range(SEQ_TILES):
                    act.wait_ge(ring_full, first + j + 1)
                    nc.scalar.activation(kv[:, j, 0:D], ring[:, j % 2, 0:D], ACT.Relu, scale=Q_SCALE)
                    nc.scalar.activation(kv[:, j, D:], ring[:, j % 2, D:], ACT.Copy).then_inc(ring_free, 1)

            def queries(first):
                for half in range(HALVES):
                    for g in range(KD):
                        i = KD * half + g
                        act.wait_ge(ring_full, first + i + 1)
                        nc.scalar.activation(qT[:, g, half * CHUNK:(half + 1) * CHUNK], ring[:, i % 2, :], ACT.Relu,
                                             scale=Q_SCALE).then_inc(ring_free, 1)

            def heads_out(b, half):
                for t in range(TILES * half, TILES * (half + 1)):
                    act.wait_ge(ou_full, SEQ_TILES * b + t + 1)
                    nc.scalar.activation(square[:, t, :], ou[:, t % TILES, 0:D], ACT.Square).then_inc(square_ready, 1)
                    nc.scalar.activation(su[:, t, :], ou[:, t % TILES, D:], ACT.Silu).then_inc(su_ready, 1)

            def back(first):
                for i in range(2):
                    act.wait_ge(ring_full, first + i + 1)
                    nc.scalar.activation(ogT[:, 2 * i:2 * i + 2, :].rearrange("p h d -> p (h d)"), ring[:, i, :],
                                         ACT.Copy).then_inc(ring_free, 1)

            act.wait_ge(w_whole, 16)
            nc.scalar.activation(w[0][:, :, :], whole[:, :, :], ACT.Copy).then_inc(w_high, 1)
            for half in range(HALVES):
                turned(0, half)
            keys_values(KV)
            queries(FIRST_Q)
            with act.Fori(0, BATCH - 1) as b:
                for half in range(HALVES):
                    heads_out(b, half)
                    turned(b + 1, half)
                keys_values(start(b) + KV)
                back(start(b) + BACK[0])
                queries(start(b) + Q)
                back(start(b) + BACK[1])
            for half in range(HALVES):
                heads_out(BATCH - 1, half)
            for half in range(HALVES):
                back(start(BATCH - 1) + 2 * half)

        @block.vector
        def _(dve):
            own = Chain(dve, dve_own)
            nc.vector.memset(pause[:, 2:3], 0.0).then_inc(out_free, 2)
            nc.vector.memset(pause[:, 3:4], 0.0).then_inc(ou_free, TILES)

            def normalise(n):
                dve.wait_ge(inv_ready, n + 1)
                for half in range(HALVES):
                    for j in range(TILES * half, TILES * (half + 1)):
                        i = SEQ_TILES * n + j
                        last = nc.vector.tensor_scalar(zn[:, j, :], res[:, i, :], norms.mv[:, i, 0:1],
                                                       norms.inv[:, i, 0:1], ALU.subtract, ALU.mult)
                    last.then_inc(zn_ready, 1)

            def low_z(n, half):
                for k in range(KD):
                    dve.wait_ge(z_high, KD * (HALVES * n + half) + k + 1)
                    at = slice(half * CHUNK, (half + 1) * CHUNK)
                    nc.vector.tensor_tensor(z[1][:, k, at], ring[:, k, :], z[0][:, k, at].bitcast(FP32),
                                            ALU.subtract).then_inc(z_low, 1)

            def keep_kv(n):
                dve.wait_ge(acc_full, n + 1)
                for g in range(KD):
                    last = nc.vector.tensor_tensor(kvh[:, g, :], acc[:, g, 0:P], same_head[:, :], ALU.mult)
                last.then_inc(kvh_ready, 1)

            def square_sums(b, half):
                at = slice(TILES * half, TILES * (half + 1))
                for t in range(TILES * half, TILES * (half + 1)):
                    dve.wait_ge(square_ready, SEQ_TILES * b + t + 1)
                    last = nc.vector.reduce_sum(ssq[:, t, :], square[:, t, :].rearrange("p (h w) -> p h w", w=HD),
                                                AX.X)
                own.link(last)
                nc.vector.tensor_scalar(ssq[:, at, :], ssq[:, at, :], 1.0 / HD, 1e-24, ALU.mult,
                                        ALU.max).then_inc(ssq_ready, 1)

            def gate(b, half):
                for t in range(TILES * half, TILES * (half + 1)):
                    dve.wait_ge(su_ready, SEQ_TILES * b + t + 1)
                    nc.vector.tensor_tensor(og[:, t, :], su[:, t, :], ou[:, t % TILES, 0:D],
                                            ALU.mult).then_inc(ou_free, 1)

            def scale(b, half):
                dve.wait_ge(rinv_ready, HALVES * b + half + 1)
                dve.wait_ge(ou_free, SEQ_TILES * b + TILES * (half + 2))
                for t in range(TILES * half, TILES * (half + 1)):
                    o = og[:, t, :].rearrange("p (h w) -> p h w", w=HD)
                    nc.vector.tensor_tensor(o, o, rinv[:, t, :].unsqueeze(2).to_broadcast([P, HEADS, HD]),
                                            ALU.mult).then_inc(og_ready, 1)

            def add_output(b, half):
                for i in range(2):
                    dve.wait_ge(out_full, 2 * HALVES * b + 2 * half + i + 1)
                    x = res[:, :, :].rearrange("p (s h) d -> p s (h d)", h=2)[:, TILES * b + 2 * half + i, :]
                    nc.vector.tensor_tensor(x, x, acc[:, i, :], ALU.add).then_inc(out_free, 1)
                dve.wait_ge(out_free, 2 * HALVES * b + 2 * half + 4)
                nc.vector.memset(pause[:, 0:1], 0.0)
                token_statistics(nc, own, norms, res, stats, mv4, pause, HALVES * b + half)

            def sequence(b, behind):
                for half in range(HALVES):
                    square_sums(b, half)
                    gate(b, half)
                    if behind > 0:
                        low_z(b + 1, half)
                scale(b, 0)
                scale(b, 1)
                if behind > 0:
                    keep_kv(b + 1)
                add_output(b, 0)
                if behind > 1:
                    normalise(b + 2)
                add_output(b, 1)

            nc.vector.tensor_scalar(norms.var[:, :], norms.mv[:, :, 1], EPS, None, ALU.add).then_inc(var_ready, 1)
            normalise(0)
            dve.wait_ge(w_high, 1)
            nc.vector.tensor_tensor(w[1][:, :, :], whole[:, :, :], w[0][:, :, :].bitcast(FP32),
                                    ALU.subtract).then_inc(w_low, 1)
            for half in range(HALVES):
                low_z(0, half)
            normalise(1)
            dve.wait_ge(const_ready, 1)
            keep_kv(0)
            with dve.Fori(0, BATCH - 2) as b:
                own.enter(b, 6)
                sequence(b, 2)
                own.leave(BATCH - 2)
            sequence(BATCH - 2, 1)
            sequence(BATCH - 1, 0)


def program(nc, dram, out):
    with ExitStack() as ctx:
        def sb(name, shape, dt=FP32):
            return ctx.enter_context(nc.sbuf_tensor(name, shape, dt))

        res = sb("res", [P, TOKENS // P, D])
        mamba(nc, res, dram)
        shared, norms = Shared(sb), Norms(sb)
        ffn(nc, res, dram, "f", shared, norms, True)
        attention(nc, res, dram, norms)
        ffn(nc, res, dram, "g", shared, norms, False, out)


def kernel(**inputs):
    import concourse.bacc as bacc
    from concourse.bass_utils import run_bass_kernel_spmd

    def a(name):
        return np.asarray(inputs["L0_" + name])

    def blocks(w):
        return np.ascontiguousarray(w.reshape(-1, P, w.shape[-1]).transpose(1, 0, 2))

    laid = {
        "x": a("attn_a_resid"),
        "norm_w": blocks(a("attn_a_norm_w")[:, None])[:, :, 0],
        "in_w": blocks(a("attn_a_in_w").T),
        "skip_w": blocks(a("attn_a_skip_w").T),
        "conv_w": blocks(a("attn_a_conv_w")),
        "conv_b": blocks(a("attn_a_conv_b")[:, None])[:, :, 0],
        "wd1": blocks(a("attn_a_wd1").T),
        "wd2": a("attn_a_wd2").T,
        "wd2_b": blocks(a("attn_a_wd2_b")[:, None])[:, :, 0],
        "wB": blocks(a("attn_a_wB").T),
        "wC": blocks(a("attn_a_wC").T),
        "A_log": blocks(a("attn_a_A_log")),
        "W_D": blocks(a("attn_a_W_D")[:, None])[:, :, 0],
        "out_w": blocks(a("attn_a_out_w").T),
        "Wkvqu": blocks(np.concatenate([a("attn_b_" + w) for w in ("Wk", "Wv", "Wq", "Wu")], axis=1)),
        "Wo": blocks(a("attn_b_Wo")),
        "W_q": blocks(a("ffn_W_q")),
        "keys": a("ffn_keys").transpose(1, 0, 2),
        "ffn_w": np.concatenate([
            blocks(np.concatenate([a("ffn_gate_w"), a("ffn_up_w"), a("ffn_down_embed").T], axis=1)).reshape(P, -1),
            blocks(np.concatenate([a("ffn_down_w"), a("ffn_up_embed")], axis=0)).reshape(P, -1),
        ], axis=1).reshape(P, PIECES, -1),
    }
    nc = bacc.Bacc("TRN2", target_bir_lowering=False, num_devices=1)
    arrays, dram = {}, {}
    for name, w in laid.items():
        arrays["in_" + name] = np.ascontiguousarray(w)
        dram[name] = nc.dram_tensor("in_" + name, w.shape, FP32, kind="ExternalInput").ap()
    out = nc.dram_tensor("out", (BATCH, SEQ, D), FP32, kind="ExternalOutput").ap()
    program(nc, dram, out)
    r = run_bass_kernel_spmd(nc, [arrays], core_ids=[0])
    return r.results[0]["out"]
```
